# Optimizing a Trainium2 kernel written in Bass

```python
import numpy as np
import jax
import jax.numpy as jnp

def _softmax(x, axis=-1):
    return jax.nn.softmax(x, axis=axis)

def _gelu(x):
    return jax.nn.gelu(x, approximate=True)

def _silu(x):
    return jax.nn.silu(x)

def _sigmoid(x):
    return jax.nn.sigmoid(x)

def _layernorm(x, axis=-1, eps=1e-05):
    m = jnp.mean(x, axis=axis, keepdims=True)
    v = jnp.var(x, axis=axis, keepdims=True)
    return (x - m) / jnp.sqrt(v + eps)

def _scatter_add(tgt, idx, src, axis=0):
    return tgt.at[idx].add(src)

def _segment_sum(src, seg, n):
    return jax.ops.segment_sum(src, seg, n)
kernel_name = 'mk_gnn_preln_d4_gnn_r64_7d6bf8'

def setup_inputs(seed: int=0):
    np.random.seed(seed)
    _w = jnp.asarray

    def _rec_inputs():
        import jax
        import jax.numpy as jnp
        _gk = jax.random.key(seed)
        x = -0.0005121 + 1.001 * jax.random.normal(jax.random.fold_in(_gk, 1), (100000, 32), jnp.float32)
        src = jax.random.randint(jax.random.fold_in(_gk, 2), (25000,), 0, 100000, jnp.int32)
        dst = jnp.minimum((100000 * jax.random.uniform(jax.random.fold_in(_gk, 3), (25000,)) ** 2.0).astype(jnp.int32), 99999)
        _o = jnp.argsort(dst, stable=True)
        src = src[_o]
        dst = dst[_o]
        edge_attr_2 = jax.random.uniform(jax.random.fold_in(_gk, 12), (25000, 2), jnp.float32, 0.0, 1)
        edge_attr_32 = 0.000196303 + 1.00016 * jax.random.normal(jax.random.fold_in(_gk, 13), (25000, 32), jnp.float32)
        edge_type_86 = jax.random.randint(jax.random.fold_in(_gk, 15), (25000,), 0, 86, jnp.int32)
        return (x, src, dst, edge_attr_2, edge_attr_32, edge_type_86)
    x, src, dst, edge_attr_2, edge_attr_32, edge_type_86 = _rec_inputs()

    def _L0_gnn_setup():
        import jax, jax.numpy as jnp
        import numpy as np
        N_NODES = 100000
        N_EDGES = 25000
        F_IN = 32
        F_OUT = 32
        DIM = 2
        K = 5
        KTOT = K ** DIM
        S = 2 ** DIM
        NEG_SLOPE = 0.2
        _OFFSETS = np.array([[s >> d & 1 for d in range(DIM)] for s in range(S)], dtype=np.int32)
        _STRIDES = np.array([K ** d for d in range(DIM)], dtype=np.int32)

        def _spline_basis(pseudo):
            offsets = jnp.asarray(_OFFSETS)
            strides = jnp.asarray(_STRIDES)
            p = pseudo * (K - 1)
            fl = jnp.floor(p)
            frac = p - fl
            b = jnp.where(offsets[None] == 0, 1.0 - frac[:, None, :], frac[:, None, :])
            basis = jnp.prod(b, axis=-1)
            idx = jnp.clip(fl.astype(jnp.int32)[:, None, :] + offsets[None], 0, K - 1)
            widx = jnp.sum(idx * strides, axis=-1)
            return (basis, widx)
        key = jax.random.key(seed)
        ks = jax.random.split(key, 7)
        x = jax.random.normal(ks[0], (N_NODES, F_IN), dtype=jnp.float32)
        edge_index = jax.random.randint(ks[1], (2, N_EDGES), 0, N_NODES)
        pseudo = jax.random.uniform(ks[2], (N_EDGES, DIM), dtype=jnp.float32)
        bound = 1.0 / np.sqrt(KTOT * F_IN)
        weight = jax.random.uniform(ks[3], (KTOT, F_IN, F_OUT), jnp.float32, -bound, bound)
        root_weight = jax.random.uniform(ks[4], (F_IN, F_OUT), jnp.float32, -bound, bound)
        att_weight = jax.random.uniform(ks[5], (2 * F_OUT,), jnp.float32, -bound, bound)
        bias = jax.random.uniform(ks[6], (F_OUT,), jnp.float32, -bound, bound)
        return {'x': x, 'edge_index': edge_index, 'pseudo': pseudo, 'weight': weight, 'root_weight': root_weight, 'att_weight': att_weight, 'bias': bias}
    _L0_gnn_all = _L0_gnn_setup()
    _L0_gnn_in = {k: v for k, v in _L0_gnn_all.items() if k in ('weight', 'root_weight', 'att_weight', 'bias')}
    del _L0_gnn_all

    def _L1_gnn_setup():
        import jax, jax.numpy as jnp
        import numpy as np
        N_NODES = 50000
        N_EDGES = 12500
        X_DIM = 32
        E_DIM = 32
        HID = 64
        OUT = 32
        key = jax.random.key(seed)
        ks = jax.random.split(key, 6)
        x = jax.random.normal(ks[0], (N_NODES, X_DIM), dtype=jnp.float32)
        edge_index = jax.random.randint(ks[1], (2, N_EDGES), 0, N_NODES, dtype=jnp.int64)
        edge_attr = jax.random.normal(ks[2], (N_EDGES, E_DIM), dtype=jnp.float32)
        in_dim = 2 * X_DIM + E_DIM
        W1 = jax.random.normal(ks[3], (in_dim, HID), dtype=jnp.float32) * (1.0 / np.sqrt(in_dim))
        b1 = jnp.zeros((HID,), dtype=jnp.float32)
        W2 = jax.random.normal(ks[4], (HID, OUT), dtype=jnp.float32) * (1.0 / np.sqrt(HID))
        b2 = jnp.zeros((OUT,), dtype=jnp.float32)
        return {'x': x, 'edge_index': edge_index, 'edge_attr': edge_attr, 'W1': W1, 'b1': b1, 'W2': W2, 'b2': b2}
    _L1_gnn_all = _L1_gnn_setup()
    _L1_gnn_in = {k: v for k, v in _L1_gnn_all.items() if k in ('W1', 'b1', 'W2', 'b2')}
    del _L1_gnn_all

    def _L2_gnn_setup():
        import jax, jax.numpy as jnp
        import numpy as np
        N_NODES = 50000
        N_EDGES = 12500
        INP_DIM = 32
        OUT_DIM = 32
        ATTN_DIM = 32
        NUM_RELS = 86
        NUM_BASES = 16
        GAMMA = 0.0
        key = jax.random.key(seed)
        ks = jax.random.split(key, 12)
        return {'h': jax.random.normal(ks[0], (N_NODES, INP_DIM), jnp.float32), 'weight': jax.random.normal(ks[1], (NUM_BASES, INP_DIM, OUT_DIM), jnp.float32), 'w_comp': jax.random.normal(ks[2], (NUM_RELS, NUM_BASES), jnp.float32), 'self_loop_weight': jax.random.normal(ks[3], (INP_DIM, OUT_DIM), jnp.float32), 'A1_w': jax.random.normal(ks[4], (ATTN_DIM, INP_DIM), jnp.float32), 'A1_b': jax.random.normal(ks[5], (ATTN_DIM,), jnp.float32), 'A2_w': jax.random.normal(ks[6], (ATTN_DIM, INP_DIM), jnp.float32), 'A2_b': jax.random.normal(ks[7], (ATTN_DIM,), jnp.float32), 'rel_emb': jax.random.normal(ks[8], (NUM_RELS, ATTN_DIM), jnp.float32), 'src': jax.random.randint(ks[9], (N_EDGES,), 0, N_NODES, jnp.int32), 'dst': jax.random.randint(ks[10], (N_EDGES,), 0, N_NODES, jnp.int32), 'etype': jax.random.randint(ks[11], (N_EDGES,), 0, NUM_RELS, jnp.int32)}
    _L2_gnn_all = _L2_gnn_setup()
    _L2_gnn_in = {k: v for k, v in _L2_gnn_all.items() if k in ('weight', 'w_comp', 'self_loop_weight', 'A1_w', 'A1_b', 'A2_w', 'A2_b', 'rel_emb')}
    del _L2_gnn_all

    def _L3_gnn_setup():
        import jax, jax.numpy as jnp
        import numpy as np
        N, E, D = (50000, 25000, 32)
        P = 2.0

        def gcn_conv(X, edge_index, W, b, n):
            src, dst = (edge_index[0], edge_index[1])
            loops = jnp.arange(n)
            row = jnp.concatenate([dst, loops])
            col = jnp.concatenate([src, loops])
            deg = jax.ops.segment_sum(jnp.ones(row.shape, X.dtype), row, num_segments=n)
            dinv = jax.lax.rsqrt(jnp.maximum(deg, 1.0))
            h = X @ W
            msg = h[col] * (dinv[col] * dinv[row])[:, None]
            return jax.ops.segment_sum(msg, row, num_segments=n) + b
        key = jax.random.key(seed)
        k1, k2, k3 = jax.random.split(key, 3)
        X = jax.random.normal(k1, (N, D), dtype=jnp.float32)
        edge_index = jax.random.randint(k2, (2, E), 0, N)
        W = jax.random.normal(k3, (D, D), dtype=jnp.float32) / np.float32(np.sqrt(D))
        b = jnp.zeros((D,), dtype=jnp.float32)
        return {'X': X, 'edge_index': edge_index, 'W': W, 'b': b}
    _L3_gnn_all = _L3_gnn_setup()
    _L3_gnn_in = {k: v for k, v in _L3_gnn_all.items() if k in ('W', 'b')}
    del _L3_gnn_all
    return {'x': x, 'src': src, 'dst': dst, 'edge_attr_2': edge_attr_2, 'edge_attr_32': edge_attr_32, 'edge_type_86': edge_type_86, 'L0_gnn_weight': _L0_gnn_in['weight'], 'L0_gnn_root_weight': _L0_gnn_in['root_weight'], 'L0_gnn_att_weight': _L0_gnn_in['att_weight'], 'L0_gnn_bias': _L0_gnn_in['bias'], 'L1_gnn_W1': _L1_gnn_in['W1'], 'L1_gnn_b1': _L1_gnn_in['b1'], 'L1_gnn_W2': _L1_gnn_in['W2'], 'L1_gnn_b2': _L1_gnn_in['b2'], 'L2_gnn_weight': _L2_gnn_in['weight'], 'L2_gnn_w_comp': _L2_gnn_in['w_comp'], 'L2_gnn_self_loop_weight': _L2_gnn_in['self_loop_weight'], 'L2_gnn_A1_w': _L2_gnn_in['A1_w'], 'L2_gnn_A1_b': _L2_gnn_in['A1_b'], 'L2_gnn_A2_w': _L2_gnn_in['A2_w'], 'L2_gnn_A2_b': _L2_gnn_in['A2_b'], 'L2_gnn_rel_emb': _L2_gnn_in['rel_emb'], 'L3_gnn_W': _L3_gnn_in['W'], 'L3_gnn_b': _L3_gnn_in['b']}

def reference(x, src, dst, edge_attr_2, edge_attr_32, edge_type_86, L0_gnn_weight, L0_gnn_root_weight, L0_gnn_att_weight, L0_gnn_bias, L1_gnn_W1, L1_gnn_b1, L1_gnn_W2, L1_gnn_b2, L2_gnn_weight, L2_gnn_w_comp, L2_gnn_self_loop_weight, L2_gnn_A1_w, L2_gnn_A1_b, L2_gnn_A2_w, L2_gnn_A2_b, L2_gnn_rel_emb, L3_gnn_W, L3_gnn_b):
    import jax
    import jax.numpy as jnp

    def _L0_gnn_ref(x, edge_index, pseudo, weight, root_weight, att_weight, bias):
        import jax, jax.numpy as jnp
        import numpy as np
        N_NODES = 100000
        N_EDGES = 25000
        F_IN = 32
        F_OUT = 32
        DIM = 2
        K = 5
        KTOT = K ** DIM
        S = 2 ** DIM
        NEG_SLOPE = 0.2
        _OFFSETS = np.array([[s >> d & 1 for d in range(DIM)] for s in range(S)], dtype=np.int32)
        _STRIDES = np.array([K ** d for d in range(DIM)], dtype=np.int32)

        def _spline_basis(pseudo):
            offsets = jnp.asarray(_OFFSETS)
            strides = jnp.asarray(_STRIDES)
            p = pseudo * (K - 1)
            fl = jnp.floor(p)
            frac = p - fl
            b = jnp.where(offsets[None] == 0, 1.0 - frac[:, None, :], frac[:, None, :])
            basis = jnp.prod(b, axis=-1)
            idx = jnp.clip(fl.astype(jnp.int32)[:, None, :] + offsets[None], 0, K - 1)
            widx = jnp.sum(idx * strides, axis=-1)
            return (basis, widx)
        row, col = (edge_index[0], edge_index[1])
        basis, widx = _spline_basis(pseudo)
        xw = jnp.einsum('nf,kfo->nko', x, weight)
        flat = col[:, None] * KTOT + widx
        gathered = xw.reshape(-1, F_OUT)[flat]
        msg = jnp.einsum('es,esf->ef', basis, gathered)
        x_root = x @ root_weight
        alpha = x_root[row] @ att_weight[:F_OUT] + msg @ att_weight[F_OUT:]
        alpha = jnp.where(alpha > 0, alpha, NEG_SLOPE * alpha)
        amax = jax.ops.segment_max(alpha, row, num_segments=N_NODES)
        amax = jnp.where(jnp.isfinite(amax), amax, 0.0)
        ex = jnp.exp(alpha - amax[row])
        denom = jax.ops.segment_sum(ex, row, num_segments=N_NODES)
        att = ex / (denom[row] + 1e-16)
        out = jax.ops.segment_sum(msg * att[:, None], row, num_segments=N_NODES)
        return out + x_root + bias

    def _L1_gnn_ref(x, edge_index, edge_attr, W1, b1, W2, b2):
        import jax, jax.numpy as jnp
        import numpy as np
        N_NODES = 50000
        N_EDGES = 12500
        X_DIM = 32
        E_DIM = 32
        HID = 64
        OUT = 32
        num_nodes = x.shape[0]
        rol, col = (edge_index[0], edge_index[1])
        e_feat = jnp.concatenate([x[rol], x[col], edge_attr], axis=-1)
        h = jax.nn.relu(e_feat @ W1 + b1)
        v = h @ W2 + b2
        x_cand = jax.ops.segment_max(v, col, num_segments=num_nodes)
        return jnp.maximum(x_cand, x[:, -v.shape[-1]:])

    def _L2_gnn_ref(h, weight, w_comp, self_loop_weight, A1_w, A1_b, A2_w, A2_b, rel_emb, src, dst, etype):
        import jax, jax.numpy as jnp
        import numpy as np
        N_NODES = 50000
        N_EDGES = 12500
        INP_DIM = 32
        OUT_DIM = 32
        ATTN_DIM = 32
        NUM_RELS = 86
        NUM_BASES = 16
        GAMMA = 0.0
        E = src.shape[0]
        N = h.shape[0]
        x = h[src]
        y = h[dst]
        c = w_comp[etype]
        xb = jnp.einsum('ei,bio->ebo', x, weight)
        msg = jnp.einsum('eb,ebo->eo', c, xb)
        x_hat = x @ A1_w.T + A1_b
        y_hat = y @ A2_w.T + A2_b + rel_emb[etype]
        scale = jnp.sqrt(jnp.asarray(INP_DIM, h.dtype))
        a = jnp.tanh(jax.nn.relu(jnp.sum(x_hat * y_hat, axis=-1) / scale))
        a = jnp.where(a > GAMMA, a, jnp.zeros_like(a))
        nei = jax.ops.segment_sum(a[:, None] * msg, dst, num_segments=N)
        last_e = jax.ops.segment_max(jnp.arange(E, dtype=jnp.int32), dst, num_segments=N)
        last_e = jnp.clip(last_e, 0, E - 1)
        curr = h[src[last_e]] @ self_loop_weight
        in_deg = jax.ops.segment_sum(jnp.ones((E,), h.dtype), dst, num_segments=N)
        h_new = jnp.where((in_deg > 0)[:, None], nei + curr, jnp.zeros_like(nei))
        return jax.nn.relu(h_new)

    def _L3_gnn_ref(X, edge_index, W, b):
        import jax, jax.numpy as jnp
        import numpy as np
        N, E, D = (50000, 25000, 32)
        P = 2.0

        def gcn_conv(X, edge_index, W, b, n):
            src, dst = (edge_index[0], edge_index[1])
            loops = jnp.arange(n)
            row = jnp.concatenate([dst, loops])
            col = jnp.concatenate([src, loops])
            deg = jax.ops.segment_sum(jnp.ones(row.shape, X.dtype), row, num_segments=n)
            dinv = jax.lax.rsqrt(jnp.maximum(deg, 1.0))
            h = X @ W
            msg = h[col] * (dinv[col] * dinv[row])[:, None]
            return jax.ops.segment_sum(msg, row, num_segments=n) + b
        n = X.shape[0]
        h = jax.nn.relu(gcn_conv(X, edge_index, W, b, n))
        src, dst = (edge_index[0], edge_index[1])
        e = jnp.abs(h[src] - h[dst]) ** P
        s = jax.ops.segment_sum(e, src, num_segments=n)
        cnt = jax.ops.segment_sum(jnp.ones((e.shape[0],), h.dtype), src, num_segments=n)
        mean = s / jnp.maximum(cnt, 1.0)[:, None]
        return jnp.tanh(mean)
    edge_index = jnp.stack([src, dst])
    h = jnp.maximum(_layernorm(x, axis=-1), 0.0)
    x = x + _L0_gnn_ref(h, edge_index, edge_attr_2, L0_gnn_weight, L0_gnn_root_weight, L0_gnn_att_weight, L0_gnn_bias)
    h = jnp.maximum(_layernorm(x, axis=-1), 0.0)
    x = x + _L1_gnn_ref(h, edge_index, edge_attr_32, L1_gnn_W1, L1_gnn_b1, L1_gnn_W2, L1_gnn_b2)
    h = jnp.maximum(_layernorm(x, axis=-1), 0.0)
    x = x + _L2_gnn_ref(h, L2_gnn_weight, L2_gnn_w_comp, L2_gnn_self_loop_weight, L2_gnn_A1_w, L2_gnn_A1_b, L2_gnn_A2_w, L2_gnn_A2_b, L2_gnn_rel_emb, src, dst, edge_type_86)
    h = jnp.maximum(_layernorm(x, axis=-1), 0.0)
    x = x + _L3_gnn_ref(h, edge_index, L3_gnn_W, L3_gnn_b)
    return x

_drawn_inputs = setup_inputs


def setup_inputs(seed=0):
    import zlib

    import numpy as np

    out = dict(_drawn_inputs(seed))
    spreads = {'L1_gnn_b1': (0.0, 0.1), 'L1_gnn_b2': (0.0, 0.1), 'L3_gnn_b': (0.0, 2.0)}
    factors = {'L0_gnn_att_weight': 200.0, 'L3_gnn_W': 3.422}
    for name, (base, spread) in spreads.items():
        noise = np.random.default_rng([zlib.crc32(name.encode()), seed]).standard_normal(out[name].shape)
        drawn = base * np.exp(spread * noise) if base else spread * noise
        out[name] = jnp.asarray(drawn.astype(out[name].dtype))
    for name, factor in factors.items():
        out[name] = (out[name] * factor).astype(out[name].dtype)
    return out
```

```python
import concourse.bass as bass
from concourse import mybir
from contextlib import ExitStack

fp32 = mybir.dt.float32
i32 = mybir.dt.int32
ALU = mybir.AluOpType
ACT = mybir.ActivationFunctionType
AX = mybir.AxisListType

P = 128
N = 100000
F = 32
E = 25000
ROWS_E = 125
T = E // ROWS_E
G = 4
NG = T // G
TP = T + G
PAD_KEY = 200000
NT = 100352
EPS = 1e-5
BIG = 1e30
SLOPE = 0.2
KS = 5
TAPS = KS * KS
TC = 15
HID = 64
NB = 16
REL = 86
K = 48
NCH = 17
STRIDE = (N - P * K) // (NCH - 1)
LN_EPS = EPS * F * F * F
LN_GAIN = float(F) ** 0.5


PER_E0 = 27
PER_D0 = 14
PER_E1 = 5
PER_R1 = 5
PER_D1 = 4
PER_E2 = 14
PER_D2 = 4
PER_D3 = 2
PER_E4 = 3
PER_D4 = 2


class Steps:

    def __init__(self, eng, sem, per=0, first=0):
        self.eng, self.sem, self.per, self.first = eng, sem, per, first
        self.base, self.n = 0, 0

    def start(self, g):
        self.base, self.n = self.first + g * self.per, 0

    def done(self, ins):
        ins.then_inc(self.sem, 1)
        self.n += 1

    def sync(self):
        self.eng.wait_ge(self.sem, self.base + self.n)

    def end(self):
        assert self.n == self.per, self.n


def wait(eng, sem, value):
    if not (isinstance(value, int) and value <= 0):
        eng.wait_ge(sem, value)


def rep(ap, n):
    return ap.unsqueeze(2).to_broadcast([ap.shape[0], ap.shape[1], n])


def along(ap, n):
    return ap.unsqueeze(1).to_broadcast([ap.shape[0], n, ap.shape[1]])


def cols(g):
    return slice(G * g, G * g + G) if isinstance(g, int) else bass.ds(G * g, G)


def each_group(eng, body):
    body(1, 1, 0)
    with eng.Fori(0, (NG - 2) // 2) as i:
        body(2 * i + 2, 0, i + 1)
        body(2 * i + 3, 1, i + 1)


def each_chunk(eng, body):
    body(0, 0, 0)
    body(1, 1, 0)
    with eng.Fori(0, (NCH - 5) // 2) as i:
        body(2 * i + 2, 0, i + 1)
        body(2 * i + 3, 1, i + 1)
    for c in range(NCH - 3, NCH):
        body(c, c % 2, c // 2)


def chunk(table, c):
    lo = c * STRIDE
    rows = table[lo:lo + P * K, :] if isinstance(c, int) else table[bass.ds(lo, P * K), :]
    return rows.rearrange("(p k) f -> p k f", p=P)


class Semaphores:

    def __init__(self, nc, ctx):
        self.nc, self.ctx = nc, ctx
        self.free, self.resting, self.retired = [], [], []

    def phase(self, prefix, taken):
        self.free, self.resting = self.free + self.resting, []

        def sem(name):
            taken.append(self.free.pop() if self.free else self.ctx.enter_context(self.nc.semaphore(prefix + name)))
            return taken[-1]
        return sem

    def retire(self, taken):
        self.retired += taken

    def clear(self, sp):
        for s in self.retired:
            sp.sem_clear(s)
        self.resting, self.retired = self.resting + self.retired, []


class Memory:

    def __init__(self, nc, ctx):
        def sb(name, shape, dt=fp32):
            return ctx.enter_context(nc.sbuf_tensor(name, shape, dt))

        def table(name, shape, dt=fp32):
            return nc.dram_tensor(name, shape, dt).ap()

        self.sems = Semaphores(nc, ctx)
        self.keyT = {k: table("keyT_" + k, [T, P]) for k in ("src", "dst", "type")}
        self.softmax_state = [table(f"softmax_state{k}", [NT, F + 2]) for k in range(2)]
        self.max_state = [table(f"max_state{k}", [NT, F + 1]) for k in range(2)]
        self.rel_sums = table("rel_sums", [NT, F + 1])
        self.conv_sums = table("conv_sums", [NT, F])
        self.square_sums = table("square_sums", [NT, F + 1])
        self.x1 = table("x1", [N, F])
        self.x2 = table("x2", [N, F + 1])
        self.x3 = table("x3", [N, F])
        self.hs = table("hs", [N, F + 1])
        self.conv = table("conv", [N, F])

        self.ident = sb("ident", [P, P])
        self.lower = sb("lower", [P, P])
        self.ones = sb("ones", [P, P])
        self.zeros = sb("zeros", [P, 28 * (F + 2)])
        self.pid = sb("pid", [P, 1])
        self.waste = sb("waste", [P, 1])
        self.ln_eps = sb("ln_eps", [P, 1])
        self.eid1 = sb("eid1", [P, T])
        self.gidx = {k: sb("gidx_" + k, [P, TP], i32) for k in ("src", "dst")}
        self.key = {k: sb("key_" + k, [P, T]) for k in ("src", "dst", "type")}
        self.rank = {k: sb("rank_" + k, [P, T]) for k in ("src", "dst")}
        self.sidx = {k: sb("sidx_" + k, [P, T], i32) for k in ("src", "dst")}
        self.rounds = sb("rounds", [1, 1], i32)
        self.C = sb("C", [P, T, TAPS])
        self.WB = sb("WB", [P, G, TAPS, F + 1])
        self.RA = sb("RA", [P, G])
        self.ROOT = sb("ROOT", [P, P])
        self.bias0 = sb("bias0", [P, F])
        self.W1S = sb("W1S", [P, 2, P])
        self.W1D = sb("W1D", [P, 2, P])
        self.W1E = sb("W1E", [P, 2, P])
        self.b1col = sb("b1col", [P, 1])
        self.W2B = sb("W2B", [P, 2 * F])
        self.b2row = sb("b2row", [P, F])
        self.V1 = sb("V1", [P, T, F + 1])
        self.WB2 = sb("WB2", [P, G, NB, F])
        self.A1B = sb("A1B", [P, P])
        self.A2B = sb("A2B", [P, P])
        self.SLB = sb("SLB", [P, P])
        self.WCR = sb("WCR", [P, NB + F])
        self.a1row = sb("a1row", [P, F])
        self.a2row = sb("a2row", [P, F])
        self.W3B = sb("W3B", [P, P])
        self.b3row = sb("b3row", [P, F])
        self.wstage = sb("wstage", [P, TAPS, F])


def setup(nc, t, M):
    with ExitStack() as ctx:
        sb = lambda name, shape, dt=fp32: ctx.enter_context(nc.sbuf_tensor(name, shape, dt))
        taken = []
        sem = M.sems.phase("set_", taken)
        keyI = {k: sb("keyI_" + k, [P, T], i32) for k in ("src", "dst", "type")}
        kT = sb("kT", [T // 2, 3, 2, P])
        kB = sb("kB", [P, 2, G, P])
        attr = sb("attr", [P, T, 2])
        dist = sb("dist", [P, T, 2])
        hat = sb("hat", [P, T, 2, KS])
        fall = sb("fall", [P, T, 2, KS])
        rise = sb("rise", [P, T, 2, KS])
        rootw = sb("rootw", [P, F])
        att = sb("att", [P, 2, F])
        watt = sb("watt", [P, TAPS, F])
        wattk = sb("wattk", [P, TAPS])
        rattf = sb("rattf", [P, F])
        ratt = sb("ratt", [P, 1])
        a12 = sb("a12", [F, 2, G, F])
        same = sb("same", [P, G, P])
        again = sb("again", [P, T])
        pad = sb("pad", [P, T])
        gap = sb("gap", [P, T])
        rmax = sb("rmax", [P, 1])
        rmax1 = sb("rmax1", [1, 1])
        psK = [ctx.enter_context(nc.psum_tensor(f"psK{h}", [P, 3, P], fp32)) for h in range(2)]
        psR = ctx.enter_context(nc.psum_tensor("psR", [P, P], fp32))
        psW = ctx.enter_context(nc.psum_tensor("psW", [P, 2, F], fp32))
        s_zero = sem("zeroed")
        s_fill = sem("filled")
        s_sel = sem("masks")
        s_idx = sem("indices")
        s_attr = sem("attr")
        s_w = sem("weights")
        s_wz = sem("weights_cleared")
        s_kf = sem("keys_float")
        s_kp = sem("keys_transposed")
        s_kc = sem("keys_copied")
        s_kt = sem("keys_stored")
        s_kb = [sem(f"set_keys_spread{u}") for u in range(2)]
        s_kbu = sem("keys_free")
        s_mr = sem("rank_max")
        s_mp = sem("rank_row")
        s_dve = sem("dve_steps")
        block = ctx.enter_context(nc.Block())
        half = T // 2
        n_weights = [0]

        @block.sync
        def _(sp):
            sp.wait_ge(s_fill, 1)
            view = lambda a: a.rearrange("(p t) -> p t", p=ROWS_E)
            for k in ("src", "dst"):
                sp.dma_start(M.gidx[k][0:ROWS_E, 0:T], view(t[k])).then_inc(s_idx, 16)
                sp.dma_start(keyI[k][0:ROWS_E, :], view(t[k])).then_inc(s_idx, 16)
            sp.dma_start(keyI["type"][0:ROWS_E, :], view(t["edge_type_86"])).then_inc(s_idx, 16)
            sp.dma_start(attr[0:ROWS_E, :, :],
                         t["edge_attr_2"].rearrange("(p t) d -> p t d", p=ROWS_E)).then_inc(s_attr, 16)

            sp.wait_ge(s_kc, 2)
            for n, k in enumerate(("src", "dst", "type")):
                sp.dma_start(M.keyT[k].rearrange("(h a) p -> a h p", h=2), kT[:, n, :, :]).then_inc(s_kt, 16)
            sp.wait_ge(s_kt, 48)
            for n, k in enumerate(("src", "dst")):
                with sp.Fori(0, NG // 2) as i:
                    for u in range(2):
                        g = 2 * i + u
                        sp.wait_ge(s_kbu, n * NG + g + 1)
                        sp.nop(nofuse=True)
                        sp.dma_start(kB[:, u, :, :], M.keyT[k][cols(g), :].unsqueeze(0)
                                     .to_broadcast([P, G, P])).then_inc(s_kb[u], 16)

        @block.scalar
        def _(act):
            act.wait_ge(s_fill, 1)
            for tab in M.softmax_state:
                w = tab.shape[1]
                act.dma_start(tab.rearrange("(p a r) w -> p a (r w)", p=P, a=28),
                              along(M.zeros[:, 0:28 * w], 28)).then_inc(s_zero, 16)
            act.wait_ge(s_wz, 1)
            w0 = t["L0_gnn_weight"].rearrange("k f o -> f k o")
            w2 = t["L2_gnn_weight"].rearrange("b i o -> i b o")
            root = t["L0_gnn_root_weight"]
            w1 = t["L1_gnn_W1"]
            row = lambda a: a.rearrange("(a f) -> a f", a=1).to_broadcast([P, F])

            def load(dst, src):
                act.dma_start(dst, src).then_inc(s_w, 16)
                n_weights[0] += 1

            for i in range(G):
                b = slice(F * i, F * i + F)
                load(M.wstage[b, :, :], w0)
                load(rootw[b, :], root)
                load(M.ROOT[b, b], root)
                load(M.WB2[b, i, :, :], w2)
                load(M.SLB[b, b], t["L2_gnn_self_loop_weight"])
                load(M.W3B[b, b], t["L3_gnn_W"])
                j, c = i // 2, slice(HID * (i % 2), HID * (i % 2) + HID)
                load(M.W1S[b, j, c], w1[0:F, :])
                load(M.W1D[b, j, c], w1[F:2 * F, :])
                load(M.W1E[b, j, c], w1[2 * F:3 * F, :])
                for n, a in enumerate((t["L2_gnn_A1_w"], t["L2_gnn_A2_w"])):
                    load(a12[:, n, i, :], a)
            for i in range(2):
                b = slice(HID * i, HID * i + HID)
                load(M.b1col[b, :], t["L1_gnn_b1"].rearrange("(f a) -> f a", a=1))
                load(M.W2B[b, F * i:F * i + F], t["L1_gnn_W2"])
                load(att[:, i, :], row(t["L0_gnn_att_weight"][F * i:F * i + F]))
            load(M.bias0[:, :], row(t["L0_gnn_bias"]))
            load(M.b2row[:, :], row(t["L1_gnn_b2"]))
            load(M.a1row[:, :], row(t["L2_gnn_A1_b"]))
            load(M.a2row[:, :], row(t["L2_gnn_A2_b"]))
            load(M.b3row[:, :], row(t["L3_gnn_b"]))
            load(M.WCR[0:REL, 0:NB], t["L2_gnn_w_comp"])
            load(M.WCR[0:REL, NB:NB + F], t["L2_gnn_rel_emb"])
            act.wait_ge(s_w, 16 * n_weights[0])
            act.wait_ge(s_zero, 32)

        @block.gpsimd
        def _(pool):
            nc.gpsimd.memset(M.zeros[:, :], 0.0)
            for k in ("src", "dst"):
                nc.gpsimd.memset(M.gidx[k][:, :], 0)
                nc.gpsimd.memset(keyI[k][:, :], PAD_KEY)
            nc.gpsimd.memset(attr[:, :, :], 0.0)
            nc.gpsimd.memset(keyI["type"][:, :], 0).then_inc(s_fill, 1)
            nc.gpsimd.memset(M.ident[:, :], 0.0).then_inc(s_sel, 1)
            nc.gpsimd.memset(M.lower[:, :], 1.0).then_inc(s_sel, 1)
            nc.gpsimd.memset(M.ones[:, :], 1.0)
            nc.gpsimd.memset(M.ln_eps[:, :], LN_EPS)
            nc.gpsimd.iota(M.pid[:, :], [[0, 1]], base=0, channel_multiplier=1,
                           allow_small_or_imprecise_dtypes=True)
            nc.gpsimd.iota(M.waste[:, :], [[0, 1]], base=N, channel_multiplier=1,
                           allow_small_or_imprecise_dtypes=True)
            nc.gpsimd.iota(M.eid1[:, :], [[1, T]], base=1, channel_multiplier=T,
                           allow_small_or_imprecise_dtypes=True)
            pool.wait_ge(s_sel, 2)
            nc.gpsimd.affine_select(out=M.ident[:, :], in_=M.ident[:, :], compare_op=ALU.not_equal, fill=1.0,
                                    base=0, pattern=[[-1, P]], channel_multiplier=1).then_inc(s_sel, 1)
            nc.gpsimd.affine_select(out=M.lower[:, :], in_=M.lower[:, :], compare_op=ALU.is_gt, fill=0.0,
                                    base=0, pattern=[[-1, P]], channel_multiplier=1).then_inc(s_sel, 1)

        @block.tensor
        def _(pe):
            pe.wait_ge(s_kf, 1)
            pe.wait_ge(s_sel, 4)
            for h in range(2):
                for n, k in enumerate(("src", "dst", "type")):
                    last = nc.tensor.transpose(psK[h][0:half, n, :], M.key[k][:, half * h:half * h + half],
                                               M.ident[:, :])
            last.then_inc(s_kp, 1)
            pe.wait_ge(s_w, 16 * n_weights[0])
            for n in range(2):
                last = nc.tensor.transpose(psW[:, n, :], a12[:, n, :, :].rearrange("a i f -> a (i f)"),
                                           M.ident[0:F, 0:F])
            last.then_inc(s_kp, 1)
            pe.wait_ge(s_mr, 1)
            nc.tensor.transpose(psR[0:1, :], rmax[:, :], M.ident[:, :]).then_inc(s_mp, 1)

        @block.vector
        def _(dve):
            s = Steps(dve, s_dve)
            nc.vector.memset(M.WB[:, :, :, :], 0.0)
            nc.vector.memset(M.WB2[:, :, :, :], 0.0)
            for w in (M.RA, M.ROOT, M.A1B, M.A2B, M.SLB, M.W3B, M.W2B, M.WCR):
                nc.vector.memset(w[:, :], 0.0)
            for w in (M.W1S, M.W1D):
                nc.vector.memset(w[:, :, :], 0.0)
            nc.vector.memset(M.W1E[:, :, :], 0.0).then_inc(s_wz, 1)
            nc.vector.sem_inc(s_kbu, 2)
            dve.wait_ge(s_idx, 80)
            for k in ("src", "dst", "type"):
                last = nc.vector.tensor_copy(M.key[k][:, :], keyI[k][:, :])
            last.then_inc(s_kf, 1)
            dve.wait_ge(s_attr, 16)
            s.done(nc.vector.tensor_scalar(dist[:, :, :], attr[:, :, :], float(KS - 1), 0.0, ALU.mult, ALU.max))
            s.sync()
            s.done(nc.vector.tensor_scalar(dist[:, :, :], dist[:, :, :], float(KS - 1), None, ALU.min))
            s.sync()
            for j in range(KS):
                s.done(nc.vector.tensor_scalar(hat[:, :, :, j], dist[:, :, :], float(-j), None, ALU.add))
            s.sync()
            s.done(nc.vector.tensor_scalar(fall[:, :, :, :], hat[:, :, :, :], -1.0, 1.0, ALU.mult, ALU.add))
            s.done(nc.vector.tensor_scalar(rise[:, :, :, :], hat[:, :, :, :], 1.0, None, ALU.add))
            s.sync()
            s.done(nc.vector.tensor_tensor(hat[:, :, :, :], fall[:, :, :, :], rise[:, :, :, :], ALU.min))
            s.sync()
            s.done(nc.vector.tensor_scalar(hat[:, :, :, :], hat[:, :, :, :], 0.0, None, ALU.max))
            s.sync()
            taps = M.C[:, :, :].rearrange("p t (b a) -> p t b a", b=KS)
            for b in range(KS):
                s.done(nc.vector.tensor_tensor(taps[:, :, b, :], hat[:, :, 0, :], rep(hat[:, :, 1, b], KS), ALU.mult))
            dve.wait_ge(s_kp, 1)
            for h in range(2):
                nc.vector.tensor_copy(kT[:, :, h, :], psK[h][0:half, :, :]).then_inc(s_kc, 1)
            dve.wait_ge(s_w, 16 * n_weights[0])
            s.done(nc.vector.tensor_tensor(watt[:, :, :], M.wstage[:, :, :], along(att[:, 1, :], TAPS), ALU.mult))
            s.done(nc.vector.tensor_tensor(rattf[:, :], rootw[:, :], att[:, 0, :], ALU.mult))
            s.sync()
            s.done(nc.vector.reduce_sum(wattk[:, :], watt[:, :, :], AX.X))
            s.done(nc.vector.reduce_sum(ratt[:, :], rattf[:, :], AX.X))
            s.sync()
            dve.wait_ge(s_kp, 2)
            for i in range(G):
                b = slice(F * i, F * i + F)
                s.done(nc.vector.tensor_copy(M.WB[b, i, :, 0:F], M.wstage[b, :, :]))
                s.done(nc.vector.tensor_copy(M.WB[b, i, :, F], wattk[b, :]))
                s.done(nc.vector.tensor_copy(M.RA[b, i:i + 1], ratt[b, :]))
                s.done(nc.vector.tensor_copy(M.A1B[b, b], psW[b, 0, :]))
                s.done(nc.vector.tensor_copy(M.A2B[b, b], psW[b, 1, :]))
            dve.wait_ge(s_sel, 4)
            for n, k in enumerate(("src", "dst")):
                with dve.Fori(0, NG // 2) as i:
                    for u in range(2):
                        g = 2 * i + u
                        dve.wait_ge(s_kbu, n * NG + g + 2)
                        dve.wait_ge(s_kb[u], (n * (NG // 2) + i + 1) * 16)
                        for j in range(G):
                            last = nc.vector.scalar_tensor_tensor(
                                same[:, j, :], kB[:, u, j, :], M.key[k][:, bass.ds(G * g + j, 1)], M.lower[:, :],
                                ALU.is_equal, ALU.mult, accum_out=M.rank[k][:, bass.ds(G * g + j, 1)])
                        last.then_inc(s_kbu, 1)
            dve.wait_ge(s_kbu, 2 + 2 * NG)
            for k in ("src", "dst"):
                s.done(nc.vector.tensor_scalar(again[:, :], M.rank[k][:, :], 0.5, None, ALU.is_gt))
                s.done(nc.vector.tensor_scalar(pad[:, :], M.key[k][:, :], float(N), None, ALU.is_ge))
                s.done(nc.vector.tensor_scalar(gap[:, :], M.key[k][:, :], M.waste[:, 0:1], -1.0, ALU.subtract, ALU.mult))
                s.sync()
                s.done(nc.vector.tensor_tensor(again[:, :], again[:, :], pad[:, :], ALU.max))
                s.sync()
                s.done(nc.vector.tensor_tensor(again[:, :], again[:, :], gap[:, :], ALU.mult))
                s.sync()
                s.done(nc.vector.tensor_tensor(M.sidx[k][:, :], again[:, :], M.key[k][:, :], ALU.add))
                s.sync()
            s.done(nc.vector.tensor_scalar(gap[:, :], pad[:, :], -1.0, 1.0, ALU.mult, ALU.add))
            s.sync()
            s.done(nc.vector.tensor_tensor(gap[:, :], M.rank["dst"][:, :], gap[:, :], ALU.mult))
            s.sync()
            nc.vector.reduce_max(rmax[:, :], gap[:, :], AX.X).then_inc(s_mr, 1)
            dve.wait_ge(s_mp, 1)
            s.done(nc.vector.reduce_max(rmax1[:, :], psR[0:1, :], AX.X))
            s.sync()
            s.done(nc.vector.tensor_copy(M.rounds[:, :], rmax1[:, :]))
            s.sync()
    M.sems.retire(taken)


def spread_keys(sp, M, name, buf, free, landed):
    with sp.Fori(0, NG // 2) as i:
        for u in range(2):
            sp.wait_ge(free, 2 * i + u + 1)
            sp.nop(nofuse=True)
            sp.dma_start(buf[:, u, :, :], M.keyT[name][cols(2 * i + u), :].unsqueeze(0)
                         .to_broadcast([P, G, P])).then_inc(landed[u], 16)


def rows_at(idx, j):
    return bass.IndirectOffsetOnAxis(ap=idx[:, j:j + 1], axis=0)


def gather_and_merge(nc, pool, M, key, source, state, X, gi, si, old, new, sems):
    staged, x_in, x_used, state_in, state_out, merged = sems

    def stage_x(g, v):
        for n, k in enumerate(("src", "dst")):
            nc.gpsimd.tensor_copy(gi[v][:, G * n:G * n + G], M.gidx[k][:, cols(g)]).then_inc(staged, 1)

    def gather_x(v, some):
        for j in some:
            nc.gpsimd.indirect_dma_start(out=X[v][:, j, :], out_offset=None, in_=source,
                                         in_offset=rows_at(gi[v], j)).then_inc(x_in[v], 16)

    def gather_state(v, pair):
        for j in pair:
            nc.gpsimd.indirect_dma_start(out=old[j // 2][:, j % 2, :], out_offset=None, in_=state[j % 2],
                                         in_offset=rows_at(si[v], j)).then_inc(state_in[j], 16)

    def scatter_state(v, pair):
        for j in pair:
            nc.gpsimd.indirect_dma_start(out=state[j % 2], out_offset=rows_at(si[v], j),
                                         in_=new[j // 2][:, j % 2, :], in_offset=None).then_inc(state_out[j], 16)

    def chain(g, v, staged_now, ahead):
        nc.gpsimd.tensor_copy(si[v][:, :], M.sidx[key][:, cols(g)]).then_inc(staged, 1)
        pool.wait_ge(staged, staged_now)
        wait(pool, state_out[2], 16 * g)
        wait(pool, state_out[3], 16 * g)
        pool.nop(nofuse=True)
        gather_state(v, (0, 1))
        ahead(0, 3)
        pool.wait_ge(merged, 2 * g + 1)
        pool.nop(nofuse=True)
        scatter_state(v, (0, 1))
        ahead(3, 5)
        pool.wait_ge(state_out[0], 16 * g + 16)
        pool.wait_ge(state_out[1], 16 * g + 16)
        pool.nop(nofuse=True)
        gather_state(v, (2, 3))
        ahead(5, 7)
        pool.wait_ge(merged, 2 * g + 2)
        pool.nop(nofuse=True)
        scatter_state(v, (2, 3))
        ahead(7, 8)

    def body(g, u, h):
        v = 1 - u
        pool.wait_ge(x_used, g)
        pool.nop(nofuse=True)
        stage_x(g + 1, v)
        chain(g - 1, v, 3 * g + 4, lambda a, b: gather_x(v, range(a, b)))

    stage_x(0, 0)
    stage_x(1, 1)
    pool.wait_ge(staged, 4)
    gather_x(0, range(2 * G))
    gather_x(1, range(2 * G))
    each_group(pool, body)
    chain(NG - 1, 1, 3 * NG + 2, lambda a, b: None)
    for j in range(G):
        pool.wait_ge(state_out[j], 16 * NG)
    pool.wait_ge(x_in[0], 16 * 2 * G * (NG // 2 + 1))
    pool.wait_ge(x_in[1], 16 * 2 * G * (NG // 2))


NORM_SEMS = ("centred", "squared", "summed", "rooted", "scaled")


def norm_vector(nc, dve, s, x, n, b, sems, g):
    centred, squared, summed, rooted, scaled = sems
    s.done(nc.vector.reduce_sum(b["total"][:, :], x, AX.X))
    s.sync()
    nc.vector.scalar_tensor_tensor(b["diff"][:, :, :], x, float(F), rep(b["total"][:, :], F),
                                   ALU.mult, ALU.subtract).then_inc(centred, 1)
    dve.wait_ge(squared, g + 1)
    nc.vector.reduce_sum(b["ssq"][:, :], b["sq"][:, :, :], AX.X).then_inc(summed, 1)
    dve.wait_ge(rooted, g + 1)
    s.done(nc.vector.reciprocal(b["rstd"][:, :], b["root"][:, :]))
    s.sync()
    nc.vector.tensor_tensor(b["normed"][:, :, :], b["diff"][:, :, :], rep(b["rstd"][:, :], F),
                            ALU.mult).then_inc(scaled, 1)


def norm_scalar(nc, act, M, b, sems, h_ready, g):
    centred, squared, summed, rooted, scaled = sems
    act.wait_ge(centred, g + 1)
    nc.scalar.activation(b["sq"][:, :, :], b["diff"][:, :, :], ACT.Square).then_inc(squared, 1)
    act.wait_ge(summed, g + 1)
    nc.scalar.activation(b["root"][:, :], b["ssq"][:, :], ACT.Sqrt, bias=M.ln_eps[:, 0:1]).then_inc(rooted, 1)
    act.wait_ge(scaled, g + 1)
    nc.scalar.activation(b["h"][:, :, :], b["normed"][:, :, :], ACT.Relu, scale=LN_GAIN).then_inc(h_ready, 1)


def norm_buffers(sb, n):
    return dict(total=sb("total", [P, n]), diff=sb("diff", [P, n, F]), sq=sb("sq", [P, n, F]),
                ssq=sb("ssq", [P, n]), root=sb("root", [P, n]), rstd=sb("rstd", [P, n]), normed=sb("normed", [P, n, F]),
                h=sb("h", [P, n, F]))


def layer0_edges(nc, t, M):
    with ExitStack() as ctx:
        sb = lambda name, shape, dt=fp32: ctx.enter_context(nc.sbuf_tensor("e0_" + name, shape, dt))
        ps = lambda name, shape: ctx.enter_context(nc.psum_tensor("e0_" + name, shape, fp32))
        taken = []
        sem = M.sems.phase("e0_", taken)
        W = F + 2
        DEN, MAX = F, F + 1
        X = [sb(f"X{u}", [P, 2 * G, F]) for u in range(2)]
        gi = [sb(f"gi{u}", [P, 2 * G], i32) for u in range(2)]
        si = [sb(f"si{u}", [P, G], i32) for u in range(2)]
        keys = sb("keys", [P, 2, G, P])
        nb = norm_buffers(sb, 2 * G)
        h = nb["h"]
        hT = sb("hT", [P, 2, P])
        prod = [sb(f"prod{b}", [P, TAPS, F + 1]) for b in range(2)]
        msg = sb("msg", [P, G, F + 1])
        score = sb("score", [P, G])
        alpha = sb("alpha", [P, G])
        same = sb("same", [P, G, P])
        off = sb("off", [P, G, P])
        diag = sb("diag", [P, G, P])
        masked = sb("masked", [P, G, P])
        less = sb("less", [P, G])
        V = sb("V", [P, G, F + 1])
        part = [sb(f"part{u}", [P, G, W]) for u in range(2)]
        old = [sb(f"old{q}", [P, 2, W]) for q in range(2)]
        new = [sb(f"new{q}", [P, 2, W]) for q in range(2)]
        empty = sb("empty", [P, 2])
        was_max = sb("was_max", [P, 2])
        gaps = sb("gaps", [P, 2, 2])
        fade = sb("fade", [P, 2, 2])
        kept = sb("kept", [P, 2, F + 1])
        added = sb("added", [P, 2, F + 1])
        psT = ps("psT", [P, 2, P])
        psX = [[ps(f"psX{b}{c}", [P, 512]) for c in range(2)] for b in range(2)]
        psA = ps("psA", [P, G, P])
        psS = ps("psS", [P, G])
        psV = ps("psV", [P, G, F + 1])

        staged = sem("staged")
        x_in = [sem(f"x_in{u}") for u in range(2)]
        state_in = [sem(f"state_in{j}") for j in range(G)]
        state_out = [sem(f"state_out{j}") for j in range(G)]
        keys_in = [sem(f"keys_in{u}") for u in range(2)]
        keys_free = sem("keys_free")
        norm_sems = [sem(n) for n in NORM_SEMS]
        h_ready, hT_psum, hT_ready = sem("h_ready"), sem("hT_psum"), sem("hT_ready")
        taps_ready, taps_used = sem("taps_ready"), sem("taps_used")
        score_ready, alpha_ready, diag_ready = sem("score_ready"), sem("alpha_ready"), sem("diag_ready")
        spread_ready, less_ready, ex_ready = sem("spread_ready"), sem("less_ready"), sem("ex_ready")
        V_ready, sums_ready = sem("V_ready"), sem("sums_ready")
        gaps_ready, fade_ready, merged = sem("gaps_ready"), sem("fade_ready"), sem("merged")
        s_dve, cleared = sem("dve_steps"), sem("cleared")
        block = ctx.enter_context(nc.Block())

        @block.sync
        def _(sp):
            M.sems.clear(sp)
            for tab in M.max_state + [M.rel_sums]:
                w = tab.shape[1]
                sp.dma_start(tab.rearrange("(p a r) w -> p a (r w)", p=P, a=28),
                             along(M.zeros[:, 0:28 * w], 28)).then_inc(cleared, 16)
            spread_keys(sp, M, "src", keys, keys_free, keys_in)
            sp.wait_ge(cleared, 48)

        @block.gpsimd
        def _(pool):
            gather_and_merge(nc, pool, M, "src", t["x"], M.softmax_state, X, gi, si, old, new,
                             (staged, x_in, norm_sems[0], state_in, state_out, merged))

        @block.scalar
        def _(act):
            def merge(pair, g):
                act.wait_ge(gaps_ready, 2 * g + pair + 1)
                nc.scalar.activation(fade[:, :, :], gaps[:, :, :], ACT.Exp).then_inc(fade_ready, 1)

            def edges(g, between):
                norm_scalar(nc, act, M, nb, norm_sems, h_ready, g)
                act.wait_ge(hT_psum, g + 1)
                nc.scalar.activation(hT[:, :, :], psT[:, :, :], ACT.Copy).then_inc(hT_ready, 1)
                between()
                act.wait_ge(alpha_ready, g + 1)
                for j in range(G):
                    last = nc.scalar.activation(diag[:, j, :], M.ident[:, :], ACT.Copy, scale=alpha[:, j:j + 1])
                last.then_inc(diag_ready, 1)
                act.wait_ge(less_ready, g + 1)
                nc.scalar.activation(V[:, :, F], less[:, :], ACT.Exp).then_inc(ex_ready, 1)

            def body(g, u, i):
                merge(0, g - 1)
                edges(g, lambda: merge(1, g - 1))

            edges(0, lambda: None)
            each_group(act, body)
            merge(0, NG - 1)
            merge(1, NG - 1)

        @block.tensor
        def _(pe):
            def edges(g):
                pe.wait_ge(h_ready, g + 1)
                for n in range(2):
                    last = nc.tensor.transpose(psT[:, n, :], h[:, G * n:G * n + G, :].rearrange("p a f -> p (a f)"),
                                               M.ident[:, :])
                last.then_inc(hT_psum, 1)
                pe.wait_ge(hT_ready, g + 1)
                nc.tensor.matmul(psS[:, :], hT[:, 0, :], M.RA[:, :], start=True, stop=True).then_inc(score_ready, 1)
                for j in range(G):
                    wait(pe, taps_used, G * g + j - 1)
                    w = M.WB[:, j, :, :].rearrange("p k o -> p (k o)")
                    cut = TC * (F + 1)
                    nc.tensor.matmul(psX[j % 2][0][:, 0:cut], hT[:, 1, :], w[:, 0:cut], start=True, stop=True)
                    nc.tensor.matmul(psX[j % 2][1][:, 0:TAPS * (F + 1) - cut], hT[:, 1, :], w[:, cut:],
                                     start=True, stop=True).then_inc(taps_ready, 1)
                pe.wait_ge(diag_ready, g + 1)
                nc.tensor.matmul(psA[:, :, :].rearrange("p a b -> p (a b)"), M.ones[:, :],
                                 diag[:, :, :].rearrange("p a b -> p (a b)"),
                                 start=True, stop=True).then_inc(spread_ready, 1)
                pe.wait_ge(V_ready, g + 1)
                for j in range(G):
                    last = nc.tensor.matmul(psV[:, j, :], same[:, j, :], V[:, j, :], start=True, stop=True)
                last.then_inc(sums_ready, 1)

            edges(0)
            each_group(pe, lambda g, u, i: edges(g))

        @block.vector
        def _(dve):
            s = Steps(dve, s_dve)

            def merge(pair, g, v):
                mine = part[v][:, 2 * pair:2 * pair + 2, :]
                o, n = old[pair], new[pair]
                for j in (2 * pair, 2 * pair + 1):
                    dve.wait_ge(state_in[j], 16 * g + 16)
                s.done(nc.vector.tensor_scalar(empty[:, :], o[:, :, DEN], 0.0, -BIG, ALU.is_equal, ALU.mult))
                s.sync()
                s.done(nc.vector.tensor_tensor(was_max[:, :], o[:, :, MAX], empty[:, :], ALU.add))
                s.sync()
                s.done(nc.vector.tensor_tensor(n[:, :, MAX], was_max[:, :], mine[:, :, MAX], ALU.max))
                s.sync()
                s.done(nc.vector.tensor_tensor(gaps[:, 0, :], was_max[:, :], n[:, :, MAX], ALU.subtract))
                nc.vector.tensor_tensor(gaps[:, 1, :], mine[:, :, MAX], n[:, :, MAX], ALU.subtract).then_inc(gaps_ready, 1)
                dve.wait_ge(fade_ready, 2 * g + pair + 1)
                s.done(nc.vector.tensor_tensor(kept[:, :, :], o[:, :, 0:F + 1], rep(fade[:, 0, :], F + 1), ALU.mult))
                s.done(nc.vector.tensor_tensor(added[:, :, :], mine[:, :, 0:F + 1], rep(fade[:, 1, :], F + 1), ALU.mult))
                s.sync()
                nc.vector.tensor_tensor(n[:, :, 0:F + 1], kept[:, :, :], added[:, :, :], ALU.add).then_inc(merged, 1)

            def message(g, j):
                dve.wait_ge(taps_ready, G * g + j + 1)
                coef = M.C[:, bass.ds(G * g + j, 1), :].rearrange("p a k -> p (a k)")
                for c, (lo, hi) in enumerate(((0, TC), (TC, TAPS))):
                    last = nc.vector.tensor_tensor(
                        prod[j % 2][:, lo:hi, :], psX[j % 2][c][:, 0:(hi - lo) * (F + 1)].rearrange("p (k o) -> p k o", o=F + 1),
                        rep(coef[:, lo:hi], F + 1), ALU.mult)
                    if c == 0:
                        s.done(last)
                last.then_inc(taps_used, 1)
                s.sync()
                dve.wait_ge(taps_used, G * g + j + 1)
                s.done(nc.vector.reduce_sum(msg[:, j, :], prod[j % 2][:, :, :].rearrange("p k o -> p o k"), AX.X))

            def edges(g, u, i, between):
                dve.wait_ge(x_in[u], 16 * 2 * G * (i + 1))
                norm_vector(nc, dve, s, X[u][:, :, :], 2 * G, nb, norm_sems, g)
                dve.wait_ge(keys_in[u], 16 * (i + 1))
                keyc = M.key["src"][:, cols(g)]
                s.done(nc.vector.tensor_tensor(same[:, :, :], keys[:, u, :, :], rep(keyc, P), ALU.is_equal))
                s.sync()
                nc.vector.tensor_scalar(off[:, :, :], same[:, :, :], 1.0, BIG, ALU.subtract, ALU.mult).then_inc(keys_free, 1)
                message(g, 0)
                message(g, 1)
                between()
                message(g, 2)
                message(g, 3)
                dve.wait_ge(score_ready, g + 1)
                s.sync()
                s.done(nc.vector.tensor_tensor(score[:, :], msg[:, :, F], psS[:, :], ALU.add))
                s.sync()
                nc.vector.scalar_tensor_tensor(alpha[:, :], score[:, :], SLOPE, score[:, :],
                                               ALU.mult, ALU.max).then_inc(alpha_ready, 1)
                dve.wait_ge(spread_ready, g + 1)
                dve.wait_ge(keys_free, g + 3)
                s.done(nc.vector.tensor_tensor(masked[:, :, :], off[:, :, :], psA[:, :, :], ALU.add))
                s.sync()
                s.done(nc.vector.reduce_max(part[u][:, :, MAX], masked[:, :, :], AX.X))
                s.sync()
                nc.vector.tensor_tensor(less[:, :], alpha[:, :], part[u][:, :, MAX], ALU.subtract).then_inc(less_ready, 1)
                dve.wait_ge(ex_ready, g + 1)
                nc.vector.tensor_tensor(V[:, :, 0:F], msg[:, :, 0:F], rep(V[:, :, F], F), ALU.mult).then_inc(V_ready, 1)
                dve.wait_ge(sums_ready, g + 1)
                s.done(nc.vector.tensor_copy(part[u][:, :, 0:F + 1], psV[:, :, :]))
                s.sync()

            def body(g, u, i):
                s.start(g - 1)
                merge(0, g - 1, 1 - u)
                edges(g, u, i, lambda: merge(1, g - 1, 1 - u))
                s.end()

            nc.vector.sem_inc(keys_free, 2)
            edges(0, 0, 0, lambda: None)
            s.first, s.per = s.n, PER_E0
            each_group(dve, body)
            s.start(NG - 1)
            merge(0, NG - 1, 1)
            merge(1, NG - 1, 1)


def project_pe(nc, pe, M, weights, h, psT, hT, psR, sems, c, u):
    h_ready, hT_psum, hT_ready, round_ready, used = sems
    flat = h[:, :, :].rearrange("p k f -> p (k f)")
    pe.wait_ge(h_ready, c + 1)
    for q in range(3):
        r, b = 3 * c + q, (u + q) % 2
        wait(pe, hT_ready, r - 1)
        for n in range(G):
            last = nc.tensor.transpose(psT[b][:, n, :], flat[:, P * (G * q + n):P * (G * q + n) + P], M.ident[:, :])
        last.then_inc(hT_psum, 1)
        if q == 0:
            wait(pe, used, c)
        pe.wait_ge(hT_ready, r + 1)
        for n in range(G):
            last = nc.tensor.matmul(psR[q][:, P * n:P * n + P], hT[b][:, n, :], weights[:, :], start=True, stop=True)
        last.then_inc(round_ready, 1)


def project_scalar(nc, act, psT, hT, sems, c, u):
    h_ready, hT_psum, hT_ready, round_ready, used = sems
    for q in range(3):
        r, b = 3 * c + q, (u + q) % 2
        act.wait_ge(hT_psum, r + 1)
        wait(act, round_ready, r - 1)
        nc.scalar.activation(hT[b][:, :, :], psT[b][:, :, :], ACT.Copy).then_inc(hT_ready, 1)


def dense0(nc, t, M, dest):
    with ExitStack() as ctx:
        sb = lambda name, shape, dt=fp32: ctx.enter_context(nc.sbuf_tensor("d0_" + name, shape, dt))
        ps = lambda name, shape: ctx.enter_context(nc.psum_tensor("d0_" + name, shape, fp32))
        taken = []
        sem = M.sems.phase("d0_", taken)
        W = F + 2
        DEN, MAX = F, F + 1
        X = [sb(f"X{u}", [P, K, F]) for u in range(2)]
        S = [[sb(f"S{u}{k}", [P, K, W]) for k in range(2)] for u in range(2)]
        Y = [sb(f"Y{u}", [P, K, F]) for u in range(2)]
        nb = norm_buffers(sb, K)
        h = nb["h"]
        hT = [sb(f"hT{q}", [P, G, P]) for q in range(2)]
        empty = sb("empty", [P, 2, K])
        top = sb("top", [P, K])
        gaps = sb("gaps", [P, 2, K])
        fade = sb("fade", [P, 2, K])
        dens = sb("dens", [P, 2, K])
        den = sb("den", [P, K])
        inv = sb("inv", [P, K])
        part = [sb(f"part{k}", [P, K, F]) for k in range(2)]
        was = sb("was", [P, 2, K])
        share = sb("share", [P, 2, K])
        sums = sb("sums", [P, K, F])
        both = sb("both", [P, K, F])
        psT = [ps(f"psT{q}", [P, G, P]) for q in range(2)]
        psR = [ps(f"psR{q}", [P, G * P]) for q in range(3)]
        loaded = [sem(f"loaded{u}") for u in range(2)]
        stored = sem("stored")
        norm_sems = [sem(n) for n in NORM_SEMS]
        h_ready, hT_psum, hT_ready = sem("h_ready"), sem("hT_psum"), sem("hT_ready")
        gaps_ready, fade_ready, share_ready, sums_ready = sem("gaps_ready"), sem("fade_ready"), sem("share_ready"), sem("sums_ready")
        round_ready = sem("round_ready")
        done = sem("done")
        proj_sems = h_ready, hT_psum, hT_ready, round_ready, done
        s_dve, s_pool = sem("dve_steps"), sem("pool_steps")
        block = ctx.enter_context(nc.Block())

        @block.sync
        def _(sp):
            M.sems.clear(sp)
            def load(c, u):
                sp.dma_start(X[u][:, :, :], chunk(t["x"], c)).then_inc(loaded[u], 16)
                for k in range(2):
                    sp.dma_start(S[u][k][:, :, :], chunk(M.softmax_state[k], c)).then_inc(loaded[u], 16)

            def body(c, u, i):
                sp.wait_ge(done, c + 1)
                sp.nop(nofuse=True)
                wait(sp, stored, 16 * c)
                sp.nop(nofuse=True)
                sp.dma_start(chunk(dest, c), Y[u][:, :, :]).then_inc(stored, 16)
                if not isinstance(c, int) or c + 2 < NCH:
                    load(c + 2, u)

            load(0, 0)
            load(1, 1)
            each_chunk(sp, body)
            sp.wait_ge(stored, 16 * NCH)

        @block.gpsimd
        def _(pool):
            s = Steps(pool, s_pool, 3)

            def body(c, u, i):
                s.start(c)
                pool.wait_ge(loaded[u], 48 * (i + 1))
                wait(pool, stored, 16 * (c - 1))
                s.done(nc.gpsimd.tensor_tensor(Y[u][:, :, :], X[u][:, :, :], along(M.bias0[:, :], K), ALU.add))
                pool.wait_ge(share_ready, c + 1)
                for k in range(2):
                    s.done(nc.gpsimd.tensor_tensor(part[k][:, :, :], S[u][k][:, :, 0:F], rep(share[:, k, :], F), ALU.mult))
                s.sync()
                nc.gpsimd.tensor_tensor(sums[:, :, :], part[0][:, :, :], part[1][:, :, :], ALU.add).then_inc(sums_ready, 1)
                s.end()

            each_chunk(pool, body)

        @block.scalar
        def _(act):
            def body(c, u, i):
                act.wait_ge(gaps_ready, c + 1)
                nc.scalar.activation(fade[:, :, :], gaps[:, :, :], ACT.Exp).then_inc(fade_ready, 1)
                norm_scalar(nc, act, M, nb, norm_sems, h_ready, c)
                project_scalar(nc, act, psT, hT, proj_sems, c, u)

            each_chunk(act, body)

        @block.tensor
        def _(pe):
            each_chunk(pe, lambda c, u, i: project_pe(nc, pe, M, M.ROOT, h, psT, hT, psR, proj_sems, c, u))

        @block.vector
        def _(dve):
            s = Steps(dve, s_dve, PER_D0)

            def body(c, u, i):
                s.start(c)
                dve.wait_ge(loaded[u], 48 * (i + 1))
                for k in range(2):
                    s.done(nc.vector.tensor_scalar(empty[:, k, :], S[u][k][:, :, DEN], 0.0, -BIG, ALU.is_equal, ALU.mult))
                s.sync()
                for k in range(2):
                    s.done(nc.vector.tensor_tensor(was[:, k, :], S[u][k][:, :, MAX], empty[:, k, :], ALU.add))
                s.sync()
                s.done(nc.vector.tensor_tensor(top[:, :], was[:, 0, :], was[:, 1, :], ALU.max))
                s.sync()
                nc.vector.tensor_tensor(gaps[:, :, :], was[:, :, :], along(top[:, :], 2), ALU.subtract).then_inc(gaps_ready, 1)
                dve.wait_ge(fade_ready, c + 1)
                for k in range(2):
                    s.done(nc.vector.tensor_tensor(dens[:, k, :], S[u][k][:, :, DEN], fade[:, k, :], ALU.mult))
                s.sync()
                s.done(nc.vector.scalar_tensor_tensor(den[:, :], dens[:, 0, :], 1e-16, dens[:, 1, :], ALU.add, ALU.add))
                s.sync()
                s.done(nc.vector.reciprocal(inv[:, :], den[:, :]))
                s.sync()
                wait(dve, sums_ready, c)
                nc.vector.tensor_tensor(share[:, :, :], fade[:, :, :], along(inv[:, :], 2), ALU.mult).then_inc(share_ready, 1)
                norm_vector(nc, dve, s, X[u][:, :, :], K, nb, norm_sems, c)
                dve.wait_ge(sums_ready, c + 1)
                s.done(nc.vector.tensor_tensor(both[:, :, :], Y[u][:, :, :], sums[:, :, :], ALU.add))
                s.sync()
                dve.wait_ge(round_ready, 3 * c + 3)
                n = G * G
                for q in range(3):
                    last = nc.vector.tensor_tensor(Y[u][:, n * q:n * q + n, :], both[:, n * q:n * q + n, :],
                                                   psR[q][:, :].rearrange("p (k f) -> p k f", f=F), ALU.add)
                    if q < 2:
                        s.done(last)
                last.then_inc(done, 1)
                s.end()

            each_chunk(dve, body)
    M.sems.retire(taken)


def layer1_edges(nc, t, M):
    with ExitStack() as ctx:
        sb = lambda name, shape, dt=fp32: ctx.enter_context(nc.sbuf_tensor("e1_" + name, shape, dt))
        ps = lambda name, shape: ctx.enter_context(nc.psum_tensor("e1_" + name, shape, fp32))
        taken = []
        sem = M.sems.phase("e1_", taken)
        W = F + 1
        X = [sb(f"X{u}", [P, 2 * G, F]) for u in range(2)]
        gi = [sb(f"gi{u}", [P, 2 * G], i32) for u in range(2)]
        si = [sb(f"si{u}", [P, G], i32) for u in range(2)]
        attr = [sb(f"attr{u}", [P, G, F]) for u in range(2)]
        nb = norm_buffers(sb, 2 * G)
        h = nb["h"]
        hT = sb("hT", [P, 3, P])
        hidden = sb("hidden", [P, 2, P])
        biased = sb("biased", [P, G, F])
        old = [sb(f"old{q}", [P, 2, W]) for q in range(2)]
        new = [sb(f"new{q}", [P, 2, W]) for q in range(2)]
        psT = ps("psT", [P, 3, P])
        psH = ps("psH", [P, 2, P])
        psV = ps("psV", [P, G, F])

        staged = sem("staged")
        x_in = [sem(f"x_in{u}") for u in range(2)]
        state_in = [sem(f"state_in{j}") for j in range(G)]
        state_out = [sem(f"state_out{j}") for j in range(G)]
        attr_in = [sem(f"attr_in{u}") for u in range(2)]
        attr_free, attr_clear = sem("attr_free"), sem("attr_clear")
        norm_sems = [sem(n) for n in NORM_SEMS]
        h_ready, hT_psum, hT_ready = sem("h_ready"), sem("hT_psum"), sem("hT_ready")
        hidden_psum, hidden_ready, out_ready = sem("hidden_psum"), sem("hidden_ready"), sem("out_ready")
        merged, s_dve, cleared = sem("merged"), sem("dve_steps"), sem("cleared")
        block = ctx.enter_context(nc.Block())

        @block.sync
        def _(sp):
            M.sems.clear(sp)
            for tab in (M.conv_sums, M.square_sums):
                w = tab.shape[1]
                sp.dma_start(tab.rearrange("(p a r) w -> p a (r w)", p=P, a=28),
                             along(M.zeros[:, 0:28 * w], 28)).then_inc(cleared, 16)
            sp.wait_ge(attr_clear, 1)
            rows = t["edge_attr_32"].rearrange("(p t) f -> p t f", p=ROWS_E)
            with sp.Fori(0, NG // 2) as i:
                for u in range(2):
                    sp.wait_ge(attr_free, 2 * i + u + 1)
                    sp.nop(nofuse=True)
                    sp.dma_start(attr[u][0:ROWS_E, :, :], rows[:, cols(2 * i + u), :]).then_inc(attr_in[u], 16)
            sp.wait_ge(cleared, 32)

        @block.gpsimd
        def _(pool):
            gather_and_merge(nc, pool, M, "dst", M.x1, M.max_state, X, gi, si, old, new,
                             (staged, x_in, norm_sems[0], state_in, state_out, merged))

        @block.scalar
        def _(act):
            def edges(g):
                norm_scalar(nc, act, M, nb, norm_sems, h_ready, g)
                act.wait_ge(hT_psum, g + 1)
                nc.scalar.activation(hT[:, :, :], psT[:, :, :], ACT.Copy).then_inc(hT_ready, 1)
                act.wait_ge(hidden_psum, g + 1)
                nc.scalar.activation(hidden[:, :, :], psH[:, :, :], ACT.Relu, bias=M.b1col[:, 0:1]).then_inc(hidden_ready, 1)

            edges(0)
            each_group(act, lambda g, u, i: edges(g))

        @block.tensor
        def _(pe):
            def edges(g, u, i):
                pe.wait_ge(attr_in[u], 16 * (i + 1))
                nc.tensor.transpose(psT[:, 2, :], attr[u][:, :, :].rearrange("p a f -> p (a f)"),
                                    M.ident[:, :]).then_inc(attr_free, 1)
                pe.wait_ge(h_ready, g + 1)
                for n in range(2):
                    last = nc.tensor.transpose(psT[:, n, :], h[:, G * n:G * n + G, :].rearrange("p a f -> p (a f)"),
                                               M.ident[:, :])
                last.then_inc(hT_psum, 1)
                pe.wait_ge(hT_ready, g + 1)
                for j in range(2):
                    for n, w in enumerate((M.W1S, M.W1D, M.W1E)):
                        last = nc.tensor.matmul(psH[:, j, :], w[:, j, :], hT[:, n, :], start=(n == 0), stop=(n == 2))
                last.then_inc(hidden_psum, 1)
                pe.wait_ge(hidden_ready, g + 1)
                for j in range(2):
                    last = nc.tensor.matmul(psV[:, 2 * j:2 * j + 2, :].rearrange("p a f -> p (a f)"), hidden[:, j, :],
                                            M.W2B[:, :], start=True, stop=True)
                last.then_inc(out_ready, 1)

            edges(0, 0, 0)
            each_group(pe, edges)

        @block.vector
        def _(dve):
            s = Steps(dve, s_dve)

            def merge(pair, g):
                lo = G * g + 2 * pair
                mine = M.V1[:, lo:lo + 2, :] if isinstance(lo, int) else M.V1[:, bass.ds(lo, 2), :]
                for j in (2 * pair, 2 * pair + 1):
                    dve.wait_ge(state_in[j], 16 * g + 16)
                nc.vector.tensor_tensor(new[pair][:, :, :], old[pair][:, :, :], mine, ALU.max).then_inc(merged, 1)

            def edges(g, u, i, between):
                dve.wait_ge(x_in[u], 16 * 2 * G * (i + 1))
                norm_vector(nc, dve, s, X[u][:, :, :], 2 * G, nb, norm_sems, g)
                between()
                dve.wait_ge(out_ready, g + 1)
                s.done(nc.vector.tensor_tensor(biased[:, :, :], psV[:, :, :], along(M.b2row[:, :], G), ALU.add))
                s.sync()
                s.done(nc.vector.tensor_scalar(M.V1[:, cols(g), 0:F], biased[:, :, :], 0.0, None, ALU.max))
                s.done(nc.vector.tensor_copy(M.V1[:, cols(g), F], M.eid1[:, cols(g)]))
                s.sync()

            def body(g, u, i):
                s.start(g - 1)
                merge(0, g - 1)
                edges(g, u, i, lambda: merge(1, g - 1))
                s.end()

            for u in range(2):
                last = nc.vector.memset(attr[u][:, :, :], 0.0)
            last.then_inc(attr_clear, 1)
            nc.vector.sem_inc(attr_free, 2)
            edges(0, 0, 0, lambda: None)
            s.first, s.per = s.n, PER_E1
            each_group(dve, body)
            merge(0, NG - 1)
            merge(1, NG - 1)


def more_maxima(nc, M):
    with ExitStack() as ctx:
        sb = lambda name, shape, dt=fp32: ctx.enter_context(nc.sbuf_tensor("r1_" + name, shape, dt))
        taken = []
        sem = M.sems.phase("r1_", taken)
        W = F + 1
        ridx = sb("ridx", [P, T], i32)
        si = sb("si", [P, 2], i32)
        old = sb("old", [P, 2, W])
        new = sb("new", [P, 2, W])
        turn = sb("turn", [P, 2])
        other = sb("other", [P, T])
        pad = sb("pad", [P, T])
        gap = sb("gap", [P, T])
        shift = sb("shift", [P, T])
        chosen, staged, state_in, merged, state_out = (sem(n) for n in ("chosen", "staged", "state_in", "merged", "state_out"))
        state_in = [sem(f"state_in_{k}") for k in range(2)]
        state_out = [sem(f"state_out_{k}") for k in range(2)]
        s_dve, round_over = sem("dve_steps"), sem("round_over")
        block = ctx.enter_context(nc.Block())
        pairs = T // 2

        @block.gpsimd
        def _(pool):
            rounds = pool.value_load(M.rounds[0:1, 0:1], min_val=0, max_val=P)
            with pool.If(rounds > 0):
                with pool.Fori(0, rounds) as r:
                    pool.wait_ge(chosen, r + 1)
                    pool.nop(nofuse=True)
                    with pool.Fori(0, pairs) as i:
                        n = r * pairs + i
                        nc.gpsimd.tensor_copy(si[:, :], ridx[:, bass.ds(2 * i, 2)]).then_inc(staged, 1)
                        pool.wait_ge(staged, n + 1)
                        pool.nop(nofuse=True)
                        for k in range(2):
                            nc.gpsimd.indirect_dma_start(out=old[:, k, :], out_offset=None, in_=M.max_state[k],
                                                         in_offset=rows_at(si, k)).then_inc(state_in[k], 16)
                        pool.wait_ge(merged, n + 1)
                        pool.nop(nofuse=True)
                        for k in range(2):
                            nc.gpsimd.indirect_dma_start(out=M.max_state[k], out_offset=rows_at(si, k),
                                                         in_=new[:, k, :], in_offset=None).then_inc(state_out[k], 16)
                        pool.wait_ge(state_out[0], 16 * n + 16)
                        pool.wait_ge(state_out[1], 16 * n + 16)
                        pool.nop(nofuse=True)

        @block.vector
        def _(dve):
            rounds = dve.value_load(M.rounds[0:1, 0:1], min_val=0, max_val=P)
            s = Steps(dve, s_dve)
            s.done(nc.vector.memset(turn[:, 0:1], 0.0))
            s.done(nc.vector.tensor_scalar(pad[:, :], M.key["dst"][:, :], float(N), None, ALU.is_ge))
            s.done(nc.vector.tensor_scalar(gap[:, :], M.key["dst"][:, :], M.waste[:, 0:1], -1.0, ALU.subtract, ALU.mult))
            s.sync()
            s.first, s.per = s.n, PER_R1
            with dve.If(rounds > 0):
                with dve.Fori(0, rounds) as r:
                    s.start(r)
                    s.done(nc.vector.tensor_scalar(turn[:, 1:2], turn[:, 0:1], 1.0, None, ALU.add))
                    s.sync()
                    s.done(nc.vector.tensor_copy(turn[:, 0:1], turn[:, 1:2]))
                    s.done(nc.vector.tensor_scalar(other[:, :], M.rank["dst"][:, :], turn[:, 1:2], None, ALU.not_equal))
                    s.sync()
                    s.done(nc.vector.tensor_tensor(shift[:, :], other[:, :], pad[:, :], ALU.max))
                    s.sync()
                    s.done(nc.vector.tensor_tensor(other[:, :], shift[:, :], gap[:, :], ALU.mult))
                    s.sync()
                    nc.vector.tensor_tensor(ridx[:, :], other[:, :], M.key["dst"][:, :], ALU.add).then_inc(chosen, 1)
                    s.end()
                    with dve.Fori(0, pairs) as i:
                        n = r * pairs + i
                        for k in range(2):
                            dve.wait_ge(state_in[k], 16 * n + 16)
                        nc.vector.tensor_tensor(new[:, :, :], old[:, :, :], M.V1[:, bass.ds(2 * i, 2), :],
                                                ALU.max).then_inc(merged, 1)


def dense1(nc, t, M, early):
    with ExitStack() as ctx:
        sb = lambda name, shape, dt=fp32: ctx.enter_context(nc.sbuf_tensor("d1_" + name, shape, dt))
        taken = []
        sem = M.sems.phase("d1_", taken)
        W = F + 1
        X = [sb(f"X{u}", [P, K, F]) for u in range(2)]
        S = [[sb(f"S{u}{k}", [P, K, W]) for k in range(2)] for u in range(2)]
        Y = [sb(f"Y{u}", [P, K, W]) for u in range(2)]
        nb = norm_buffers(sb, K)
        top = sb("top", [P, K, W])
        best = sb("best", [P, K, F])
        loaded = [sem(f"loaded{u}") for u in range(2)]
        stored, norm_sems = sem("stored"), [sem(n) for n in NORM_SEMS]
        h_ready, best_ready, done = sem("h_ready"), sem("best_ready"), sem("done")
        s_dve = sem("dve_steps")
        block = ctx.enter_context(nc.Block())

        @block.sync
        def _(sp):
            M.sems.clear(sp)
            def load(c, u):
                sp.dma_start(X[u][:, :, :], chunk(M.x1, c)).then_inc(loaded[u], 16)
                for k in range(2):
                    sp.dma_start(S[u][k][:, :, :], chunk(M.max_state[k], c)).then_inc(loaded[u], 16)

            def body(c, u, i):
                sp.wait_ge(done, c + 1)
                sp.nop(nofuse=True)
                wait(sp, stored, 16 * c)
                sp.nop(nofuse=True)
                if early:
                    sp.dma_start(chunk(early, c), Y[u][:, :, 0:F]).then_inc(stored, 16)
                else:
                    sp.dma_start(chunk(M.x2, c), Y[u][:, :, :]).then_inc(stored, 16)
                if not isinstance(c, int) or c + 2 < NCH:
                    load(c + 2, u)

            load(0, 0)
            load(1, 1)
            each_chunk(sp, body)
            sp.wait_ge(stored, 16 * NCH)

        @block.gpsimd
        def _(pool):
            def body(c, u, i):
                pool.wait_ge(loaded[u], 48 * (i + 1))
                pool.wait_ge(best_ready, c + 1)
                nc.gpsimd.tensor_tensor(Y[u][:, :, 0:F], X[u][:, :, :], best[:, :, :], ALU.add).then_inc(done, 1)

            each_chunk(pool, body)

        @block.scalar
        def _(act):
            each_chunk(act, lambda c, u, i: norm_scalar(nc, act, M, nb, norm_sems, h_ready, c))

        @block.vector
        def _(dve):
            s = Steps(dve, s_dve, PER_D1)

            def body(c, u, i):
                s.start(c)
                dve.wait_ge(loaded[u], 48 * (i + 1))
                norm_vector(nc, dve, s, X[u][:, :, :], K, nb, norm_sems, c)
                s.done(nc.vector.tensor_tensor(top[:, :, :], S[u][0][:, :, :], S[u][1][:, :, :], ALU.max))
                s.sync()
                wait(dve, stored, 16 * (c - 1))
                s.done(nc.vector.tensor_copy(Y[u][:, :, F], top[:, :, F]))
                dve.wait_ge(h_ready, c + 1)
                wait(dve, done, c)
                nc.vector.tensor_tensor(best[:, :, :], nb["h"][:, :, :], top[:, :, 0:F], ALU.max).then_inc(best_ready, 1)
                s.end()

            each_chunk(dve, body)
    M.sems.retire(taken)


def gather_and_add(nc, pool, M, wanted, key, source, sums, X, gi, si, part, sems):
    staged, x_in, x_used, part_ready, landed = sems
    nx = G * len(wanted)

    def stage_x(g, v):
        for n, k in enumerate(wanted):
            nc.gpsimd.tensor_copy(gi[v][:, G * n:G * n + G], M.gidx[k][:, cols(g)]).then_inc(staged, 1)

    def gather_x(v, some):
        for j in some:
            nc.gpsimd.indirect_dma_start(out=X[v][:, j, :], out_offset=None, in_=source,
                                         in_offset=rows_at(gi[v], j)).then_inc(x_in[v], 16)

    def adds(g, v, staged_now, ahead):
        wait(pool, landed, 16 * G * g)
        pool.nop(nofuse=True)
        nc.gpsimd.tensor_copy(si[v][:, :], M.sidx[key][:, cols(g)]).then_inc(staged, 1)
        pool.wait_ge(staged, staged_now)
        pool.nop(nofuse=True)
        pool.wait_ge(part_ready, g + 1)
        pool.nop(nofuse=True)
        for j in range(G):
            if j:
                pool.wait_ge(landed, 16 * (G * g + j))
                pool.nop(nofuse=True)
            nc.gpsimd.indirect_dma_start(out=sums, out_offset=rows_at(si[v], j), in_=part[v][:, j, :],
                                         in_offset=None, compute_op=ALU.add).then_inc(landed, 16)
            ahead(j * nx // G, (j + 1) * nx // G)

    def body(g, u, h):
        v = 1 - u
        pool.wait_ge(x_used, g)
        pool.nop(nofuse=True)
        stage_x(g + 1, v)
        adds(g - 1, v, len(wanted) * (g + 2) + g, lambda a, b: gather_x(v, range(a, b)))

    stage_x(0, 0)
    stage_x(1, 1)
    pool.wait_ge(staged, 2 * len(wanted))
    gather_x(0, range(nx))
    gather_x(1, range(nx))
    each_group(pool, body)
    adds(NG - 1, 1, len(wanted) * (NG + 1) + NG, lambda a, b: None)
    pool.wait_ge(landed, 16 * G * NG)
    pool.wait_ge(x_in[0], 16 * nx * (NG // 2 + 1))
    pool.wait_ge(x_in[1], 16 * nx * (NG // 2))


def layer2_edges(nc, t, M):
    with ExitStack() as ctx:
        sb = lambda name, shape, dt=fp32: ctx.enter_context(nc.sbuf_tensor("e2_" + name, shape, dt))
        ps = lambda name, shape: ctx.enter_context(nc.psum_tensor("e2_" + name, shape, fp32))
        taken = []
        sem = M.sems.phase("e2_", taken)
        W = F + 1
        X = [sb(f"X{u}", [P, 2 * G, W]) for u in range(2)]
        gi = [sb(f"gi{u}", [P, 2 * G], i32) for u in range(2)]
        si = [sb(f"si{u}", [P, G], i32) for u in range(2)]
        keys = sb("keys", [P, 2, G, P])
        types = sb("types", [P, 2, G, P])
        nb = norm_buffers(sb, 2 * G)
        h = nb["h"]
        hT = sb("hT", [P, 2, P])
        same = sb("same", [P, G, P])
        onehot = sb("onehot", [P, G, P])
        is_last = sb("is_last", [P, G])
        CR = sb("CR", [P, G, NB + F])
        xhat = sb("xhat", [P, G, F])
        yhat = sb("yhat", [P, G, F])
        yrel = sb("yrel", [P, G, F])
        pair = sb("pair", [P, G, F])
        dot = sb("dot", [P, G])
        dot0 = sb("dot0", [P, G])
        gate = sb("gate", [P, G])
        prod = [sb(f"prod{b}", [P, NB, F]) for b in range(2)]
        msg = sb("msg", [P, G, F])
        gated = sb("gated", [P, G, F])
        loop = sb("loop", [P, G, F])
        V = sb("V", [P, G, W])
        part = [sb(f"part{u}", [P, G, W]) for u in range(2)]
        psT = ps("psT", [P, 2, P])
        psB = [ps(f"psB{b}", [P, NB, F]) for b in range(2)]
        psQ = ps("psQ", [P, 3, G, F])
        psC = ps("psC", [P, G, NB + F])
        psV = ps("psV", [P, G, W])

        staged, landed, part_ready = sem("staged"), sem("landed"), sem("part_ready")
        x_in = [sem(f"x_in{u}") for u in range(2)]
        keys_in = [sem(f"keys_in{u}") for u in range(2)]
        types_in = [sem(f"types_in{u}") for u in range(2)]
        spread_free = sem("spread_free")
        norm_sems = [sem(n) for n in NORM_SEMS]
        h_ready, hT_psum, hT_ready = sem("h_ready"), sem("hT_psum"), sem("hT_ready")
        onehot_ready, CR_psum, CR_ready = sem("onehot_ready"), sem("CR_psum"), sem("CR_ready")
        hats_ready, bases_ready, bases_used = sem("hats_ready"), sem("bases_ready"), sem("bases_used")
        dot_ready, gate_ready, V_ready, sums_ready = sem("dot_ready"), sem("gate_ready"), sem("V_ready"), sem("sums_ready")
        s_dve = sem("dve_steps")
        block = ctx.enter_context(nc.Block())

        @block.sync
        def _(sp):
            M.sems.clear(sp)
            with sp.Fori(0, NG // 2) as i:
                for u in range(2):
                    sp.wait_ge(spread_free, 2 * i + u + 1)
                    sp.nop(nofuse=True)
                    for name, buf, landed_ in (("dst", keys, keys_in), ("type", types, types_in)):
                        sp.dma_start(buf[:, u, :, :], M.keyT[name][cols(2 * i + u), :].unsqueeze(0)
                                     .to_broadcast([P, G, P])).then_inc(landed_[u], 16)

        @block.gpsimd
        def _(pool):
            gather_and_add(nc, pool, M, ("src", "dst"), "dst", M.x2, M.rel_sums, X, gi, si, part,
                           (staged, x_in, norm_sems[0], part_ready, landed))

        @block.scalar
        def _(act):
            def edges(g, u, i):
                norm_scalar(nc, act, M, nb, norm_sems, h_ready, g)
                act.wait_ge(hT_psum, g + 1)
                nc.scalar.activation(hT[:, :, :], psT[:, :, :], ACT.Copy).then_inc(hT_ready, 1)
                act.wait_ge(CR_psum, g + 1)
                nc.scalar.activation(CR[:, :, :], psC[:, :, :], ACT.Copy).then_inc(CR_ready, 1)
                act.wait_ge(dot_ready, g + 1)
                nc.scalar.activation(gate[:, :], dot0[:, :], ACT.Tanh, scale=float(F) ** -0.5).then_inc(gate_ready, 1)
                act.wait_ge(sums_ready, g + 1)
                wait(act, landed, 16 * G * (g - 1))
                nc.scalar.activation(part[u][:, :, :], psV[:, :, :], ACT.Copy).then_inc(part_ready, 1)

            edges(0, 0, 0)
            each_group(act, edges)

        @block.tensor
        def _(pe):
            def edges(g):
                pe.wait_ge(onehot_ready, g + 1)
                for j in range(G):
                    last = nc.tensor.matmul(psC[:, j, :], onehot[:, j, :], M.WCR[:, :], start=True, stop=True)
                last.then_inc(CR_psum, 1)
                pe.wait_ge(h_ready, g + 1)
                for n in range(2):
                    last = nc.tensor.transpose(psT[:, n, :], h[:, G * n:G * n + G, :].rearrange("p a f -> p (a f)"),
                                               M.ident[:, :])
                last.then_inc(hT_psum, 1)
                pe.wait_ge(hT_ready, g + 1)
                for n, (side, w) in enumerate(((0, M.A1B), (1, M.A2B), (0, M.SLB))):
                    last = nc.tensor.matmul(psQ[:, n, :, :].rearrange("p a f -> p (a f)"), hT[:, side, :], w[:, :],
                                            start=True, stop=True)
                last.then_inc(hats_ready, 1)
                for j in range(G):
                    wait(pe, bases_used, G * g + j - 1)
                    nc.tensor.matmul(psB[j % 2][:, :, :].rearrange("p b f -> p (b f)"), hT[:, 0, :],
                                     M.WB2[:, j, :, :].rearrange("p b f -> p (b f)"),
                                     start=True, stop=True).then_inc(bases_ready, 1)
                pe.wait_ge(V_ready, g + 1)
                for j in range(G):
                    last = nc.tensor.matmul(psV[:, j, :], same[:, j, :], V[:, j, :], start=True, stop=True)
                last.then_inc(sums_ready, 1)

            edges(0)
            each_group(pe, lambda g, u, i: edges(g))

        @block.vector
        def _(dve):
            s = Steps(dve, s_dve)

            def edges(g, u, i):
                s.start(g)
                dve.wait_ge(x_in[u], 16 * 2 * G * (i + 1))
                s.done(nc.vector.tensor_tensor(is_last[:, :], X[u][:, G:2 * G, F], M.eid1[:, cols(g)], ALU.is_equal))
                norm_vector(nc, dve, s, X[u][:, :, 0:F], 2 * G, nb, norm_sems, g)
                dve.wait_ge(types_in[u], 16 * (i + 1))
                nc.vector.tensor_scalar(onehot[:, :, :], types[:, u, :, :], M.pid[:, 0:1], None,
                                        ALU.is_equal).then_inc(onehot_ready, 1)
                dve.wait_ge(keys_in[u], 16 * (i + 1))
                nc.vector.tensor_tensor(same[:, :, :], keys[:, u, :, :], rep(M.key["dst"][:, cols(g)], P),
                                        ALU.is_equal).then_inc(spread_free, 1)
                dve.wait_ge(hats_ready, g + 1)
                s.done(nc.vector.tensor_tensor(xhat[:, :, :], psQ[:, 0, :, :], along(M.a1row[:, :], G), ALU.add))
                s.done(nc.vector.tensor_tensor(yhat[:, :, :], psQ[:, 1, :, :], along(M.a2row[:, :], G), ALU.add))
                s.done(nc.vector.tensor_tensor(loop[:, :, :], psQ[:, 2, :, :], rep(is_last[:, :], F), ALU.mult))
                s.sync()
                dve.wait_ge(CR_ready, g + 1)
                s.done(nc.vector.tensor_tensor(yrel[:, :, :], yhat[:, :, :], CR[:, :, NB:NB + F], ALU.add))
                s.sync()
                s.done(nc.vector.tensor_tensor(pair[:, :, :], xhat[:, :, :], yrel[:, :, :], ALU.mult))
                s.sync()
                s.done(nc.vector.reduce_sum(dot[:, :], pair[:, :, :], AX.X))
                s.sync()
                nc.vector.tensor_scalar(dot0[:, :], dot[:, :], 0.0, None, ALU.max).then_inc(dot_ready, 1)
                for j in range(G):
                    dve.wait_ge(bases_ready, G * g + j + 1)
                    nc.vector.tensor_tensor(prod[j % 2][:, :, :], psB[j % 2][:, :, :], rep(CR[:, j, 0:NB], F),
                                            ALU.mult).then_inc(bases_used, 1)
                    s.sync()
                    dve.wait_ge(bases_used, G * g + j + 1)
                    s.done(nc.vector.reduce_sum(msg[:, j, :], prod[j % 2][:, :, :].rearrange("p b f -> p f b"), AX.X))
                s.sync()
                dve.wait_ge(gate_ready, g + 1)
                s.done(nc.vector.tensor_tensor(gated[:, :, :], msg[:, :, :], rep(gate[:, :], F), ALU.mult))
                s.sync()
                nc.vector.tensor_tensor(V[:, :, 0:F], gated[:, :, :], loop[:, :, :], ALU.add).then_inc(V_ready, 1)
                dve.wait_ge(sums_ready, g + 1)
                s.end()

            nc.vector.memset(V[:, :, :], 1.0).then_inc(spread_free, 2)
            dve.wait_ge(spread_free, 2)
            s.per = PER_E2
            edges(0, 0, 0)
            each_group(dve, edges)


def dense2(nc, t, M, early):
    with ExitStack() as ctx:
        sb = lambda name, shape, dt=fp32: ctx.enter_context(nc.sbuf_tensor("d2_" + name, shape, dt))
        ps = lambda name, shape: ctx.enter_context(nc.psum_tensor("d2_" + name, shape, fp32))
        taken = []
        sem = M.sems.phase("d2_", taken)
        W = F + 1
        X = [sb(f"X{u}", [P, K, W]) for u in range(2)]
        S = [sb(f"S{u}", [P, K, W]) for u in range(2)]
        Y = [sb(f"Y{u}", [P, K, F]) for u in range(2)]
        Z = [sb(f"Z{u}", [P, K, W]) for u in range(2)]
        nb = norm_buffers(sb, K)
        h = nb["h"]
        hT = [sb(f"hT{q}", [P, G, P]) for q in range(2)]
        droot = sb("droot", [P, K])
        psT = [ps(f"psT{q}", [P, G, P]) for q in range(2)]
        psR = [ps(f"psR{q}", [P, G * P]) for q in range(3)]
        loaded = [sem(f"loaded{u}") for u in range(2)]
        stored, norm_sems = sem("stored"), [sem(n) for n in NORM_SEMS]
        h_ready, hT_psum, hT_ready, round_ready = sem("h_ready"), sem("hT_psum"), sem("hT_ready"), sem("round_ready")
        degree_root, x3_ready, done, s_dve = sem("degree_root"), sem("x3_ready"), sem("done"), sem("dve_steps")
        proj_sems = h_ready, hT_psum, hT_ready, round_ready, done
        block = ctx.enter_context(nc.Block())
        stores = 1 if early else 2

        @block.sync
        def _(sp):
            M.sems.clear(sp)
            def load(c, u):
                sp.dma_start(X[u][:, :, :], chunk(M.x2, c)).then_inc(loaded[u], 16)
                sp.dma_start(S[u][:, :, :], chunk(M.rel_sums, c)).then_inc(loaded[u], 16)

            def body(c, u, i):
                sp.wait_ge(done, c + 1)
                sp.nop(nofuse=True)
                wait(sp, stored, 16 * stores * c)
                sp.nop(nofuse=True)
                if early:
                    sp.dma_start(chunk(early, c), Y[u][:, :, :]).then_inc(stored, 16)
                else:
                    sp.dma_start(chunk(M.x3, c), Y[u][:, :, :]).then_inc(stored, 16)
                    sp.dma_start(chunk(M.hs, c), Z[u][:, :, :]).then_inc(stored, 16)
                if not isinstance(c, int) or c + 2 < NCH:
                    load(c + 2, u)

            load(0, 0)
            load(1, 1)
            each_chunk(sp, body)
            sp.wait_ge(stored, 16 * stores * NCH)

        @block.scalar
        def _(act):
            def body(c, u, i):
                act.wait_ge(loaded[u], 32 * (i + 1))
                wait(act, done, c)
                nc.scalar.activation(droot[:, :], S[u][:, :, F], ACT.Sqrt, bias=M.ones[:, 0:1]).then_inc(degree_root, 1)
                norm_scalar(nc, act, M, nb, norm_sems, h_ready, c)
                project_scalar(nc, act, psT, hT, proj_sems, c, u)

            each_chunk(act, body)

        @block.tensor
        def _(pe):
            each_chunk(pe, lambda c, u, i: project_pe(nc, pe, M, M.W3B, h, psT, hT, psR, proj_sems, c, u))

        @block.vector
        def _(dve):
            s = Steps(dve, s_dve, PER_D2)

            def body(c, u, i):
                s.start(c)
                dve.wait_ge(loaded[u], 32 * (i + 1))
                wait(dve, stored, 16 * stores * (c - 1))
                s.done(nc.vector.scalar_tensor_tensor(Y[u][:, :, :], S[u][:, :, 0:F], 0.0, X[u][:, :, 0:F], ALU.max, ALU.add))
                s.sync()
                norm_vector(nc, dve, s, Y[u][:, :, :], K, nb, norm_sems, c)
                dve.wait_ge(degree_root, c + 1)
                s.done(nc.vector.reciprocal(Z[u][:, :, F], droot[:, :]))
                s.sync()
                dve.wait_ge(round_ready, 3 * c + 3)
                n = G * G
                for q in range(3):
                    last = nc.vector.tensor_tensor(Z[u][:, n * q:n * q + n, 0:F],
                                                   psR[q][:, :].rearrange("p (k f) -> p k f", f=F),
                                                   rep(Z[u][:, n * q:n * q + n, F], F), ALU.mult)
                last.then_inc(done, 1)
                s.end()

            each_chunk(dve, body)
    M.sems.retire(taken)


def conv_edges(nc, t, M):
    with ExitStack() as ctx:
        sb = lambda name, shape, dt=fp32: ctx.enter_context(nc.sbuf_tensor("e3_" + name, shape, dt))
        taken = []
        sem = M.sems.phase("e3_", taken)
        X = [sb(f"X{u}", [P, G, F + 1]) for u in range(2)]
        gi = [sb(f"gi{u}", [P, G], i32) for u in range(2)]
        si = [sb(f"si{u}", [P, G], i32) for u in range(2)]
        keys = sb("keys", [P, 2, G, P])
        same = [sb(f"same{u}", [P, G, P]) for u in range(2)]
        part = [sb(f"part{u}", [P, G, F]) for u in range(2)]
        psV = [ctx.enter_context(nc.psum_tensor(f"e3_psV{u}", [P, G, F], fp32)) for u in range(2)]
        staged, landed, part_ready = sem("staged"), sem("landed"), sem("part_ready")
        x_in = [sem(f"x_in{u}") for u in range(2)]
        keys_in = [sem(f"keys_in{u}") for u in range(2)]
        same_ready, sums_ready, keys_free = sem("same_ready"), sem("sums_ready"), sem("keys_free")
        block = ctx.enter_context(nc.Block())

        @block.sync
        def _(sp):
            M.sems.clear(sp)
            spread_keys(sp, M, "dst", keys, keys_free, keys_in)

        @block.gpsimd
        def _(pool):
            gather_and_add(nc, pool, M, ("src",), "dst", M.hs, M.conv_sums, X, gi, si, part,
                           (staged, x_in, sums_ready, part_ready, landed))

        @block.scalar
        def _(act):
            def edges(g, u, i):
                act.wait_ge(sums_ready, g + 1)
                wait(act, landed, 16 * G * (g - 1))
                nc.scalar.activation(part[u][:, :, :], psV[u][:, :, :], ACT.Copy).then_inc(part_ready, 1)

            edges(0, 0, 0)
            each_group(act, edges)

        @block.tensor
        def _(pe):
            def edges(g, u, i):
                pe.wait_ge(x_in[u], 16 * G * (i + 1))
                pe.wait_ge(same_ready, g + 1)
                wait(pe, part_ready, g - 1)
                for j in range(G):
                    last = nc.tensor.matmul(psV[u][:, j, :], same[u][:, j, :], X[u][:, j, 0:F], start=True, stop=True)
                last.then_inc(sums_ready, 1)

            edges(0, 0, 0)
            each_group(pe, edges)

        @block.vector
        def _(dve):
            def edges(g, u, i):
                dve.wait_ge(keys_in[u], 16 * (i + 1))
                wait(dve, sums_ready, g - 1)
                nc.vector.tensor_tensor(same[u][:, :, :], keys[:, u, :, :], rep(M.key["dst"][:, cols(g)], P),
                                        ALU.is_equal).then_inc(same_ready, 1)
                dve.wait_ge(same_ready, g + 1)
                nc.vector.sem_inc(keys_free, 1)

            nc.vector.sem_inc(keys_free, 2)
            edges(0, 0, 0)
            each_group(dve, edges)


def dense3(nc, t, M):
    with ExitStack() as ctx:
        sb = lambda name, shape, dt=fp32: ctx.enter_context(nc.sbuf_tensor("d3_" + name, shape, dt))
        taken = []
        sem = M.sems.phase("d3_", taken)
        Z = [sb(f"Z{u}", [P, K, F + 1]) for u in range(2)]
        S = [sb(f"S{u}", [P, K, F]) for u in range(2)]
        Y = [sb(f"Y{u}", [P, K, F]) for u in range(2)]
        both = sb("both", [P, K, F])
        scaled = sb("scaled", [P, K, F])
        biased = sb("biased", [P, K, F])
        loaded = [sem(f"loaded{u}") for u in range(2)]
        stored, biased_ready, done, s_dve = sem("stored"), sem("biased_ready"), sem("done"), sem("dve_steps")
        block = ctx.enter_context(nc.Block())

        @block.sync
        def _(sp):
            M.sems.clear(sp)
            def load(c, u):
                sp.dma_start(Z[u][:, :, :], chunk(M.hs, c)).then_inc(loaded[u], 16)
                sp.dma_start(S[u][:, :, :], chunk(M.conv_sums, c)).then_inc(loaded[u], 16)

            def body(c, u, i):
                sp.wait_ge(done, c + 1)
                sp.nop(nofuse=True)
                wait(sp, stored, 16 * c)
                sp.nop(nofuse=True)
                sp.dma_start(chunk(M.conv, c), Y[u][:, :, :]).then_inc(stored, 16)
                if not isinstance(c, int) or c + 2 < NCH:
                    load(c + 2, u)

            load(0, 0)
            load(1, 1)
            each_chunk(sp, body)
            sp.wait_ge(stored, 16 * NCH)

        @block.scalar
        def _(act):
            def body(c, u, i):
                act.wait_ge(biased_ready, c + 1)
                wait(act, stored, 16 * (c - 1))
                nc.scalar.activation(Y[u][:, :, :], biased[:, :, :], ACT.Relu).then_inc(done, 1)

            each_chunk(act, body)

        @block.vector
        def _(dve):
            s = Steps(dve, s_dve, PER_D3)

            def body(c, u, i):
                s.start(c)
                dve.wait_ge(loaded[u], 32 * (i + 1))
                s.done(nc.vector.tensor_tensor(both[:, :, :], Z[u][:, :, 0:F], S[u][:, :, :], ALU.add))
                s.sync()
                s.done(nc.vector.tensor_tensor(scaled[:, :, :], both[:, :, :], rep(Z[u][:, :, F], F), ALU.mult))
                s.sync()
                wait(dve, done, c)
                nc.vector.tensor_tensor(biased[:, :, :], scaled[:, :, :], along(M.b3row[:, :], K),
                                        ALU.add).then_inc(biased_ready, 1)
                dve.wait_ge(biased_ready, c + 1)
                s.end()

            each_chunk(dve, body)
    M.sems.retire(taken)


def square_edges(nc, t, M):
    with ExitStack() as ctx:
        sb = lambda name, shape, dt=fp32: ctx.enter_context(nc.sbuf_tensor("e4_" + name, shape, dt))
        taken = []
        sem = M.sems.phase("e4_", taken)
        W = F + 1
        X = [sb(f"X{u}", [P, 2 * G, F]) for u in range(2)]
        gi = [sb(f"gi{u}", [P, 2 * G], i32) for u in range(2)]
        si = [sb(f"si{u}", [P, G], i32) for u in range(2)]
        keys = sb("keys", [P, 2, G, P])
        same = [sb(f"same{u}", [P, G, P]) for u in range(2)]
        diff = [sb(f"diff{u}", [P, G, F]) for u in range(2)]
        V = [sb(f"V{u}", [P, G, W]) for u in range(2)]
        part = [sb(f"part{u}", [P, G, W]) for u in range(2)]
        psV = [ctx.enter_context(nc.psum_tensor(f"e4_psV{u}", [P, G, W], fp32)) for u in range(2)]
        staged, landed, part_ready = sem("staged"), sem("landed"), sem("part_ready")
        x_in = [sem(f"x_in{u}") for u in range(2)]
        keys_in = [sem(f"keys_in{u}") for u in range(2)]
        diff_ready, V_ready, sums_ready, keys_free = sem("diff_ready"), sem("V_ready"), sem("sums_ready"), sem("keys_free")
        ones_ready = sem("ones_ready")
        block = ctx.enter_context(nc.Block())

        @block.sync
        def _(sp):
            M.sems.clear(sp)
            spread_keys(sp, M, "src", keys, keys_free, keys_in)

        @block.gpsimd
        def _(pool):
            gather_and_add(nc, pool, M, ("src", "dst"), "src", M.conv, M.square_sums, X, gi, si, part,
                           (staged, x_in, diff_ready, part_ready, landed))

        @block.scalar
        def _(act):
            def edges(g, u, i):
                act.wait_ge(diff_ready, g + 1)
                wait(act, sums_ready, g - 1)
                nc.scalar.activation(V[u][:, :, 0:F], diff[u][:, :, :], ACT.Square).then_inc(V_ready, 1)
                act.wait_ge(sums_ready, g + 1)
                wait(act, landed, 16 * G * (g - 1))
                nc.scalar.activation(part[u][:, :, :], psV[u][:, :, :], ACT.Copy).then_inc(part_ready, 1)

            act.wait_ge(ones_ready, 1)
            edges(0, 0, 0)
            each_group(act, edges)

        @block.tensor
        def _(pe):
            def edges(g, u, i):
                pe.wait_ge(V_ready, g + 1)
                pe.wait_ge(keys_free, g + 3)
                wait(pe, part_ready, g - 1)
                for j in range(G):
                    last = nc.tensor.matmul(psV[u][:, j, :], same[u][:, j, :], V[u][:, j, :], start=True, stop=True)
                last.then_inc(sums_ready, 1)

            edges(0, 0, 0)
            each_group(pe, edges)

        @block.vector
        def _(dve):
            def edges(g, u, i):
                dve.wait_ge(x_in[u], 16 * 2 * G * (i + 1))
                wait(dve, V_ready, g - 1)
                nc.vector.tensor_tensor(diff[u][:, :, :], X[u][:, 0:G, :], X[u][:, G:2 * G, :],
                                        ALU.subtract).then_inc(diff_ready, 1)
                dve.wait_ge(keys_in[u], 16 * (i + 1))
                wait(dve, sums_ready, g - 1)
                nc.vector.tensor_tensor(same[u][:, :, :], keys[:, u, :, :], rep(M.key["src"][:, cols(g)], P),
                                        ALU.is_equal).then_inc(keys_free, 1)

            for u in range(2):
                last = nc.vector.memset(V[u][:, :, :], 1.0)
            last.then_inc(ones_ready, 1)
            nc.vector.sem_inc(keys_free, 2)
            edges(0, 0, 0)
            each_group(dve, edges)


def dense4(nc, t, M, out):
    with ExitStack() as ctx:
        sb = lambda name, shape, dt=fp32: ctx.enter_context(nc.sbuf_tensor("d4_" + name, shape, dt))
        taken = []
        sem = M.sems.phase("d4_", taken)
        X = [sb(f"X{u}", [P, K, F]) for u in range(2)]
        S = [sb(f"S{u}", [P, K, F + 1]) for u in range(2)]
        Y = [sb(f"Y{u}", [P, K, F]) for u in range(2)]
        count = sb("count", [P, K])
        share = sb("share", [P, K])
        mean = [sb(f"mean{u}", [P, K, F]) for u in range(2)]
        curve = [sb(f"curve{u}", [P, K, F]) for u in range(2)]
        loaded = [sem(f"loaded{u}") for u in range(2)]
        stored, mean_ready, curve_ready, done, s_dve = sem("stored"), sem("mean_ready"), sem("curve_ready"), sem("done"), sem("dve_steps")
        block = ctx.enter_context(nc.Block())

        @block.sync
        def _(sp):
            M.sems.clear(sp)
            def load(c, u):
                sp.dma_start(X[u][:, :, :], chunk(M.x3, c)).then_inc(loaded[u], 16)
                sp.dma_start(S[u][:, :, :], chunk(M.square_sums, c)).then_inc(loaded[u], 16)

            def body(c, u, i):
                sp.wait_ge(done, c + 1)
                sp.nop(nofuse=True)
                wait(sp, stored, 16 * c)
                sp.nop(nofuse=True)
                sp.dma_start(chunk(out, c), Y[u][:, :, :]).then_inc(stored, 16)
                if not isinstance(c, int) or c + 2 < NCH:
                    load(c + 2, u)

            load(0, 0)
            load(1, 1)
            each_chunk(sp, body)
            sp.wait_ge(stored, 16 * NCH)

        @block.gpsimd
        def _(pool):
            def body(c, u, i):
                pool.wait_ge(curve_ready, c + 1)
                wait(pool, stored, 16 * (c - 1))
                nc.gpsimd.tensor_tensor(Y[u][:, :, :], X[u][:, :, :], curve[u][:, :, :], ALU.add).then_inc(done, 1)

            each_chunk(pool, body)

        @block.scalar
        def _(act):
            def body(c, u, i):
                act.wait_ge(mean_ready, c + 1)
                wait(act, done, c - 1)
                nc.scalar.activation(curve[u][:, :, :], mean[u][:, :, :], ACT.Tanh).then_inc(curve_ready, 1)

            each_chunk(act, body)

        @block.vector
        def _(dve):
            s = Steps(dve, s_dve, PER_D4)

            def body(c, u, i):
                s.start(c)
                dve.wait_ge(loaded[u], 32 * (i + 1))
                wait(dve, mean_ready, c)
                s.done(nc.vector.tensor_scalar(count[:, :], S[u][:, :, F], 1.0, None, ALU.max))
                s.sync()
                s.done(nc.vector.reciprocal(share[:, :], count[:, :]))
                s.sync()
                wait(dve, curve_ready, c - 1)
                nc.vector.tensor_tensor(mean[u][:, :, :], S[u][:, :, 0:F], rep(share[:, :], F),
                                        ALU.mult).then_inc(mean_ready, 1)
                s.end()

            each_chunk(dve, body)
    M.sems.retire(taken)


def gnn_program(nc, t, out, stage=9):
    with ExitStack() as ctx:
        ctx.enter_context(nc.allow_non_contiguous_dma(reason="small tables, once"))
        M = Memory(nc, ctx)
        setup(nc, t, M)
        layer0_edges(nc, t, M)
        dense0(nc, t, M, out if stage == 1 else M.x1)
        if stage == 1:
            return
        layer1_edges(nc, t, M)
        more_maxima(nc, M)
        dense1(nc, t, M, stage == 2 and out)
        if stage == 2:
            return
        layer2_edges(nc, t, M)
        dense2(nc, t, M, stage == 3 and out)
        if stage == 3:
            return
        conv_edges(nc, t, M)
        dense3(nc, t, M)
        square_edges(nc, t, M)
        dense4(nc, t, M, out)


_INS = ['x', 'src', 'dst', 'edge_attr_2', 'edge_attr_32', 'edge_type_86', 'L0_gnn_weight', 'L0_gnn_root_weight',
        'L0_gnn_att_weight', 'L0_gnn_bias', 'L1_gnn_W1', 'L1_gnn_b1', 'L1_gnn_W2', 'L1_gnn_b2', 'L2_gnn_weight',
        'L2_gnn_w_comp', 'L2_gnn_self_loop_weight', 'L2_gnn_A1_w', 'L2_gnn_A1_b', 'L2_gnn_A2_w', 'L2_gnn_A2_b',
        'L2_gnn_rel_emb', 'L3_gnn_W', 'L3_gnn_b']


def kernel(**inputs):
    import numpy as _np
    import concourse.bacc as _bacc
    from concourse import mybir as _mybir
    from concourse.bass_utils import run_bass_kernel_spmd as _run

    nc = _bacc.Bacc("TRN2", target_bir_lowering=False, num_devices=1)
    arrays, tensors = {}, {}
    for name in _INS:
        a = _np.ascontiguousarray(inputs[name])
        arrays[f"in_{name}_dram"] = a
        tensors[name] = nc.dram_tensor(f"in_{name}_dram", a.shape, _mybir.dt.from_np(a.dtype),
                                       kind="ExternalInput").ap()
    out = nc.dram_tensor("out_0_dram", (N, F), fp32, kind="ExternalOutput").ap()
    gnn_program(nc, tensors, out)
    r = _run(nc, [arrays], core_ids=[0])
    return r.results[0]["out_0_dram"]
```

```python
import concourse.bass as bass
from concourse import mybir
from contextlib import ExitStack

fp32 = mybir.dt.float32
i32 = mybir.dt.int32
ALU = mybir.AluOpType
ACT = mybir.ActivationFunctionType
AX = mybir.AxisListType

P = 128
N = 100000
F = 32
E = 25000
ROWS_E = 125
T = E // ROWS_E
G = 4
NG = T // G
PAD_KEY = 200000
NT = 100352
EPS = 1e-5
BIG = 1e30
SLOPE = 0.2
KS = 5
TAPS = KS * KS
TC = 15
HID = 64
NB = 16
REL = 86
K = 48
NCH = 17
STRIDE = (N - P * K) // (NCH - 1)
LN_EPS = EPS * F * F * F
LN_GAIN = float(F) ** 0.5


LAG0 = 2
PER_E0 = 26
PER_D0 = 11
PER_E1 = 4
PER_R1 = 5
PER_D1 = 3
PER_E2 = 14
PER_D2 = 4
PER_D3 = 2
PER_E4 = 3
PER_D4 = 2


class Steps:

    def __init__(self, eng, sem, per=0):
        self.eng, self.sem, self.per = eng, sem, per
        self.base, self.n = 0, 0

    def done(self, ins):
        ins.then_inc(self.sem, 1)
        self.n += 1

    def sync(self):
        self.eng.wait_ge(self.sem, self.base + self.n)

    def enter(self, first, turn):
        self.base, self.n = first + turn * self.per, 0

    def leave(self):
        assert self.n == self.per, self.n

    def resume(self, n):
        self.base, self.n = 0, n


def wait(eng, sem, value):
    if not (isinstance(value, int) and value <= 0):
        eng.wait_ge(sem, value)


def rep(ap, n):
    return ap.unsqueeze(2).to_broadcast([ap.shape[0], ap.shape[1], n])


def along(ap, n):
    return ap.unsqueeze(1).to_broadcast([ap.shape[0], n, ap.shape[1]])


def cols(g):
    return slice(G * g, G * g + G) if isinstance(g, int) else bass.ds(G * g, G)


def each_group(eng, body, steps=None, lead=2, extra=0):
    for g in range(lead):
        body(g, g % 2, g // 2)
    first, turns = steps.n if steps else 0, NG - 2 - lead
    with eng.Fori(0, turns // 2) as i:
        for u in range(2):
            if steps:
                steps.enter(first, 2 * i + u)
            body(2 * i + lead + u, u, i + lead // 2)
            if steps:
                steps.leave()
    if steps:
        steps.resume(first + turns * steps.per)
    for g in range(NG - 2, NG + extra):
        body(g, g % 2, g // 2)


def live(g):
    return not isinstance(g, int) or 0 <= g < NG


def each_chunk(eng, body, steps=None):
    lead = 2
    for c in range(lead):
        body(c, c % 2, c // 2)
    first, turns = steps.n if steps else 0, NCH - 3 - lead
    with eng.Fori(0, turns // 2) as i:
        for u in range(2):
            if steps:
                steps.enter(first, 2 * i + u)
            body(2 * i + lead + u, u, i + lead // 2)
            if steps:
                steps.leave()
    if steps:
        steps.resume(first + turns * steps.per)
    for c in range(NCH - 3, NCH):
        body(c, c % 2, c // 2)


def chunk(table, c):
    lo = c * STRIDE
    rows = table[lo:lo + P * K, :] if isinstance(c, int) else table[bass.ds(lo, P * K), :]
    return rows.rearrange("(p k) f -> p k f", p=P)


class Semaphores:

    def __init__(self, nc, ctx):
        self.nc, self.ctx = nc, ctx
        self.free, self.resting, self.retired = [], [], []

    def phase(self, prefix, taken):
        self.free, self.resting = self.free + self.resting, []

        def sem(name):
            taken.append(self.free.pop() if self.free else self.ctx.enter_context(self.nc.semaphore(prefix + name)))
            return taken[-1]
        return sem

    def retire(self, taken):
        self.retired += taken

    def clear(self, sp):
        for s in self.retired:
            sp.sem_clear(s)
        self.resting, self.retired = self.resting + self.retired, []


class Memory:

    def __init__(self, nc, ctx):
        def sb(name, shape, dt=fp32):
            return ctx.enter_context(nc.sbuf_tensor(name, shape, dt))

        def table(name, shape, dt=fp32):
            return nc.dram_tensor(name, shape, dt).ap()

        self.sems = Semaphores(nc, ctx)
        self.keyT = {k: table("keyT_" + k, [T, P]) for k in ("src", "dst", "type")}
        self.softmax_state = [table(f"softmax_state{k}", [NT, F + 2]) for k in range(2)]
        self.max_state = [table(f"max_state{k}", [NT, F + 1]) for k in range(2)]
        self.rel_sums = table("rel_sums", [NT, F + 1])
        self.conv_sums = table("conv_sums", [NT, F])
        self.square_sums = table("square_sums", [NT, F + 1])
        self.x1 = table("x1", [N, F])
        self.x2 = table("x2", [N, F + 1])
        self.x3 = table("x3", [N, F])
        self.hs = table("hs", [N, F + 1])
        self.conv = table("conv", [N, F])

        self.ident = sb("ident", [P, P])
        self.lower = sb("lower", [P, P])
        self.ones = sb("ones", [P, P])
        self.zeros = sb("zeros", [P, 28 * (F + 2)])
        self.pid = sb("pid", [P, 1])
        self.waste = sb("waste", [P, 1])
        self.ln_eps = sb("ln_eps", [P, 1])
        self.eid1 = sb("eid1", [P, T])
        self.gidx = {k: sb("gidx_" + k, [P, T], i32) for k in ("src", "dst")}
        self.key = {k: sb("key_" + k, [P, T]) for k in ("src", "dst", "type")}
        self.rank = {k: sb("rank_" + k, [P, T]) for k in ("src", "dst")}
        self.sidx = {k: sb("sidx_" + k, [P, T], i32) for k in ("src", "dst")}
        self.rounds = sb("rounds", [1, 1], i32)
        kept = sb("kept", [P, T * (F + 1)])
        self.C = kept[:, 0:T * TAPS].rearrange("p (t k) -> p t k", k=TAPS)
        self.V1 = kept[:, :].rearrange("p (t f) -> p t f", f=F + 1)
        self.WB = sb("WB", [P, G, TAPS, F + 1])
        self.RA = sb("RA", [P, G])
        self.ROOT = sb("ROOT", [P, P])
        self.bias0 = sb("bias0", [P, F])
        self.W1S = sb("W1S", [P, 2, P])
        self.W1D = sb("W1D", [P, 2, P])
        self.W1E = sb("W1E", [P, 2, P])
        self.b1col = sb("b1col", [P, 1])
        self.W2B = sb("W2B", [P, 2 * F])
        self.b2row = sb("b2row", [P, F])
        self.WB2 = sb("WB2", [P, G, NB, F])
        self.A1B = sb("A1B", [P, P])
        self.A2B = sb("A2B", [P, P])
        self.SLB = sb("SLB", [P, P])
        self.WCR = sb("WCR", [P, NB + F])
        self.a1row = sb("a1row", [P, F])
        self.a2row = sb("a2row", [P, F])
        self.W3B = sb("W3B", [P, P])
        self.b3row = sb("b3row", [P, F])
        self.wstage = sb("wstage", [P, TAPS, F])


def setup(nc, t, M):
    with ExitStack() as ctx:
        sb = lambda name, shape, dt=fp32: ctx.enter_context(nc.sbuf_tensor(name, shape, dt))
        taken = []
        sem = M.sems.phase("set_", taken)
        keyI = {k: sb("keyI_" + k, [P, T], i32) for k in ("src", "dst", "type")}
        kT = sb("kT", [T // 2, 3, 2, P])
        kB = sb("kB", [P, 2, G, P])
        attr = sb("attr", [P, T, 2])
        dist = sb("dist", [P, T, 2])
        hat = sb("hat", [P, T, 2, KS])
        fall = sb("fall", [P, T, 2, KS])
        rise = sb("rise", [P, T, 2, KS])
        rootw = sb("rootw", [P, F])
        att = sb("att", [P, 2, F])
        watt = sb("watt", [P, TAPS, F])
        wattk = sb("wattk", [P, TAPS])
        rattf = sb("rattf", [P, F])
        ratt = sb("ratt", [P, 1])
        a12 = sb("a12", [F, 2, G, F])
        same = sb("same", [P, G, P])
        again = sb("again", [P, T])
        pad = sb("pad", [P, T])
        gap = sb("gap", [P, T])
        rmax = sb("rmax", [P, 1])
        rmax1 = sb("rmax1", [1, 1])
        psK = [ctx.enter_context(nc.psum_tensor(f"psK{h}", [P, 3, P], fp32)) for h in range(2)]
        psR = ctx.enter_context(nc.psum_tensor("psR", [P, P], fp32))
        psW = ctx.enter_context(nc.psum_tensor("psW", [P, 2, F], fp32))
        s_zero = sem("zeroed")
        s_fill = sem("filled")
        s_sel = sem("masks")
        s_idx = sem("indices")
        s_attr = sem("attr")
        s_w = sem("weights")
        s_wz = sem("weights_cleared")
        s_kf = sem("keys_float")
        s_kp = sem("keys_transposed")
        s_kc = sem("keys_copied")
        s_kt = sem("keys_stored")
        s_kb = [sem(f"set_keys_spread{u}") for u in range(2)]
        s_kbu = sem("keys_free")
        s_mr = sem("rank_max")
        s_mp = sem("rank_row")
        s_dve = sem("dve_steps")
        block = ctx.enter_context(nc.Block())
        half = T // 2
        n_weights = [0]

        @block.sync
        def _(sp):
            sp.wait_ge(s_fill, 1)
            view = lambda a: a.rearrange("(p t) -> p t", p=ROWS_E)
            for k in ("src", "dst"):
                sp.dma_start(M.gidx[k][0:ROWS_E, 0:T], view(t[k])).then_inc(s_idx, 16)
                sp.dma_start(keyI[k][0:ROWS_E, :], view(t[k])).then_inc(s_idx, 16)
            sp.dma_start(keyI["type"][0:ROWS_E, :], view(t["edge_type_86"])).then_inc(s_idx, 16)
            sp.dma_start(attr[0:ROWS_E, :, :],
                         t["edge_attr_2"].rearrange("(p t) d -> p t d", p=ROWS_E)).then_inc(s_attr, 16)

            sp.wait_ge(s_kc, 2)
            for n, k in enumerate(("src", "dst", "type")):
                sp.dma_start(M.keyT[k].rearrange("(h a) p -> a h p", h=2), kT[:, n, :, :]).then_inc(s_kt, 16)
            sp.wait_ge(s_kt, 48)
            for n, k in enumerate(("src", "dst")):
                with sp.Fori(0, NG // 2) as i:
                    for u in range(2):
                        g = 2 * i + u
                        sp.wait_ge(s_kbu, n * NG + g + 1)
                        sp.nop(nofuse=True)
                        sp.dma_start(kB[:, u, :, :], M.keyT[k][cols(g), :].unsqueeze(0)
                                     .to_broadcast([P, G, P])).then_inc(s_kb[u], 16)

        @block.scalar
        def _(act):
            act.wait_ge(s_fill, 1)
            for tab in M.softmax_state:
                w = tab.shape[1]
                act.dma_start(tab.rearrange("(p a r) w -> p a (r w)", p=P, a=28),
                              along(M.zeros[:, 0:28 * w], 28)).then_inc(s_zero, 16)
            act.wait_ge(s_wz, 1)
            w0 = t["L0_gnn_weight"].rearrange("k f o -> f k o")
            w2 = t["L2_gnn_weight"].rearrange("b i o -> i b o")
            root = t["L0_gnn_root_weight"]
            w1 = t["L1_gnn_W1"]
            row = lambda a: a.rearrange("(a f) -> a f", a=1).to_broadcast([P, F])

            def load(dst, src):
                act.dma_start(dst, src).then_inc(s_w, 16)
                n_weights[0] += 1

            for i in range(G):
                b = slice(F * i, F * i + F)
                load(M.wstage[b, :, :], w0)
                load(rootw[b, :], root)
                load(M.ROOT[b, b], root)
                load(M.WB2[b, i, :, :], w2)
                load(M.SLB[b, b], t["L2_gnn_self_loop_weight"])
                load(M.W3B[b, b], t["L3_gnn_W"])
                j, c = i // 2, slice(HID * (i % 2), HID * (i % 2) + HID)
                load(M.W1S[b, j, c], w1[0:F, :])
                load(M.W1D[b, j, c], w1[F:2 * F, :])
                load(M.W1E[b, j, c], w1[2 * F:3 * F, :])
                for n, a in enumerate((t["L2_gnn_A1_w"], t["L2_gnn_A2_w"])):
                    load(a12[:, n, i, :], a)
            for i in range(2):
                b = slice(HID * i, HID * i + HID)
                load(M.b1col[b, :], t["L1_gnn_b1"].rearrange("(f a) -> f a", a=1))
                load(M.W2B[b, F * i:F * i + F], t["L1_gnn_W2"])
                load(att[:, i, :], row(t["L0_gnn_att_weight"][F * i:F * i + F]))
            load(M.bias0[:, :], row(t["L0_gnn_bias"]))
            load(M.b2row[:, :], row(t["L1_gnn_b2"]))
            load(M.a1row[:, :], row(t["L2_gnn_A1_b"]))
            load(M.a2row[:, :], row(t["L2_gnn_A2_b"]))
            load(M.b3row[:, :], row(t["L3_gnn_b"]))
            load(M.WCR[0:REL, 0:NB], t["L2_gnn_w_comp"])
            load(M.WCR[0:REL, NB:NB + F], t["L2_gnn_rel_emb"])
            act.wait_ge(s_w, 16 * n_weights[0])
            act.wait_ge(s_zero, 32)

        @block.gpsimd
        def _(pool):
            nc.gpsimd.memset(M.zeros[:, :], 0.0)
            for k in ("src", "dst"):
                nc.gpsimd.memset(M.gidx[k][:, :], 0)
                nc.gpsimd.memset(keyI[k][:, :], PAD_KEY)
            nc.gpsimd.memset(attr[:, :, :], 0.0)
            nc.gpsimd.memset(keyI["type"][:, :], 0).then_inc(s_fill, 1)
            nc.gpsimd.memset(M.ident[:, :], 0.0).then_inc(s_sel, 1)
            nc.gpsimd.memset(M.lower[:, :], 1.0).then_inc(s_sel, 1)
            nc.gpsimd.memset(M.ones[:, :], 1.0)
            nc.gpsimd.memset(M.ln_eps[:, :], LN_EPS)
            nc.gpsimd.iota(M.pid[:, :], [[0, 1]], base=0, channel_multiplier=1,
                           allow_small_or_imprecise_dtypes=True)
            nc.gpsimd.iota(M.waste[:, :], [[0, 1]], base=N, channel_multiplier=1,
                           allow_small_or_imprecise_dtypes=True)
            nc.gpsimd.iota(M.eid1[:, :], [[1, T]], base=1, channel_multiplier=T,
                           allow_small_or_imprecise_dtypes=True)
            pool.wait_ge(s_sel, 2)
            nc.gpsimd.affine_select(out=M.ident[:, :], in_=M.ident[:, :], compare_op=ALU.not_equal, fill=1.0,
                                    base=0, pattern=[[-1, P]], channel_multiplier=1).then_inc(s_sel, 1)
            nc.gpsimd.affine_select(out=M.lower[:, :], in_=M.lower[:, :], compare_op=ALU.is_gt, fill=0.0,
                                    base=0, pattern=[[-1, P]], channel_multiplier=1).then_inc(s_sel, 1)

        @block.tensor
        def _(pe):
            pe.wait_ge(s_kf, 1)
            pe.wait_ge(s_sel, 4)
            for h in range(2):
                for n, k in enumerate(("src", "dst", "type")):
                    last = nc.tensor.transpose(psK[h][0:half, n, :], M.key[k][:, half * h:half * h + half],
                                               M.ident[:, :])
            last.then_inc(s_kp, 1)
            pe.wait_ge(s_w, 16 * n_weights[0])
            for n in range(2):
                last = nc.tensor.transpose(psW[:, n, :], a12[:, n, :, :].rearrange("a i f -> a (i f)"),
                                           M.ident[0:F, 0:F])
            last.then_inc(s_kp, 1)
            pe.wait_ge(s_mr, 1)
            nc.tensor.transpose(psR[0:1, :], rmax[:, :], M.ident[:, :]).then_inc(s_mp, 1)

        @block.vector
        def _(dve):
            s = Steps(dve, s_dve)
            nc.vector.memset(M.WB[:, :, :, :], 0.0)
            nc.vector.memset(M.WB2[:, :, :, :], 0.0)
            for w in (M.RA, M.ROOT, M.A1B, M.A2B, M.SLB, M.W3B, M.W2B, M.WCR):
                nc.vector.memset(w[:, :], 0.0)
            for w in (M.W1S, M.W1D):
                nc.vector.memset(w[:, :, :], 0.0)
            nc.vector.memset(M.W1E[:, :, :], 0.0).then_inc(s_wz, 1)
            nc.vector.sem_inc(s_kbu, 2)
            dve.wait_ge(s_idx, 80)
            for k in ("src", "dst", "type"):
                last = nc.vector.tensor_copy(M.key[k][:, :], keyI[k][:, :])
            last.then_inc(s_kf, 1)
            dve.wait_ge(s_attr, 16)
            s.done(nc.vector.tensor_scalar(dist[:, :, :], attr[:, :, :], float(KS - 1), 0.0, ALU.mult, ALU.max))
            s.sync()
            s.done(nc.vector.tensor_scalar(dist[:, :, :], dist[:, :, :], float(KS - 1), None, ALU.min))
            s.sync()
            for j in range(KS):
                s.done(nc.vector.tensor_scalar(hat[:, :, :, j], dist[:, :, :], float(-j), None, ALU.add))
            s.sync()
            s.done(nc.vector.tensor_scalar(fall[:, :, :, :], hat[:, :, :, :], -1.0, 1.0, ALU.mult, ALU.add))
            s.done(nc.vector.tensor_scalar(rise[:, :, :, :], hat[:, :, :, :], 1.0, None, ALU.add))
            s.sync()
            s.done(nc.vector.tensor_tensor(hat[:, :, :, :], fall[:, :, :, :], rise[:, :, :, :], ALU.min))
            s.sync()
            s.done(nc.vector.tensor_scalar(hat[:, :, :, :], hat[:, :, :, :], 0.0, None, ALU.max))
            s.sync()
            taps = M.C[:, :, :].rearrange("p t (b a) -> p t b a", b=KS)
            for b in range(KS):
                s.done(nc.vector.tensor_tensor(taps[:, :, b, :], hat[:, :, 0, :], rep(hat[:, :, 1, b], KS), ALU.mult))
            dve.wait_ge(s_kp, 1)
            for h in range(2):
                nc.vector.tensor_copy(kT[:, :, h, :], psK[h][0:half, :, :]).then_inc(s_kc, 1)
            dve.wait_ge(s_w, 16 * n_weights[0])
            s.done(nc.vector.tensor_tensor(watt[:, :, :], M.wstage[:, :, :], along(att[:, 1, :], TAPS), ALU.mult))
            s.done(nc.vector.tensor_tensor(rattf[:, :], rootw[:, :], att[:, 0, :], ALU.mult))
            s.sync()
            s.done(nc.vector.reduce_sum(wattk[:, :], watt[:, :, :], AX.X))
            s.done(nc.vector.reduce_sum(ratt[:, :], rattf[:, :], AX.X))
            s.sync()
            dve.wait_ge(s_kp, 2)
            for i in range(G):
                b = slice(F * i, F * i + F)
                s.done(nc.vector.tensor_copy(M.WB[b, i, :, 0:F], M.wstage[b, :, :]))
                s.done(nc.vector.tensor_copy(M.WB[b, i, :, F], wattk[b, :]))
                s.done(nc.vector.tensor_copy(M.RA[b, i:i + 1], ratt[b, :]))
                s.done(nc.vector.tensor_copy(M.A1B[b, b], psW[b, 0, :]))
                s.done(nc.vector.tensor_copy(M.A2B[b, b], psW[b, 1, :]))
            dve.wait_ge(s_sel, 4)
            for n, k in enumerate(("src", "dst")):
                with dve.Fori(0, NG // 2) as i:
                    for u in range(2):
                        g = 2 * i + u
                        dve.wait_ge(s_kbu, n * NG + g + 2)
                        dve.wait_ge(s_kb[u], (n * (NG // 2) + i + 1) * 16)
                        for j in range(G):
                            last = nc.vector.scalar_tensor_tensor(
                                same[:, j, :], kB[:, u, j, :], M.key[k][:, bass.ds(G * g + j, 1)], M.lower[:, :],
                                ALU.is_equal, ALU.mult, accum_out=M.rank[k][:, bass.ds(G * g + j, 1)])
                        last.then_inc(s_kbu, 1)
            dve.wait_ge(s_kbu, 2 + 2 * NG)
            for k in ("src", "dst"):
                s.done(nc.vector.tensor_scalar(again[:, :], M.rank[k][:, :], 0.5, None, ALU.is_gt))
                s.done(nc.vector.tensor_scalar(pad[:, :], M.key[k][:, :], float(N), None, ALU.is_ge))
                s.done(nc.vector.tensor_scalar(gap[:, :], M.key[k][:, :], M.waste[:, 0:1], -1.0, ALU.subtract, ALU.mult))
                s.sync()
                s.done(nc.vector.tensor_tensor(again[:, :], again[:, :], pad[:, :], ALU.max))
                s.sync()
                s.done(nc.vector.tensor_tensor(again[:, :], again[:, :], gap[:, :], ALU.mult))
                s.sync()
                s.done(nc.vector.tensor_tensor(M.sidx[k][:, :], again[:, :], M.key[k][:, :], ALU.add))
                s.sync()
            s.done(nc.vector.tensor_scalar(gap[:, :], pad[:, :], -1.0, 1.0, ALU.mult, ALU.add))
            s.sync()
            s.done(nc.vector.tensor_tensor(gap[:, :], M.rank["dst"][:, :], gap[:, :], ALU.mult))
            s.sync()
            nc.vector.reduce_max(rmax[:, :], gap[:, :], AX.X).then_inc(s_mr, 1)
            dve.wait_ge(s_mp, 1)
            s.done(nc.vector.reduce_max(rmax1[:, :], psR[0:1, :], AX.X))
            s.sync()
            s.done(nc.vector.tensor_copy(M.rounds[:, :], rmax1[:, :]))
            s.sync()
    M.sems.retire(taken)


def spread_keys(sp, M, name, buf, free, landed):
    with sp.Fori(0, NG // 2) as i:
        for u in range(2):
            sp.wait_ge(free, 2 * i + u + 1)
            sp.nop(nofuse=True)
            sp.dma_start(buf[:, u, :, :], M.keyT[name][cols(2 * i + u), :].unsqueeze(0)
                         .to_broadcast([P, G, P])).then_inc(landed[u], 16)


def rows_at(idx, j):
    return bass.IndirectOffsetOnAxis(ap=idx[:, j:j + 1], axis=0)


def gather_and_merge(nc, pool, M, key, source, state, X, gi, si, old, new, sems, lag):
    staged_x, staged_s, x_in, x_used, state_in, state_out, merged = sems

    def stage_x(g, v):
        for n, k in enumerate(("src", "dst")):
            nc.gpsimd.tensor_copy(gi[v][:, G * n:G * n + G], M.gidx[k][:, cols(g)]).then_inc(staged_x, 1)

    def gather_x(v, some):
        for j in some:
            nc.gpsimd.indirect_dma_start(out=X[v][:, j, :], out_offset=None, in_=source,
                                         in_offset=rows_at(gi[v], j)).then_inc(x_in[v], 16)

    def gather_state(v, pair):
        for j in pair:
            nc.gpsimd.indirect_dma_start(out=old[j // 2][:, j % 2, :], out_offset=None, in_=state[j % 2],
                                         in_offset=rows_at(si[v], j)).then_inc(state_in[j], 16)

    def scatter_state(v, pair):
        for j in pair:
            nc.gpsimd.indirect_dma_start(out=state[j % 2], out_offset=rows_at(si[v], j),
                                         in_=new[j // 2][:, j % 2, :], in_offset=None).then_inc(state_out[j], 16)

    def chain(g, v, ahead):
        nc.gpsimd.tensor_copy(si[v][:, :], M.sidx[key][:, cols(g)]).then_inc(staged_s, 1)
        pool.wait_ge(staged_s, g + 1)
        wait(pool, state_out[2], 16 * g)
        wait(pool, state_out[3], 16 * g)
        pool.nop(nofuse=True)
        gather_state(v, (0, 1))
        ahead(0, 3)
        pool.wait_ge(merged, 2 * g + 1)
        pool.nop(nofuse=True)
        scatter_state(v, (0, 1))
        ahead(3, 5)
        pool.wait_ge(state_out[0], 16 * g + 16)
        pool.wait_ge(state_out[1], 16 * g + 16)
        pool.nop(nofuse=True)
        gather_state(v, (2, 3))
        ahead(5, 8)
        pool.wait_ge(merged, 2 * g + 2)
        pool.nop(nofuse=True)
        scatter_state(v, (2, 3))

    def body(g, u, h):
        if live(g + 2):
            pool.wait_ge(x_used, g + 1)
            pool.nop(nofuse=True)
            stage_x(g + 2, u)
            pool.wait_ge(staged_x, 2 * (g + 3))
            pool.nop(nofuse=True)
            ahead = lambda a, b: gather_x(u, range(a, b))
        else:
            ahead = lambda a, b: None
        if live(g - lag):
            chain(g - lag, (u + lag) % 2, ahead)
        else:
            ahead(0, 2 * G)

    stage_x(0, 0)
    stage_x(1, 1)
    pool.wait_ge(staged_x, 4)
    gather_x(0, range(2 * G))
    gather_x(1, range(2 * G))
    each_group(pool, body, lead=2 * lag, extra=lag)
    for j in range(G):
        pool.wait_ge(state_out[j], 16 * NG)


NORM_SEMS = ("centred", "squared", "summed", "rooted", "scaled")


class Norm:

    def __init__(self, nc, M, sb, sem, n):
        self.nc, self.M, self.n = nc, M, n
        self.total, self.ssq, self.root, self.rstd = (sb(k, [P, n]) for k in ("total", "ssq", "root", "rstd"))
        self.diff, self.sq, self.normed, self.h = (sb(k, [P, n, F]) for k in ("diff", "sq", "normed", "h"))
        self.centred, self.squared, self.summed, self.rooted, self.scaled = (sem(k) for k in NORM_SEMS)
        self.h_ready = sem("h_ready")

    def centre(self, s, x):
        s.done(self.nc.vector.reduce_sum(self.total[:, :], x, AX.X))
        s.sync()
        self.nc.vector.scalar_tensor_tensor(self.diff[:, :, :], x, float(F), rep(self.total[:, :], F),
                                            ALU.mult, ALU.subtract).then_inc(self.centred, 1)

    def square(self, act, g):
        act.wait_ge(self.centred, g + 1)
        self.nc.scalar.activation(self.sq[:, :, :], self.diff[:, :, :], ACT.Square).then_inc(self.squared, 1)

    def sum_squares(self, dve, g):
        dve.wait_ge(self.squared, g + 1)
        self.nc.vector.reduce_sum(self.ssq[:, :], self.sq[:, :, :], AX.X).then_inc(self.summed, 1)

    def take_root(self, act, g):
        act.wait_ge(self.summed, g + 1)
        self.nc.scalar.activation(self.root[:, :], self.ssq[:, :], ACT.Sqrt,
                                  bias=self.M.ln_eps[:, 0:1]).then_inc(self.rooted, 1)

    def scale(self, dve, s, g):
        dve.wait_ge(self.rooted, g + 1)
        s.done(self.nc.vector.reciprocal(self.rstd[:, :], self.root[:, :]))
        s.sync()
        self.nc.vector.tensor_tensor(self.normed[:, :, :], self.diff[:, :, :], rep(self.rstd[:, :], F),
                                     ALU.mult).then_inc(self.scaled, 1)

    def relu(self, act, g, h=None):
        act.wait_ge(self.scaled, g + 1)
        self.nc.scalar.activation((h or self.h)[:, :, :], self.normed[:, :, :], ACT.Relu,
                                  scale=LN_GAIN).then_inc(self.h_ready, 1)

    def transpose(self, pe, psT, g, signal):
        pe.wait_ge(self.h_ready, g + 1)
        for n in range(2):
            last = self.nc.tensor.transpose(psT[:, n, :], self.h[:, G * n:G * n + G, :].rearrange("p a f -> p (a f)"),
                                            self.M.ident[:, :])
        last.then_inc(signal, 1)


def layer0_edges(nc, t, M):
    with ExitStack() as ctx:
        sb = lambda name, shape, dt=fp32: ctx.enter_context(nc.sbuf_tensor("e0_" + name, shape, dt))
        ps = lambda name, shape: ctx.enter_context(nc.psum_tensor("e0_" + name, shape, fp32))
        taken = []
        sem = M.sems.phase("e0_", taken)
        W = F + 2
        DEN, MAX = F, F + 1
        X = [sb(f"X{u}", [P, 2 * G, F]) for u in range(2)]
        gi = [sb(f"gi{u}", [P, 2 * G], i32) for u in range(2)]
        si = [sb(f"si{u}", [P, G], i32) for u in range(2)]
        keys = sb("keys", [P, 2, G, P])
        hT = sb("hT", [P, 2, P])
        prod = [sb(f"prod{b}", [P, TAPS, F + 1]) for b in range(2)]
        msg = [sb(f"msg{u}", [P, G, F + 1]) for u in range(2)]
        score = sb("score", [P, G])
        alpha = sb("alpha", [P, G])
        same = sb("same", [P, G, P])
        off = sb("off", [P, G, P])
        diag = sb("diag", [P, G, P])
        masked = sb("masked", [P, G, P])
        less = sb("less", [P, G])
        V = sb("V", [P, G, F + 1])
        part = [sb(f"part{u}", [P, G, W]) for u in range(2)]
        old = [sb(f"old{q}", [P, 2, W]) for q in range(2)]
        new = [sb(f"new{q}", [P, 2, W]) for q in range(2)]
        empty = sb("empty", [P, 2])
        was_max = sb("was_max", [P, 2])
        gaps = sb("gaps", [P, 2, 2])
        fade = sb("fade", [P, 2, 2])
        kept = sb("kept", [P, 2, F + 1])
        added = sb("added", [P, 2, F + 1])
        psT = ps("psT", [P, 2, P])
        psX = [[ps(f"psX{b}{c}", [P, 512]) for c in range(2)] for b in range(2)]
        psA = ps("psA", [P, G, P])
        psS = ps("psS", [P, G])
        psV = ps("psV", [P, G, F + 1])

        norm = Norm(nc, M, sb, sem, 2 * G)
        staged_x, staged_s = sem("staged_x"), sem("staged_s")
        x_in = [sem(f"x_in{u}") for u in range(2)]
        state_in = [sem(f"state_in{j}") for j in range(G)]
        state_out = [sem(f"state_out{j}") for j in range(G)]
        keys_in = [sem(f"keys_in{u}") for u in range(2)]
        keys_free = sem("keys_free")
        hT_psum, hT_ready = sem("hT_psum"), sem("hT_ready")
        taps_ready, taps_used = sem("taps_ready"), sem("taps_used")
        score_ready, alpha_ready, diag_ready = sem("score_ready"), sem("alpha_ready"), sem("diag_ready")
        spread_ready, less_ready, ex_ready = sem("spread_ready"), sem("less_ready"), sem("ex_ready")
        V_ready, sums_ready, part_ready = sem("V_ready"), sem("sums_ready"), sem("part_ready")
        gaps_ready, fade_ready, merged = sem("gaps_ready"), sem("fade_ready"), sem("merged")
        s_dve, cleared = sem("dve_steps"), sem("cleared")
        block = ctx.enter_context(nc.Block())

        @block.sync
        def _(sp):
            M.sems.clear(sp)
            for tab in M.max_state + [M.rel_sums]:
                w = tab.shape[1]
                sp.dma_start(tab.rearrange("(p a r) w -> p a (r w)", p=P, a=28),
                             along(M.zeros[:, 0:28 * w], 28)).then_inc(cleared, 16)
            spread_keys(sp, M, "src", keys, keys_free, keys_in)
            sp.wait_ge(cleared, 48)

        @block.gpsimd
        def _(pool):
            gather_and_merge(nc, pool, M, "src", t["x"], M.softmax_state, X, gi, si, old, new,
                             (staged_x, staged_s, x_in, norm.centred, state_in, state_out, merged), LAG0)

        @block.scalar
        def _(act):
            def merge(pair, g):
                act.wait_ge(gaps_ready, 2 * g + pair + 1)
                nc.scalar.activation(fade[:, :, :], gaps[:, :, :], ACT.Exp).then_inc(fade_ready, 1)

            def body(g, u, i):
                if live(g + 1):
                    norm.square(act, g + 1)
                if live(g - 1):
                    act.wait_ge(less_ready, g)
                    nc.scalar.activation(V[:, :, F], less[:, :], ACT.Exp).then_inc(ex_ready, 1)
                if live(g - LAG0):
                    merge(0, g - LAG0)
                if live(g + 1):
                    norm.take_root(act, g + 1)
                    norm.relu(act, g + 1)
                if live(g - 1):
                    act.wait_ge(sums_ready, g)
                    nc.scalar.activation(part[1 - u][:, :, 0:F + 1], psV[:, :, :], ACT.Copy).then_inc(part_ready, 1)
                if live(g + 1):
                    act.wait_ge(hT_psum, g + 2)
                    nc.scalar.activation(hT[:, :, :], psT[:, :, :], ACT.Copy).then_inc(hT_ready, 1)
                if live(g - LAG0):
                    merge(1, g - LAG0)
                if live(g):
                    act.wait_ge(alpha_ready, g + 1)
                    for j in range(G):
                        last = nc.scalar.activation(diag[:, j, :], M.ident[:, :], ACT.Copy, scale=alpha[:, j:j + 1])
                    last.then_inc(diag_ready, 1)

            norm.square(act, 0)
            norm.take_root(act, 0)
            norm.relu(act, 0)
            act.wait_ge(hT_psum, 1)
            nc.scalar.activation(hT[:, :, :], psT[:, :, :], ACT.Copy).then_inc(hT_ready, 1)
            each_group(act, body, lead=4, extra=LAG0)

        @block.tensor
        def _(pe):
            def taps(g, j):
                wait(pe, taps_used, G * g + j - 1)
                w = M.WB[:, j, :, :].rearrange("p k o -> p (k o)")
                cut = TC * (F + 1)
                nc.tensor.matmul(psX[j % 2][0][:, 0:cut], hT[:, 1, :], w[:, 0:cut], start=True, stop=True)
                nc.tensor.matmul(psX[j % 2][1][:, 0:TAPS * (F + 1) - cut], hT[:, 1, :], w[:, cut:],
                                 start=True, stop=True).then_inc(taps_ready, 1)

            def first_half(g):
                pe.wait_ge(hT_ready, g + 1)
                taps(g, 0)
                taps(g, 1)

            def body(g, u, i):
                if live(g):
                    taps(g, 2)
                    taps(g, 3)
                    wait(pe, alpha_ready, g)
                    nc.tensor.matmul(psS[:, :], hT[:, 0, :], M.RA[:, :], start=True, stop=True).then_inc(score_ready, 1)
                if live(g - 1):
                    pe.wait_ge(V_ready, g)
                    for j in range(G):
                        last = nc.tensor.matmul(psV[:, j, :], same[:, j, :], V[:, j, :], start=True, stop=True)
                    last.then_inc(sums_ready, 1)
                if live(g + 1):
                    norm.transpose(pe, psT, g + 1, hT_psum)
                    first_half(g + 1)
                if live(g):
                    pe.wait_ge(diag_ready, g + 1)
                    nc.tensor.matmul(psA[:, :, :].rearrange("p a b -> p (a b)"), M.ones[:, :],
                                     diag[:, :, :].rearrange("p a b -> p (a b)"),
                                     start=True, stop=True).then_inc(spread_ready, 1)

            norm.transpose(pe, psT, 0, hT_psum)
            first_half(0)
            each_group(pe, body, lead=4, extra=1)

        @block.vector
        def _(dve):
            s = Steps(dve, s_dve, PER_E0)

            def merge(pair, g, v):
                mine = part[v][:, 2 * pair:2 * pair + 2, :]
                o, n = old[pair], new[pair]
                for j in (2 * pair, 2 * pair + 1):
                    dve.wait_ge(state_in[j], 16 * g + 16)
                dve.wait_ge(part_ready, g + 1)
                s.done(nc.vector.tensor_scalar(empty[:, :], o[:, :, DEN], 0.0, -BIG, ALU.is_equal, ALU.mult))
                s.sync()
                s.done(nc.vector.tensor_tensor(was_max[:, :], o[:, :, MAX], empty[:, :], ALU.add))
                s.sync()
                s.done(nc.vector.tensor_tensor(n[:, :, MAX], was_max[:, :], mine[:, :, MAX], ALU.max))
                s.sync()
                s.done(nc.vector.tensor_tensor(gaps[:, 0, :], was_max[:, :], n[:, :, MAX], ALU.subtract))
                nc.vector.tensor_tensor(gaps[:, 1, :], mine[:, :, MAX], n[:, :, MAX], ALU.subtract).then_inc(gaps_ready, 1)

            def merge_end(pair, g, v):
                mine = part[v][:, 2 * pair:2 * pair + 2, :]
                o, n = old[pair], new[pair]
                dve.wait_ge(fade_ready, 2 * g + pair + 1)
                s.done(nc.vector.tensor_tensor(kept[:, :, :], o[:, :, 0:F + 1], rep(fade[:, 0, :], F + 1), ALU.mult))
                s.done(nc.vector.tensor_tensor(added[:, :, :], mine[:, :, 0:F + 1], rep(fade[:, 1, :], F + 1), ALU.mult))
                s.sync()
                nc.vector.tensor_tensor(n[:, :, 0:F + 1], kept[:, :, :], added[:, :, :], ALU.add).then_inc(merged, 1)

            def weigh(g, u, j):
                dve.wait_ge(taps_ready, G * g + j + 1)
                lo_j = G * g + j
                coef = M.C[:, lo_j, :] if isinstance(g, int) else \
                    M.C[:, bass.ds(lo_j, 1), :].rearrange("p a k -> p (a k)")
                for c, (lo, hi) in enumerate(((0, TC), (TC, TAPS))):
                    last = nc.vector.tensor_tensor(
                        prod[j % 2][:, lo:hi, :], psX[j % 2][c][:, 0:(hi - lo) * (F + 1)].rearrange("p (k o) -> p k o", o=F + 1),
                        rep(coef[:, lo:hi], F + 1), ALU.mult)
                    if c == 0:
                        s.done(last)
                last.then_inc(taps_used, 1)
                s.sync()
                dve.wait_ge(taps_used, G * g + j + 1)
                s.done(nc.vector.reduce_sum(msg[u][:, j, :], prod[j % 2][:, :, :].rearrange("p k o -> p o k"), AX.X))

            def body(g, u, i):
                if live(g + 1):
                    dve.wait_ge(x_in[1 - u], 16 * 2 * G * ((g + 1) // 2 + 1 if isinstance(g, int) else i + u + 1))
                    norm.centre(s, X[1 - u][:, :, :])
                if live(g):
                    weigh(g, u, 0)
                if live(g - 1):
                    dve.wait_ge(spread_ready, g)
                    s.done(nc.vector.tensor_tensor(masked[:, :, :], off[:, :, :], psA[:, :, :], ALU.add))
                    s.sync()
                    s.done(nc.vector.reduce_max(part[1 - u][:, :, MAX], masked[:, :, :], AX.X))
                    s.sync()
                    nc.vector.tensor_tensor(less[:, :], alpha[:, :], part[1 - u][:, :, MAX], ALU.subtract).then_inc(less_ready, 1)
                if live(g - LAG0):
                    merge(0, g - LAG0, u)
                if live(g + 1):
                    norm.sum_squares(dve, g + 1)
                if live(g):
                    weigh(g, u, 1)
                if live(g - 1):
                    dve.wait_ge(ex_ready, g)
                    nc.vector.tensor_tensor(V[:, :, 0:F], msg[1 - u][:, :, 0:F], rep(V[:, :, F], F), ALU.mult).then_inc(V_ready, 1)
                if live(g - LAG0):
                    merge_end(0, g - LAG0, u)
                if live(g + 1):
                    norm.scale(dve, s, g + 1)
                if live(g):
                    weigh(g, u, 2)
                if live(g - LAG0):
                    merge(1, g - LAG0, u)
                if live(g):
                    dve.wait_ge(keys_in[u], 16 * (i + 1))
                    wait(dve, sums_ready, g)
                    s.done(nc.vector.tensor_tensor(same[:, :, :], keys[:, u, :, :], rep(M.key["src"][:, cols(g)], P),
                                                   ALU.is_equal))
                    weigh(g, u, 3)
                if live(g - LAG0):
                    merge_end(1, g - LAG0, u)
                if live(g):
                    nc.vector.tensor_scalar(off[:, :, :], same[:, :, :], 1.0, BIG, ALU.subtract, ALU.mult).then_inc(keys_free, 1)
                    dve.wait_ge(score_ready, g + 1)
                    s.sync()
                    s.done(nc.vector.tensor_tensor(score[:, :], msg[u][:, :, F], psS[:, :], ALU.add))
                    s.sync()
                    nc.vector.scalar_tensor_tensor(alpha[:, :], score[:, :], SLOPE, score[:, :],
                                                   ALU.mult, ALU.max).then_inc(alpha_ready, 1)
                    dve.wait_ge(keys_free, g + 3)

            nc.vector.sem_inc(keys_free, 2)
            dve.wait_ge(x_in[0], 16 * 2 * G)
            norm.centre(s, X[0][:, :, :])
            norm.sum_squares(dve, 0)
            norm.scale(dve, s, 0)
            each_group(dve, body, s, lead=4, extra=LAG0)


def live_chunk(c):
    return not isinstance(c, int) or c < NCH


def after(c, u, i):
    return c + 1, 1 - u, (c + 1) // 2 if isinstance(c, int) else i + u


def project_pe(nc, pe, M, weights, h, psT, hT, psR, sems, c, u):
    h_ready, hT_psum, hT_ready, round_ready, used = sems
    flat = h[:, :, :].rearrange("p k f -> p (k f)")
    pe.wait_ge(h_ready, c + 1)
    for q in range(3):
        r, b = 3 * c + q, (u + q) % 2
        wait(pe, hT_ready, r - 1)
        for n in range(G):
            last = nc.tensor.transpose(psT[b][:, n, :], flat[:, P * (G * q + n):P * (G * q + n) + P], M.ident[:, :])
        last.then_inc(hT_psum, 1)
        if q == 0:
            wait(pe, used, c)
        pe.wait_ge(hT_ready, r + 1)
        for n in range(G):
            last = nc.tensor.matmul(psR[q][:, P * n:P * n + P], hT[b][:, n, :], weights[:, :], start=True, stop=True)
        last.then_inc(round_ready, 1)


def project_scalar(nc, act, psT, hT, sems, c, u, q):
    h_ready, hT_psum, hT_ready, round_ready, used = sems
    r, b = 3 * c + q, (u + q) % 2
    act.wait_ge(hT_psum, r + 1)
    wait(act, round_ready, r - 1)
    nc.scalar.activation(hT[b][:, :, :], psT[b][:, :, :], ACT.Copy).then_inc(hT_ready, 1)


def dense0(nc, t, M, dest):
    with ExitStack() as ctx:
        sb = lambda name, shape, dt=fp32: ctx.enter_context(nc.sbuf_tensor("d0_" + name, shape, dt))
        ps = lambda name, shape: ctx.enter_context(nc.psum_tensor("d0_" + name, shape, fp32))
        taken = []
        sem = M.sems.phase("d0_", taken)
        W = F + 2
        DEN, MAX = F, F + 1
        X = [sb(f"X{u}", [P, K, F]) for u in range(2)]
        S = [[sb(f"S{u}{k}", [P, K, W]) for k in range(2)] for u in range(2)]
        Y = [sb(f"Y{u}", [P, K, F]) for u in range(2)]
        hT = [sb(f"hT{q}", [P, G, P]) for q in range(2)]
        empty = sb("empty", [P, 2, K])
        top = sb("top", [P, K])
        gaps = sb("gaps", [P, 2, K])
        fade = sb("fade", [P, 2, K])
        dens = sb("dens", [P, 2, K])
        den = sb("den", [P, K])
        inv = sb("inv", [P, K])
        part = [sb(f"part{k}", [P, K, F]) for k in range(2)]
        was = sb("was", [P, 2, K])
        share = sb("share", [P, 2, K])
        sums = [sb(f"sums{u}", [P, K, F]) for u in range(2)]
        base = [sb(f"base{u}", [P, K, F]) for u in range(2)]
        both = sb("both", [P, K, F])
        psT = [ps(f"psT{q}", [P, G, P]) for q in range(2)]
        psR = [ps(f"psR{q}", [P, G * P]) for q in range(3)]
        loaded = [sem(f"loaded{u}") for u in range(2)]
        stored = sem("stored")
        norm = Norm(nc, M, sb, sem, K)
        h = [norm.h, sb("h1", [P, K, F])]
        hT_psum, hT_ready = sem("hT_psum"), sem("hT_ready")
        gaps_ready, fade_ready, share_ready, sums_ready = sem("gaps_ready"), sem("fade_ready"), sem("share_ready"), sem("sums_ready")
        round_ready = sem("round_ready")
        added, done = sem("added"), sem("done")
        proj_sems = norm.h_ready, hT_psum, hT_ready, round_ready, done
        s_dve, s_pool = sem("dve_steps"), sem("pool_steps")
        block = ctx.enter_context(nc.Block())

        @block.sync
        def _(sp):
            M.sems.clear(sp)
            def load(c, u):
                sp.dma_start(X[u][:, :, :], chunk(t["x"], c)).then_inc(loaded[u], 16)
                for k in range(2):
                    sp.dma_start(S[u][k][:, :, :], chunk(M.softmax_state[k], c)).then_inc(loaded[u], 16)

            def refill(c, u):
                sp.wait_ge(sums_ready, c + 1)
                sp.wait_ge(norm.centred, c + 1)
                sp.nop(nofuse=True)
                load(c + 2, u)

            def body(c, u, i):
                if not isinstance(c, int) or c + 3 < NCH:
                    refill(c + 1, 1 - u)
                sp.wait_ge(done, c + 1)
                sp.nop(nofuse=True)
                wait(sp, stored, 16 * c)
                sp.nop(nofuse=True)
                sp.dma_start(chunk(dest, c), Y[u][:, :, :]).then_inc(stored, 16)

            load(0, 0)
            load(1, 1)
            refill(0, 0)
            each_chunk(sp, body)
            sp.wait_ge(stored, 16 * NCH)

        @block.gpsimd
        def _(pool):
            s = Steps(pool, s_pool, 3)

            def body(c, u, i):
                pool.wait_ge(loaded[u], 48 * (i + 1))
                pool.wait_ge(share_ready, c + 1)
                for k in range(2):
                    s.done(nc.gpsimd.tensor_tensor(part[k][:, :, :], S[u][k][:, :, 0:F], rep(share[:, k, :], F), ALU.mult))
                wait(pool, added, c - 1)
                s.done(nc.gpsimd.tensor_tensor(base[u][:, :, :], X[u][:, :, :], along(M.bias0[:, :], K), ALU.add))
                s.sync()
                nc.gpsimd.tensor_tensor(sums[u][:, :, :], part[0][:, :, :], part[1][:, :, :], ALU.add).then_inc(sums_ready, 1)

            each_chunk(pool, body, s)

        @block.scalar
        def _(act):
            def body(c, u, i):
                n, v, _ = after(c, u, i)
                if live_chunk(n):
                    act.wait_ge(gaps_ready, n + 1)
                    nc.scalar.activation(fade[:, :, :], gaps[:, :, :], ACT.Exp).then_inc(fade_ready, 1)
                    norm.square(act, n)
                project_scalar(nc, act, psT, hT, proj_sems, c, u, 0)
                if live_chunk(n):
                    norm.take_root(act, n)
                project_scalar(nc, act, psT, hT, proj_sems, c, u, 1)
                project_scalar(nc, act, psT, hT, proj_sems, c, u, 2)
                if live_chunk(n):
                    norm.relu(act, n, h[v])

            act.wait_ge(gaps_ready, 1)
            nc.scalar.activation(fade[:, :, :], gaps[:, :, :], ACT.Exp).then_inc(fade_ready, 1)
            norm.square(act, 0)
            norm.take_root(act, 0)
            norm.relu(act, 0)
            each_chunk(act, body)

        @block.tensor
        def _(pe):
            each_chunk(pe, lambda c, u, i: project_pe(nc, pe, M, M.ROOT, h[u], psT, hT, psR, proj_sems, c, u))

        @block.vector
        def _(dve):
            s = Steps(dve, s_dve, PER_D0)

            def states(c, u, i):
                dve.wait_ge(loaded[u], 48 * (i + 1))
                wait(dve, norm.scaled, c)
                for k in range(2):
                    s.done(nc.vector.tensor_scalar(empty[:, k, :], S[u][k][:, :, DEN], 0.0, -BIG, ALU.is_equal, ALU.mult))
                s.sync()
                for k in range(2):
                    s.done(nc.vector.tensor_tensor(was[:, k, :], S[u][k][:, :, MAX], empty[:, k, :], ALU.add))
                s.sync()
                s.done(nc.vector.tensor_tensor(top[:, :], was[:, 0, :], was[:, 1, :], ALU.max))
                s.sync()
                nc.vector.tensor_tensor(gaps[:, :, :], was[:, :, :], along(top[:, :], 2), ALU.subtract).then_inc(gaps_ready, 1)

            def shares(c, u):
                dve.wait_ge(fade_ready, c + 1)
                for k in range(2):
                    s.done(nc.vector.tensor_tensor(dens[:, k, :], S[u][k][:, :, DEN], fade[:, k, :], ALU.mult))
                s.sync()
                s.done(nc.vector.scalar_tensor_tensor(den[:, :], dens[:, 0, :], 1e-16, dens[:, 1, :], ALU.add, ALU.add))
                s.sync()
                s.done(nc.vector.reciprocal(inv[:, :], den[:, :]))
                s.sync()
                wait(dve, sums_ready, c)
                nc.vector.tensor_tensor(share[:, :, :], fade[:, :, :], along(inv[:, :], 2), ALU.mult).then_inc(share_ready, 1)

            def body(c, u, i):
                n, v, k = after(c, u, i)
                if live_chunk(n):
                    states(n, v, k)
                    norm.centre(s, X[v][:, :, :])
                    shares(n, v)
                    norm.sum_squares(dve, n)
                dve.wait_ge(sums_ready, c + 1)
                wait(dve, done, c)
                nc.vector.tensor_tensor(both[:, :, :], base[u][:, :, :], sums[u][:, :, :], ALU.add).then_inc(added, 1)
                if live_chunk(n):
                    norm.scale(dve, s, n)
                dve.wait_ge(added, c + 1)
                wait(dve, stored, 16 * (c - 1))
                dve.wait_ge(round_ready, 3 * c + 3)
                m = G * G
                for q in range(3):
                    last = nc.vector.tensor_tensor(Y[u][:, m * q:m * q + m, :], both[:, m * q:m * q + m, :],
                                                   psR[q][:, :].rearrange("p (k f) -> p k f", f=F), ALU.add)
                last.then_inc(done, 1)

            states(0, 0, 0)
            norm.centre(s, X[0][:, :, :])
            shares(0, 0)
            norm.sum_squares(dve, 0)
            norm.scale(dve, s, 0)
            each_chunk(dve, body, s)
    M.sems.retire(taken)


def layer1_edges(nc, t, M):
    with ExitStack() as ctx:
        sb = lambda name, shape, dt=fp32: ctx.enter_context(nc.sbuf_tensor("e1_" + name, shape, dt))
        ps = lambda name, shape: ctx.enter_context(nc.psum_tensor("e1_" + name, shape, fp32))
        taken = []
        sem = M.sems.phase("e1_", taken)
        W = F + 1
        X = [sb(f"X{u}", [P, 2 * G, F]) for u in range(2)]
        gi = [sb(f"gi{u}", [P, 2 * G], i32) for u in range(2)]
        si = [sb(f"si{u}", [P, G], i32) for u in range(2)]
        attr = [sb(f"attr{u}", [P, G, F]) for u in range(2)]
        hT = sb("hT", [P, 3, P])
        hidden = sb("hidden", [P, 2, P])
        biased = sb("biased", [P, G, F])
        old = [sb(f"old{q}", [P, 2, W]) for q in range(2)]
        new = [sb(f"new{q}", [P, 2, W]) for q in range(2)]
        psT = ps("psT", [P, 3, P])
        psH = ps("psH", [P, 2, P])
        psV = ps("psV", [P, G, F])

        staged_x, staged_s = sem("staged_x"), sem("staged_s")
        x_in = [sem(f"x_in{u}") for u in range(2)]
        state_in = [sem(f"state_in{j}") for j in range(G)]
        state_out = [sem(f"state_out{j}") for j in range(G)]
        attr_in = [sem(f"attr_in{u}") for u in range(2)]
        attr_free, attr_clear = sem("attr_free"), sem("attr_clear")
        norm = Norm(nc, M, sb, sem, 2 * G)
        hT_psum, hT_ready = sem("hT_psum"), sem("hT_ready")
        hidden_psum, hidden_ready, out_ready = sem("hidden_psum"), sem("hidden_ready"), sem("out_ready")
        out_used = sem("out_used")
        merged, s_dve, cleared = sem("merged"), sem("dve_steps"), sem("cleared")
        block = ctx.enter_context(nc.Block())

        @block.sync
        def _(sp):
            M.sems.clear(sp)
            for tab in (M.conv_sums, M.square_sums):
                w = tab.shape[1]
                sp.dma_start(tab.rearrange("(p a r) w -> p a (r w)", p=P, a=28),
                             along(M.zeros[:, 0:28 * w], 28)).then_inc(cleared, 16)
            sp.wait_ge(attr_clear, 1)
            rows = t["edge_attr_32"].rearrange("(p t) f -> p t f", p=ROWS_E)
            with sp.Fori(0, NG // 2) as i:
                for u in range(2):
                    sp.wait_ge(attr_free, 2 * i + u + 1)
                    sp.nop(nofuse=True)
                    sp.dma_start(attr[u][0:ROWS_E, :, :], rows[:, cols(2 * i + u), :]).then_inc(attr_in[u], 16)
            sp.wait_ge(cleared, 32)

        @block.gpsimd
        def _(pool):
            gather_and_merge(nc, pool, M, "dst", M.x1, M.max_state, X, gi, si, old, new,
                             (staged_x, staged_s, x_in, norm.centred, state_in, state_out, merged), 1)

        @block.scalar
        def _(act):
            def front(g):
                norm.square(act, g)
                norm.take_root(act, g)
                norm.relu(act, g)
                act.wait_ge(hT_psum, g + 1)
                nc.scalar.activation(hT[:, :, :], psT[:, :, :], ACT.Copy).then_inc(hT_ready, 1)

            def body(g, u, i):
                act.wait_ge(hidden_psum, g + 1)
                nc.scalar.activation(hidden[:, :, :], psH[:, :, :], ACT.Relu, bias=M.b1col[:, 0:1]).then_inc(hidden_ready, 1)
                if live(g + 1):
                    front(g + 1)

            front(0)
            each_group(act, body)

        @block.tensor
        def _(pe):
            def front(g, u, i):
                pe.wait_ge(attr_in[u], 16 * (i + 1))
                nc.tensor.transpose(psT[:, 2, :], attr[u][:, :, :].rearrange("p a f -> p (a f)"),
                                    M.ident[:, :]).then_inc(attr_free, 1)
                norm.transpose(pe, psT, g, hT_psum)

            def body(g, u, i):
                pe.wait_ge(hT_ready, g + 1)
                for j in range(2):
                    for n, w in enumerate((M.W1S, M.W1D, M.W1E)):
                        last = nc.tensor.matmul(psH[:, j, :], w[:, j, :], hT[:, n, :], start=(n == 0), stop=(n == 2))
                last.then_inc(hidden_psum, 1)
                pe.wait_ge(hidden_ready, g + 1)
                wait(pe, out_used, g)
                for j in range(2):
                    last = nc.tensor.matmul(psV[:, 2 * j:2 * j + 2, :].rearrange("p a f -> p (a f)"), hidden[:, j, :],
                                            M.W2B[:, :], start=True, stop=True)
                last.then_inc(out_ready, 1)
                if live(g + 1):
                    front(g + 1, 1 - u, (g + 1) // 2 if isinstance(g, int) else i + u)

            front(0, 0, 0)
            each_group(pe, body)

        @block.vector
        def _(dve):
            s = Steps(dve, s_dve, PER_E1)

            def merge(pair, g):
                lo = G * g + 2 * pair
                mine = M.V1[:, lo:lo + 2, :] if isinstance(lo, int) else M.V1[:, bass.ds(lo, 2), :]
                for j in (2 * pair, 2 * pair + 1):
                    dve.wait_ge(state_in[j], 16 * g + 16)
                nc.vector.tensor_tensor(new[pair][:, :, :], old[pair][:, :, :], mine, ALU.max).then_inc(merged, 1)

            def body(g, u, i):
                if live(g - 1):
                    merge(0, g - 1)
                if live(g):
                    dve.wait_ge(out_ready, g + 1)
                    nc.vector.tensor_tensor(biased[:, :, :], psV[:, :, :], along(M.b2row[:, :], G), ALU.add).then_inc(out_used, 1)
                if live(g + 1):
                    dve.wait_ge(x_in[1 - u], 16 * 2 * G * ((g + 1) // 2 + 1 if isinstance(g, int) else i + u + 1))
                    norm.centre(s, X[1 - u][:, :, :])
                if live(g):
                    dve.wait_ge(out_used, g + 1)
                    s.done(nc.vector.tensor_scalar(M.V1[:, cols(g), 0:F], biased[:, :, :], 0.0, None, ALU.max))
                    s.done(nc.vector.tensor_copy(M.V1[:, cols(g), F], M.eid1[:, cols(g)]))
                if live(g + 1):
                    norm.sum_squares(dve, g + 1)
                if live(g - 1):
                    merge(1, g - 1)
                if live(g + 1):
                    norm.scale(dve, s, g + 1)
                s.sync()

            for u in range(2):
                last = nc.vector.memset(attr[u][:, :, :], 0.0)
            last.then_inc(attr_clear, 1)
            nc.vector.sem_inc(attr_free, 2)
            dve.wait_ge(x_in[0], 16 * 2 * G)
            norm.centre(s, X[0][:, :, :])
            norm.sum_squares(dve, 0)
            norm.scale(dve, s, 0)
            each_group(dve, body, s, extra=1)


def more_maxima(nc, M):
    with ExitStack() as ctx:
        sb = lambda name, shape, dt=fp32: ctx.enter_context(nc.sbuf_tensor("r1_" + name, shape, dt))
        taken = []
        sem = M.sems.phase("r1_", taken)
        W = F + 1
        ridx = sb("ridx", [P, T], i32)
        si = sb("si", [P, 2], i32)
        old = sb("old", [P, 2, W])
        new = sb("new", [P, 2, W])
        turn = sb("turn", [P, 2])
        other = sb("other", [P, T])
        pad = sb("pad", [P, T])
        gap = sb("gap", [P, T])
        shift = sb("shift", [P, T])
        chosen, staged, state_in, merged, state_out = (sem(n) for n in ("chosen", "staged", "state_in", "merged", "state_out"))
        state_in = [sem(f"state_in_{k}") for k in range(2)]
        state_out = [sem(f"state_out_{k}") for k in range(2)]
        s_dve, round_over = sem("dve_steps"), sem("round_over")
        block = ctx.enter_context(nc.Block())
        pairs = T // 2

        @block.gpsimd
        def _(pool):
            rounds = pool.value_load(M.rounds[0:1, 0:1], min_val=0, max_val=P)
            with pool.If(rounds > 0):
                with pool.Fori(0, rounds) as r:
                    pool.wait_ge(chosen, r + 1)
                    pool.nop(nofuse=True)
                    with pool.Fori(0, pairs) as i:
                        n = r * pairs + i
                        nc.gpsimd.tensor_copy(si[:, :], ridx[:, bass.ds(2 * i, 2)]).then_inc(staged, 1)
                        pool.wait_ge(staged, n + 1)
                        pool.nop(nofuse=True)
                        for k in range(2):
                            nc.gpsimd.indirect_dma_start(out=old[:, k, :], out_offset=None, in_=M.max_state[k],
                                                         in_offset=rows_at(si, k)).then_inc(state_in[k], 16)
                        pool.wait_ge(merged, n + 1)
                        pool.nop(nofuse=True)
                        for k in range(2):
                            nc.gpsimd.indirect_dma_start(out=M.max_state[k], out_offset=rows_at(si, k),
                                                         in_=new[:, k, :], in_offset=None).then_inc(state_out[k], 16)
                        pool.wait_ge(state_out[0], 16 * n + 16)
                        pool.wait_ge(state_out[1], 16 * n + 16)
                        pool.nop(nofuse=True)

        @block.vector
        def _(dve):
            rounds = dve.value_load(M.rounds[0:1, 0:1], min_val=0, max_val=P)
            s = Steps(dve, s_dve)
            s.done(nc.vector.memset(turn[:, 0:1], 0.0))
            s.done(nc.vector.tensor_scalar(pad[:, :], M.key["dst"][:, :], float(N), None, ALU.is_ge))
            s.done(nc.vector.tensor_scalar(gap[:, :], M.key["dst"][:, :], M.waste[:, 0:1], -1.0, ALU.subtract, ALU.mult))
            s.sync()
            s.per, before = PER_R1, s.n
            with dve.If(rounds > 0):
                with dve.Fori(0, rounds) as r:
                    s.enter(before, r)
                    s.done(nc.vector.tensor_scalar(turn[:, 1:2], turn[:, 0:1], 1.0, None, ALU.add))
                    s.sync()
                    s.done(nc.vector.tensor_copy(turn[:, 0:1], turn[:, 1:2]))
                    s.done(nc.vector.tensor_scalar(other[:, :], M.rank["dst"][:, :], turn[:, 1:2], None, ALU.not_equal))
                    s.sync()
                    s.done(nc.vector.tensor_tensor(shift[:, :], other[:, :], pad[:, :], ALU.max))
                    s.sync()
                    s.done(nc.vector.tensor_tensor(other[:, :], shift[:, :], gap[:, :], ALU.mult))
                    s.sync()
                    nc.vector.tensor_tensor(ridx[:, :], other[:, :], M.key["dst"][:, :], ALU.add).then_inc(chosen, 1)
                    s.leave()
                    with dve.Fori(0, pairs) as i:
                        n = r * pairs + i
                        for k in range(2):
                            dve.wait_ge(state_in[k], 16 * n + 16)
                        nc.vector.tensor_tensor(new[:, :, :], old[:, :, :], M.V1[:, bass.ds(2 * i, 2), :],
                                                ALU.max).then_inc(merged, 1)


def dense1(nc, t, M, early):
    with ExitStack() as ctx:
        sb = lambda name, shape, dt=fp32: ctx.enter_context(nc.sbuf_tensor("d1_" + name, shape, dt))
        taken = []
        sem = M.sems.phase("d1_", taken)
        W = F + 1
        X = [sb(f"X{u}", [P, K, F]) for u in range(2)]
        S = [[sb(f"S{u}{k}", [P, K, W]) for k in range(2)] for u in range(2)]
        Y = [sb(f"Y{u}", [P, K, W]) for u in range(2)]
        top = sb("top", [P, K, W])
        best = sb("best", [P, K, F])
        x_in = [sem(f"x_in{u}") for u in range(2)]
        states_in = [sem(f"states_in{u}") for u in range(2)]
        states_used = sem("states_used")
        stored = sem("stored")
        norm = Norm(nc, M, sb, sem, K)
        best_ready, done = sem("best_ready"), sem("done")
        s_dve = sem("dve_steps")
        block = ctx.enter_context(nc.Block())

        @block.sync
        def _(sp):
            M.sems.clear(sp)
            def load_x(c, u):
                sp.dma_start(X[u][:, :, :], chunk(M.x1, c)).then_inc(x_in[u], 16)

            def load_states(c, u):
                for k in range(2):
                    sp.dma_start(S[u][k][:, :, :], chunk(M.max_state[k], c)).then_inc(states_in[u], 16)

            def refill_states(c, u):
                sp.wait_ge(states_used, c + 1)
                sp.nop(nofuse=True)
                load_states(c + 2, u)

            def body(c, u, i):
                sp.wait_ge(done, c + 1)
                sp.nop(nofuse=True)
                if not isinstance(c, int) or c + 2 < NCH:
                    load_x(c + 2, u)
                wait(sp, stored, 16 * c)
                sp.nop(nofuse=True)
                if early:
                    sp.dma_start(chunk(early, c), Y[u][:, :, 0:F]).then_inc(stored, 16)
                else:
                    sp.dma_start(chunk(M.x2, c), Y[u][:, :, :]).then_inc(stored, 16)
                if not isinstance(c, int) or c + 3 < NCH:
                    refill_states(c + 1, 1 - u)

            for c in range(2):
                load_x(c, c)
                load_states(c, c)
            refill_states(0, 0)
            each_chunk(sp, body)
            sp.wait_ge(stored, 16 * NCH)

        @block.gpsimd
        def _(pool):
            def body(c, u, i):
                pool.wait_ge(x_in[u], 16 * (i + 1))
                pool.wait_ge(best_ready, c + 1)
                nc.gpsimd.tensor_tensor(Y[u][:, :, 0:F], X[u][:, :, :], best[:, :, :], ALU.add).then_inc(done, 1)

            each_chunk(pool, body)

        @block.scalar
        def _(act):
            def body(c, u, i):
                norm.square(act, c)
                norm.take_root(act, c)
                norm.relu(act, c)

            each_chunk(act, body)

        @block.vector
        def _(dve):
            s = Steps(dve, s_dve, PER_D1)

            def begin(c, u, i):
                dve.wait_ge(x_in[u], 16 * (i + 1))
                wait(dve, norm.scaled, c)
                norm.centre(s, X[u][:, :, :])

            def end(c, u, i):
                wait(dve, stored, 16 * (c - 1))
                s.done(nc.vector.tensor_copy(Y[u][:, :, F], top[:, :, F]))
                dve.wait_ge(norm.h_ready, c + 1)
                wait(dve, done, c)
                nc.vector.tensor_tensor(best[:, :, :], norm.h[:, :, :], top[:, :, 0:F], ALU.max).then_inc(best_ready, 1)

            def states(c, u, i):
                dve.wait_ge(states_in[u], 32 * (i + 1))
                wait(dve, best_ready, c)
                nc.vector.tensor_tensor(top[:, :, :], S[u][0][:, :, :], S[u][1][:, :, :], ALU.max).then_inc(states_used, 1)
                norm.sum_squares(dve, c)
                norm.scale(dve, s, c)
                dve.wait_ge(states_used, c + 1)

            def body(c, u, i):
                n, v, k = after(c, u, i)
                if live_chunk(n):
                    begin(n, v, k)
                end(c, u, i)
                if live_chunk(n):
                    s.sync()
                    states(n, v, k)

            begin(0, 0, 0)
            states(0, 0, 0)
            each_chunk(dve, body, s)
    M.sems.retire(taken)


def gather_and_add(nc, pool, M, wanted, key, source, sums, X, gi, si, part, sems):
    staged_x, staged_s, x_in, x_used, part_ready, landed = sems
    nx = G * len(wanted)

    def stage_x(g, v):
        for n, k in enumerate(wanted):
            nc.gpsimd.tensor_copy(gi[v][:, G * n:G * n + G], M.gidx[k][:, cols(g)]).then_inc(staged_x, 1)

    def gather_x(v, some):
        for j in some:
            nc.gpsimd.indirect_dma_start(out=X[v][:, j, :], out_offset=None, in_=source,
                                         in_offset=rows_at(gi[v], j)).then_inc(x_in[v], 16)

    def adds(g, v, ahead):
        wait(pool, landed, 16 * G * g)
        pool.nop(nofuse=True)
        nc.gpsimd.tensor_copy(si[v][:, :], M.sidx[key][:, cols(g)]).then_inc(staged_s, 1)
        pool.wait_ge(staged_s, g + 1)
        pool.nop(nofuse=True)
        pool.wait_ge(part_ready, g + 1)
        pool.nop(nofuse=True)
        for j in range(G):
            if j:
                pool.wait_ge(landed, 16 * (G * g + j))
                pool.nop(nofuse=True)
            nc.gpsimd.indirect_dma_start(out=sums, out_offset=rows_at(si[v], j), in_=part[v][:, j, :],
                                         in_offset=None, compute_op=ALU.add).then_inc(landed, 16)
            ahead(j * nx // G, (j + 1) * nx // G)

    def body(g, u, h):
        if live(g + 2):
            pool.wait_ge(x_used, g + 1)
            pool.nop(nofuse=True)
            stage_x(g + 2, u)
            pool.wait_ge(staged_x, len(wanted) * (g + 3))
            pool.nop(nofuse=True)
            ahead = lambda a, b: gather_x(u, range(a, b))
        else:
            ahead = lambda a, b: None
        if live(g - 1):
            adds(g - 1, 1 - u, ahead)
        else:
            ahead(0, nx)

    stage_x(0, 0)
    stage_x(1, 1)
    pool.wait_ge(staged_x, 2 * len(wanted))
    gather_x(0, range(nx))
    gather_x(1, range(nx))
    each_group(pool, body, extra=1)
    pool.wait_ge(landed, 16 * G * NG)


def layer2_edges(nc, t, M):
    with ExitStack() as ctx:
        sb = lambda name, shape, dt=fp32: ctx.enter_context(nc.sbuf_tensor("e2_" + name, shape, dt))
        ps = lambda name, shape: ctx.enter_context(nc.psum_tensor("e2_" + name, shape, fp32))
        taken = []
        sem = M.sems.phase("e2_", taken)
        W = F + 1
        X = [sb(f"X{u}", [P, 2 * G, W]) for u in range(2)]
        gi = [sb(f"gi{u}", [P, 2 * G], i32) for u in range(2)]
        si = [sb(f"si{u}", [P, G], i32) for u in range(2)]
        keys = sb("keys", [P, 2, G, P])
        types = sb("types", [P, 2, G, P])
        hT = sb("hT", [P, 2, P])
        same = sb("same", [P, G, P])
        onehot = sb("onehot", [P, G, P])
        is_last = [sb(f"is_last{u}", [P, G]) for u in range(2)]
        CR = [sb(f"CR{u}", [P, G, NB + F]) for u in range(2)]
        xhat = sb("xhat", [P, G, F])
        yhat = sb("yhat", [P, G, F])
        yrel = sb("yrel", [P, G, F])
        pair = sb("pair", [P, G, F])
        dot = sb("dot", [P, G])
        dot0 = sb("dot0", [P, G])
        gate = sb("gate", [P, G])
        prod = [sb(f"prod{b}", [P, NB, F]) for b in range(2)]
        msg = sb("msg", [P, G, F])
        gated = sb("gated", [P, G, F])
        loop = sb("loop", [P, G, F])
        V = sb("V", [P, G, W])
        part = [sb(f"part{u}", [P, G, W]) for u in range(2)]
        psT = ps("psT", [P, 2, P])
        psB = [ps(f"psB{b}", [P, NB, F]) for b in range(2)]
        psQ = ps("psQ", [P, 3, G, F])
        psC = ps("psC", [P, G, NB + F])
        psV = ps("psV", [P, G, W])

        staged_x, staged_s, landed, part_ready = sem("staged_x"), sem("staged_s"), sem("landed"), sem("part_ready")
        x_in = [sem(f"x_in{u}") for u in range(2)]
        keys_in = [sem(f"keys_in{u}") for u in range(2)]
        types_in = [sem(f"types_in{u}") for u in range(2)]
        keys_free, types_free, ones_ready = sem("keys_free"), sem("types_free"), sem("ones_ready")
        norm = Norm(nc, M, sb, sem, 2 * G)
        hT_psum, hT_ready = sem("hT_psum"), sem("hT_ready")
        onehot_ready, CR_psum, CR_ready = sem("onehot_ready"), sem("CR_psum"), sem("CR_ready")
        hats_ready, bases_ready, bases_used = sem("hats_ready"), sem("bases_ready"), sem("bases_used")
        dot_ready, gate_ready, V_ready, sums_ready = sem("dot_ready"), sem("gate_ready"), sem("V_ready"), sem("sums_ready")
        s_dve = sem("dve_steps")
        block = ctx.enter_context(nc.Block())

        @block.sync
        def _(sp):
            M.sems.clear(sp)
            with sp.Fori(0, NG // 2) as i:
                for u in range(2):
                    for name, buf, free, landed_ in (("type", types, types_free, types_in), ("dst", keys, keys_free, keys_in)):
                        sp.wait_ge(free, 2 * i + u + 1)
                        sp.nop(nofuse=True)
                        sp.dma_start(buf[:, u, :, :], M.keyT[name][cols(2 * i + u), :].unsqueeze(0)
                                     .to_broadcast([P, G, P])).then_inc(landed_[u], 16)

        @block.gpsimd
        def _(pool):
            gather_and_add(nc, pool, M, ("src", "dst"), "dst", M.x2, M.rel_sums, X, gi, si, part,
                           (staged_x, staged_s, x_in, norm.centred, part_ready, landed))

        @block.scalar
        def _(act):
            def copy_out(g, v):
                act.wait_ge(sums_ready, g + 1)
                wait(act, landed, 16 * G * (g - 1))
                nc.scalar.activation(part[v][:, :, :], psV[:, :, :], ACT.Copy).then_inc(part_ready, 1)

            def front(g, v):
                norm.take_root(act, g)
                act.wait_ge(CR_psum, g + 1)
                nc.scalar.activation(CR[v][:, :, :], psC[:, :, :], ACT.Copy).then_inc(CR_ready, 1)
                norm.relu(act, g)
                act.wait_ge(hT_psum, g + 1)
                nc.scalar.activation(hT[:, :, :], psT[:, :, :], ACT.Copy).then_inc(hT_ready, 1)

            def body(g, u, i):
                if live(g + 1):
                    norm.square(act, g + 1)
                if live(g - 1):
                    copy_out(g - 1, 1 - u)
                if live(g):
                    act.wait_ge(dot_ready, g + 1)
                    nc.scalar.activation(gate[:, :], dot0[:, :], ACT.Tanh, scale=float(F) ** -0.5).then_inc(gate_ready, 1)
                if live(g + 1):
                    front(g + 1, 1 - u)

            norm.square(act, 0)
            front(0, 0)
            each_group(act, body, lead=4, extra=1)

        @block.tensor
        def _(pe):
            def bases(g, j):
                wait(pe, bases_used, G * g + j - 1)
                nc.tensor.matmul(psB[j % 2][:, :, :].rearrange("p b f -> p (b f)"), hT[:, 0, :],
                                 M.WB2[:, j, :, :].rearrange("p b f -> p (b f)"),
                                 start=True, stop=True).then_inc(bases_ready, 1)

            def relation(g):
                pe.wait_ge(onehot_ready, g + 1)
                for j in range(G):
                    last = nc.tensor.matmul(psC[:, j, :], onehot[:, j, :], M.WCR[:, :], start=True, stop=True)
                last.then_inc(CR_psum, 1)

            def front(g):
                norm.transpose(pe, psT, g, hT_psum)
                pe.wait_ge(hT_ready, g + 1)
                for n, (side, w) in enumerate(((0, M.A1B), (1, M.A2B), (0, M.SLB))):
                    last = nc.tensor.matmul(psQ[:, n, :, :].rearrange("p a f -> p (a f)"), hT[:, side, :], w[:, :],
                                            start=True, stop=True)
                last.then_inc(hats_ready, 1)
                bases(g, 0)
                bases(g, 1)

            def body(g, u, i):
                bases(g, 2)
                if live(g + 1):
                    relation(g + 1)
                bases(g, 3)
                if live(g + 1):
                    front(g + 1)
                pe.wait_ge(V_ready, g + 1)
                wait(pe, part_ready, g)
                for j in range(G):
                    last = nc.tensor.matmul(psV[:, j, :], same[:, j, :], V[:, j, :], start=True, stop=True)
                last.then_inc(sums_ready, 1)

            relation(0)
            front(0)
            each_group(pe, body)

        @block.vector
        def _(dve):
            s = Steps(dve, s_dve, PER_E2)

            def begin(g, v, i):
                dve.wait_ge(x_in[v], 16 * 2 * G * (i + 1))
                s.done(nc.vector.tensor_tensor(is_last[v][:, :], X[v][:, G:2 * G, F], M.eid1[:, cols(g)], ALU.is_equal))
                norm.centre(s, X[v][:, :, 0:F])

            def relation(g, v, i):
                dve.wait_ge(types_in[v], 16 * (i + 1))
                nc.vector.tensor_scalar(onehot[:, :, :], types[:, v, :, :], M.pid[:, 0:1], None,
                                        ALU.is_equal).then_inc(onehot_ready, 1)
                dve.wait_ge(onehot_ready, g + 1)
                nc.vector.sem_inc(types_free, 1)

            def weigh(g, u, j):
                dve.wait_ge(bases_ready, G * g + j + 1)
                nc.vector.tensor_tensor(prod[j % 2][:, :, :], psB[j % 2][:, :, :], rep(CR[u][:, j, 0:NB], F),
                                        ALU.mult).then_inc(bases_used, 1)
                s.sync()
                dve.wait_ge(bases_used, G * g + j + 1)
                s.done(nc.vector.reduce_sum(msg[:, j, :], prod[j % 2][:, :, :].rearrange("p b f -> p f b"), AX.X))

            def body(g, u, i):
                n, v = (g + 1) // 2 if isinstance(g, int) else i + u, 1 - u
                dve.wait_ge(hats_ready, g + 1)
                s.done(nc.vector.tensor_tensor(xhat[:, :, :], psQ[:, 0, :, :], along(M.a1row[:, :], G), ALU.add))
                s.done(nc.vector.tensor_tensor(yhat[:, :, :], psQ[:, 1, :, :], along(M.a2row[:, :], G), ALU.add))
                s.done(nc.vector.tensor_tensor(loop[:, :, :], psQ[:, 2, :, :], rep(is_last[u][:, :], F), ALU.mult))
                if live(g + 1):
                    begin(g + 1, v, n)
                dve.wait_ge(CR_ready, g + 1)
                s.sync()
                s.done(nc.vector.tensor_tensor(yrel[:, :, :], yhat[:, :, :], CR[u][:, :, NB:NB + F], ALU.add))
                s.sync()
                s.done(nc.vector.tensor_tensor(pair[:, :, :], xhat[:, :, :], yrel[:, :, :], ALU.mult))
                if live(g + 1):
                    norm.sum_squares(dve, g + 1)
                s.sync()
                s.done(nc.vector.reduce_sum(dot[:, :], pair[:, :, :], AX.X))
                weigh(g, u, 0)
                nc.vector.tensor_scalar(dot0[:, :], dot[:, :], 0.0, None, ALU.max).then_inc(dot_ready, 1)
                if live(g + 1):
                    relation(g + 1, v, n)
                    norm.scale(dve, s, g + 1)
                weigh(g, u, 1)
                weigh(g, u, 2)
                dve.wait_ge(keys_in[u], 16 * (i + 1))
                wait(dve, sums_ready, g)
                nc.vector.tensor_tensor(same[:, :, :], keys[:, u, :, :], rep(M.key["dst"][:, cols(g)], P),
                                        ALU.is_equal).then_inc(keys_free, 1)
                weigh(g, u, 3)
                dve.wait_ge(gate_ready, g + 1)
                s.sync()
                s.done(nc.vector.tensor_tensor(gated[:, :, :], msg[:, :, :], rep(gate[:, :], F), ALU.mult))
                s.sync()
                nc.vector.tensor_tensor(V[:, :, 0:F], gated[:, :, :], loop[:, :, :], ALU.add).then_inc(V_ready, 1)
                dve.wait_ge(V_ready, g + 1)

            nc.vector.memset(V[:, :, :], 1.0).then_inc(ones_ready, 1)
            dve.wait_ge(ones_ready, 1)
            nc.vector.sem_inc(keys_free, 2)
            nc.vector.sem_inc(types_free, 2)
            begin(0, 0, 0)
            norm.sum_squares(dve, 0)
            relation(0, 0, 0)
            norm.scale(dve, s, 0)
            each_group(dve, body, s)


def dense2(nc, t, M, early):
    with ExitStack() as ctx:
        sb = lambda name, shape, dt=fp32: ctx.enter_context(nc.sbuf_tensor("d2_" + name, shape, dt))
        ps = lambda name, shape: ctx.enter_context(nc.psum_tensor("d2_" + name, shape, fp32))
        taken = []
        sem = M.sems.phase("d2_", taken)
        W = F + 1
        X = [sb(f"X{u}", [P, K, W]) for u in range(2)]
        S = [sb(f"S{u}", [P, K, W]) for u in range(2)]
        Y = [sb(f"Y{u}", [P, K, F]) for u in range(2)]
        Z = [sb(f"Z{u}", [P, K, W]) for u in range(2)]
        hT = [sb(f"hT{q}", [P, G, P]) for q in range(2)]
        droot = sb("droot", [P, K])
        psT = [ps(f"psT{q}", [P, G, P]) for q in range(2)]
        psR = [ps(f"psR{q}", [P, G * P]) for q in range(3)]
        loaded = [sem(f"loaded{u}") for u in range(2)]
        stored = sem("stored")
        norm = Norm(nc, M, sb, sem, K)
        h = [norm.h, sb("h1", [P, K, F])]
        hT_psum, hT_ready, round_ready = sem("hT_psum"), sem("hT_ready"), sem("round_ready")
        degree_root, x3_ready, done, s_dve = sem("degree_root"), sem("x3_ready"), sem("done"), sem("dve_steps")
        proj_sems = norm.h_ready, hT_psum, hT_ready, round_ready, done
        block = ctx.enter_context(nc.Block())
        stores = 1 if early else 2

        @block.sync
        def _(sp):
            M.sems.clear(sp)
            def load(c, u):
                sp.dma_start(X[u][:, :, :], chunk(M.x2, c)).then_inc(loaded[u], 16)
                sp.dma_start(S[u][:, :, :], chunk(M.rel_sums, c)).then_inc(loaded[u], 16)

            def refill(c, u):
                sp.wait_ge(norm.centred, c + 1)
                sp.wait_ge(degree_root, c + 1)
                sp.nop(nofuse=True)
                load(c + 2, u)

            def body(c, u, i):
                if not isinstance(c, int) or c + 3 < NCH:
                    refill(c + 1, 1 - u)
                sp.wait_ge(done, c + 1)
                sp.nop(nofuse=True)
                wait(sp, stored, 16 * stores * c)
                sp.nop(nofuse=True)
                if early:
                    sp.dma_start(chunk(early, c), Y[u][:, :, :]).then_inc(stored, 16)
                else:
                    sp.dma_start(chunk(M.x3, c), Y[u][:, :, :]).then_inc(stored, 16)
                    sp.dma_start(chunk(M.hs, c), Z[u][:, :, :]).then_inc(stored, 16)

            load(0, 0)
            load(1, 1)
            refill(0, 0)
            each_chunk(sp, body)
            sp.wait_ge(stored, 16 * stores * NCH)

        @block.scalar
        def _(act):
            def root_of_degree(c, u, i):
                act.wait_ge(loaded[u], 32 * (i + 1))
                wait(act, norm.summed, c)
                nc.scalar.activation(droot[:, :], S[u][:, :, F], ACT.Sqrt, bias=M.ones[:, 0:1]).then_inc(degree_root, 1)

            def body(c, u, i):
                n, v, k = after(c, u, i)
                if live_chunk(n):
                    root_of_degree(n, v, k)
                    norm.square(act, n)
                project_scalar(nc, act, psT, hT, proj_sems, c, u, 0)
                if live_chunk(n):
                    norm.take_root(act, n)
                project_scalar(nc, act, psT, hT, proj_sems, c, u, 1)
                project_scalar(nc, act, psT, hT, proj_sems, c, u, 2)
                if live_chunk(n):
                    norm.relu(act, n, h[v])

            root_of_degree(0, 0, 0)
            norm.square(act, 0)
            norm.take_root(act, 0)
            norm.relu(act, 0)
            each_chunk(act, body)

        @block.tensor
        def _(pe):
            each_chunk(pe, lambda c, u, i: project_pe(nc, pe, M, M.W3B, h[u], psT, hT, psR, proj_sems, c, u))

        @block.vector
        def _(dve):
            s = Steps(dve, s_dve, PER_D2)

            def begin(c, u, i):
                dve.wait_ge(loaded[u], 32 * (i + 1))
                wait(dve, norm.scaled, c)
                wait(dve, stored, 16 * stores * (c - 1))
                s.done(nc.vector.scalar_tensor_tensor(Y[u][:, :, :], S[u][:, :, 0:F], 0.0, X[u][:, :, 0:F], ALU.max, ALU.add))
                s.sync()
                norm.centre(s, Y[u][:, :, :])
                dve.wait_ge(degree_root, c + 1)
                s.done(nc.vector.reciprocal(Z[u][:, :, F], droot[:, :]))
                s.sync()
                norm.sum_squares(dve, c)

            def body(c, u, i):
                n, v, k = after(c, u, i)
                if live_chunk(n):
                    begin(n, v, k)
                    norm.scale(dve, s, n)
                dve.wait_ge(round_ready, 3 * c + 3)
                m = G * G
                for q in range(3):
                    last = nc.vector.tensor_tensor(Z[u][:, m * q:m * q + m, 0:F],
                                                   psR[q][:, :].rearrange("p (k f) -> p k f", f=F),
                                                   rep(Z[u][:, m * q:m * q + m, F], F), ALU.mult)
                last.then_inc(done, 1)

            begin(0, 0, 0)
            norm.scale(dve, s, 0)
            each_chunk(dve, body, s)
    M.sems.retire(taken)


def conv_edges(nc, t, M):
    with ExitStack() as ctx:
        sb = lambda name, shape, dt=fp32: ctx.enter_context(nc.sbuf_tensor("e3_" + name, shape, dt))
        taken = []
        sem = M.sems.phase("e3_", taken)
        X = [sb(f"X{u}", [P, G, F + 1]) for u in range(2)]
        gi = [sb(f"gi{u}", [P, G], i32) for u in range(2)]
        si = [sb(f"si{u}", [P, G], i32) for u in range(2)]
        keys = sb("keys", [P, 2, G, P])
        same = [sb(f"same{u}", [P, G, P]) for u in range(2)]
        part = [sb(f"part{u}", [P, G, F]) for u in range(2)]
        psV = [ctx.enter_context(nc.psum_tensor(f"e3_psV{u}", [P, G, F], fp32)) for u in range(2)]
        staged_x, staged_s, landed, part_ready = sem("staged_x"), sem("staged_s"), sem("landed"), sem("part_ready")
        x_in = [sem(f"x_in{u}") for u in range(2)]
        keys_in = [sem(f"keys_in{u}") for u in range(2)]
        same_ready, sums_ready, keys_free = sem("same_ready"), sem("sums_ready"), sem("keys_free")
        block = ctx.enter_context(nc.Block())

        @block.sync
        def _(sp):
            M.sems.clear(sp)
            spread_keys(sp, M, "dst", keys, keys_free, keys_in)

        @block.gpsimd
        def _(pool):
            gather_and_add(nc, pool, M, ("src",), "dst", M.hs, M.conv_sums, X, gi, si, part,
                           (staged_x, staged_s, x_in, sums_ready, part_ready, landed))

        @block.scalar
        def _(act):
            def edges(g, u, i):
                act.wait_ge(sums_ready, g + 1)
                wait(act, landed, 16 * G * (g - 1))
                nc.scalar.activation(part[u][:, :, :], psV[u][:, :, :], ACT.Copy).then_inc(part_ready, 1)

            each_group(act, edges)

        @block.tensor
        def _(pe):
            def edges(g, u, i):
                pe.wait_ge(x_in[u], 16 * G * (i + 1))
                pe.wait_ge(same_ready, g + 1)
                wait(pe, part_ready, g - 1)
                for j in range(G):
                    last = nc.tensor.matmul(psV[u][:, j, :], same[u][:, j, :], X[u][:, j, 0:F], start=True, stop=True)
                last.then_inc(sums_ready, 1)

            each_group(pe, edges)

        @block.vector
        def _(dve):
            def edges(g, u, i):
                dve.wait_ge(keys_in[u], 16 * (i + 1))
                wait(dve, sums_ready, g - 1)
                nc.vector.tensor_tensor(same[u][:, :, :], keys[:, u, :, :], rep(M.key["dst"][:, cols(g)], P),
                                        ALU.is_equal).then_inc(same_ready, 1)
                dve.wait_ge(same_ready, g + 1)
                nc.vector.sem_inc(keys_free, 1)

            nc.vector.sem_inc(keys_free, 2)
            each_group(dve, edges)


def dense3(nc, t, M):
    with ExitStack() as ctx:
        sb = lambda name, shape, dt=fp32: ctx.enter_context(nc.sbuf_tensor("d3_" + name, shape, dt))
        taken = []
        sem = M.sems.phase("d3_", taken)
        Z = [sb(f"Z{u}", [P, K, F + 1]) for u in range(2)]
        S = [sb(f"S{u}", [P, K, F]) for u in range(2)]
        Y = [sb(f"Y{u}", [P, K, F]) for u in range(2)]
        both = sb("both", [P, K, F])
        scaled = sb("scaled", [P, K, F])
        biased = sb("biased", [P, K, F])
        loaded = [sem(f"loaded{u}") for u in range(2)]
        stored, biased_ready, done, s_dve = sem("stored"), sem("biased_ready"), sem("done"), sem("dve_steps")
        block = ctx.enter_context(nc.Block())

        @block.sync
        def _(sp):
            M.sems.clear(sp)
            def load(c, u):
                sp.dma_start(Z[u][:, :, :], chunk(M.hs, c)).then_inc(loaded[u], 16)
                sp.dma_start(S[u][:, :, :], chunk(M.conv_sums, c)).then_inc(loaded[u], 16)

            def body(c, u, i):
                sp.wait_ge(done, c + 1)
                sp.nop(nofuse=True)
                wait(sp, stored, 16 * c)
                sp.nop(nofuse=True)
                sp.dma_start(chunk(M.conv, c), Y[u][:, :, :]).then_inc(stored, 16)
                if not isinstance(c, int) or c + 2 < NCH:
                    load(c + 2, u)

            load(0, 0)
            load(1, 1)
            each_chunk(sp, body)
            sp.wait_ge(stored, 16 * NCH)

        @block.scalar
        def _(act):
            def body(c, u, i):
                act.wait_ge(biased_ready, c + 1)
                wait(act, stored, 16 * (c - 1))
                nc.scalar.activation(Y[u][:, :, :], biased[:, :, :], ACT.Relu).then_inc(done, 1)

            each_chunk(act, body)

        @block.vector
        def _(dve):
            s = Steps(dve, s_dve, PER_D3)

            def body(c, u, i):
                dve.wait_ge(loaded[u], 32 * (i + 1))
                s.done(nc.vector.tensor_tensor(both[:, :, :], Z[u][:, :, 0:F], S[u][:, :, :], ALU.add))
                s.sync()
                s.done(nc.vector.tensor_tensor(scaled[:, :, :], both[:, :, :], rep(Z[u][:, :, F], F), ALU.mult))
                s.sync()
                wait(dve, done, c)
                nc.vector.tensor_tensor(biased[:, :, :], scaled[:, :, :], along(M.b3row[:, :], K),
                                        ALU.add).then_inc(biased_ready, 1)
                dve.wait_ge(biased_ready, c + 1)

            each_chunk(dve, body, s)
    M.sems.retire(taken)


def square_edges(nc, t, M):
    with ExitStack() as ctx:
        sb = lambda name, shape, dt=fp32: ctx.enter_context(nc.sbuf_tensor("e4_" + name, shape, dt))
        taken = []
        sem = M.sems.phase("e4_", taken)
        W = F + 1
        X = [sb(f"X{u}", [P, 2 * G, F]) for u in range(2)]
        gi = [sb(f"gi{u}", [P, 2 * G], i32) for u in range(2)]
        si = [sb(f"si{u}", [P, G], i32) for u in range(2)]
        keys = sb("keys", [P, 2, G, P])
        same = [sb(f"same{u}", [P, G, P]) for u in range(2)]
        diff = [sb(f"diff{u}", [P, G, F]) for u in range(2)]
        V = [sb(f"V{u}", [P, G, W]) for u in range(2)]
        part = [sb(f"part{u}", [P, G, W]) for u in range(2)]
        psV = [ctx.enter_context(nc.psum_tensor(f"e4_psV{u}", [P, G, W], fp32)) for u in range(2)]
        staged_x, staged_s, landed, part_ready = sem("staged_x"), sem("staged_s"), sem("landed"), sem("part_ready")
        x_in = [sem(f"x_in{u}") for u in range(2)]
        keys_in = [sem(f"keys_in{u}") for u in range(2)]
        diff_ready, V_ready, sums_ready, keys_free = sem("diff_ready"), sem("V_ready"), sem("sums_ready"), sem("keys_free")
        ones_ready = sem("ones_ready")
        block = ctx.enter_context(nc.Block())

        @block.sync
        def _(sp):
            M.sems.clear(sp)
            spread_keys(sp, M, "src", keys, keys_free, keys_in)

        @block.gpsimd
        def _(pool):
            gather_and_add(nc, pool, M, ("src", "dst"), "src", M.conv, M.square_sums, X, gi, si, part,
                           (staged_x, staged_s, x_in, diff_ready, part_ready, landed))

        @block.scalar
        def _(act):
            def edges(g, u, i):
                act.wait_ge(diff_ready, g + 1)
                wait(act, sums_ready, g - 1)
                nc.scalar.activation(V[u][:, :, 0:F], diff[u][:, :, :], ACT.Square).then_inc(V_ready, 1)
                act.wait_ge(sums_ready, g + 1)
                wait(act, landed, 16 * G * (g - 1))
                nc.scalar.activation(part[u][:, :, :], psV[u][:, :, :], ACT.Copy).then_inc(part_ready, 1)

            act.wait_ge(ones_ready, 1)
            each_group(act, edges)

        @block.tensor
        def _(pe):
            def edges(g, u, i):
                pe.wait_ge(V_ready, g + 1)
                pe.wait_ge(keys_free, g + 3)
                wait(pe, part_ready, g - 1)
                for j in range(G):
                    last = nc.tensor.matmul(psV[u][:, j, :], same[u][:, j, :], V[u][:, j, :], start=True, stop=True)
                last.then_inc(sums_ready, 1)

            each_group(pe, edges)

        @block.vector
        def _(dve):
            def edges(g, u, i):
                dve.wait_ge(x_in[u], 16 * 2 * G * (i + 1))
                wait(dve, V_ready, g - 1)
                nc.vector.tensor_tensor(diff[u][:, :, :], X[u][:, 0:G, :], X[u][:, G:2 * G, :],
                                        ALU.subtract).then_inc(diff_ready, 1)
                dve.wait_ge(keys_in[u], 16 * (i + 1))
                wait(dve, sums_ready, g - 1)
                nc.vector.tensor_tensor(same[u][:, :, :], keys[:, u, :, :], rep(M.key["src"][:, cols(g)], P),
                                        ALU.is_equal).then_inc(keys_free, 1)

            for u in range(2):
                last = nc.vector.memset(V[u][:, :, :], 1.0)
            last.then_inc(ones_ready, 1)
            nc.vector.sem_inc(keys_free, 2)
            each_group(dve, edges)


def dense4(nc, t, M, out):
    with ExitStack() as ctx:
        sb = lambda name, shape, dt=fp32: ctx.enter_context(nc.sbuf_tensor("d4_" + name, shape, dt))
        taken = []
        sem = M.sems.phase("d4_", taken)
        X = [sb(f"X{u}", [P, K, F]) for u in range(2)]
        S = [sb(f"S{u}", [P, K, F + 1]) for u in range(2)]
        Y = [sb(f"Y{u}", [P, K, F]) for u in range(2)]
        count = sb("count", [P, K])
        share = sb("share", [P, K])
        mean = [sb(f"mean{u}", [P, K, F]) for u in range(2)]
        curve = [sb(f"curve{u}", [P, K, F]) for u in range(2)]
        loaded = [sem(f"loaded{u}") for u in range(2)]
        stored, mean_ready, curve_ready, done, s_dve = sem("stored"), sem("mean_ready"), sem("curve_ready"), sem("done"), sem("dve_steps")
        block = ctx.enter_context(nc.Block())

        @block.sync
        def _(sp):
            M.sems.clear(sp)
            def load(c, u):
                sp.dma_start(X[u][:, :, :], chunk(M.x3, c)).then_inc(loaded[u], 16)
                sp.dma_start(S[u][:, :, :], chunk(M.square_sums, c)).then_inc(loaded[u], 16)

            def body(c, u, i):
                sp.wait_ge(done, c + 1)
                sp.nop(nofuse=True)
                wait(sp, stored, 16 * c)
                sp.nop(nofuse=True)
                sp.dma_start(chunk(out, c), Y[u][:, :, :]).then_inc(stored, 16)
                if not isinstance(c, int) or c + 2 < NCH:
                    load(c + 2, u)

            load(0, 0)
            load(1, 1)
            each_chunk(sp, body)
            sp.wait_ge(stored, 16 * NCH)

        @block.gpsimd
        def _(pool):
            def body(c, u, i):
                pool.wait_ge(curve_ready, c + 1)
                wait(pool, stored, 16 * (c - 1))
                nc.gpsimd.tensor_tensor(Y[u][:, :, :], X[u][:, :, :], curve[u][:, :, :], ALU.add).then_inc(done, 1)

            each_chunk(pool, body)

        @block.scalar
        def _(act):
            def body(c, u, i):
                act.wait_ge(mean_ready, c + 1)
                wait(act, done, c - 1)
                nc.scalar.activation(curve[u][:, :, :], mean[u][:, :, :], ACT.Tanh).then_inc(curve_ready, 1)

            each_chunk(act, body)

        @block.vector
        def _(dve):
            s = Steps(dve, s_dve, PER_D4)

            def body(c, u, i):
                dve.wait_ge(loaded[u], 32 * (i + 1))
                wait(dve, mean_ready, c)
                s.done(nc.vector.tensor_scalar(count[:, :], S[u][:, :, F], 1.0, None, ALU.max))
                s.sync()
                s.done(nc.vector.reciprocal(share[:, :], count[:, :]))
                s.sync()
                wait(dve, curve_ready, c - 1)
                nc.vector.tensor_tensor(mean[u][:, :, :], S[u][:, :, 0:F], rep(share[:, :], F),
                                        ALU.mult).then_inc(mean_ready, 1)

            each_chunk(dve, body, s)
    M.sems.retire(taken)


def gnn_program(nc, t, out, stage=9):
    with ExitStack() as ctx:
        ctx.enter_context(nc.allow_non_contiguous_dma(reason="small tables, once"))
        M = Memory(nc, ctx)
        setup(nc, t, M)
        layer0_edges(nc, t, M)
        dense0(nc, t, M, out if stage == 1 else M.x1)
        if stage == 1:
            return
        layer1_edges(nc, t, M)
        more_maxima(nc, M)
        dense1(nc, t, M, stage == 2 and out)
        if stage == 2:
            return
        layer2_edges(nc, t, M)
        dense2(nc, t, M, stage == 3 and out)
        if stage == 3:
            return
        conv_edges(nc, t, M)
        dense3(nc, t, M)
        square_edges(nc, t, M)
        dense4(nc, t, M, out)


_INS = ['x', 'src', 'dst', 'edge_attr_2', 'edge_attr_32', 'edge_type_86', 'L0_gnn_weight', 'L0_gnn_root_weight',
        'L0_gnn_att_weight', 'L0_gnn_bias', 'L1_gnn_W1', 'L1_gnn_b1', 'L1_gnn_W2', 'L1_gnn_b2', 'L2_gnn_weight',
        'L2_gnn_w_comp', 'L2_gnn_self_loop_weight', 'L2_gnn_A1_w', 'L2_gnn_A1_b', 'L2_gnn_A2_w', 'L2_gnn_A2_b',
        'L2_gnn_rel_emb', 'L3_gnn_W', 'L3_gnn_b']


def kernel(**inputs):
    import numpy as _np
    import concourse.bacc as _bacc
    from concourse import mybir as _mybir
    from concourse.bass_utils import run_bass_kernel_spmd as _run

    nc = _bacc.Bacc("TRN2", target_bir_lowering=False, num_devices=1)
    arrays, tensors = {}, {}
    for name in _INS:
        a = _np.ascontiguousarray(inputs[name])
        arrays[f"in_{name}_dram"] = a
        tensors[name] = nc.dram_tensor(f"in_{name}_dram", a.shape, _mybir.dt.from_np(a.dtype),
                                       kind="ExternalInput").ap()
    out = nc.dram_tensor("out_0_dram", (N, F), fp32, kind="ExternalOutput").ap()
    gnn_program(nc, tensors, out)
    r = _run(nc, [arrays], core_ids=[0])
    return r.results[0]["out_0_dram"]
```

```python
import concourse.bass as bass
from concourse import mybir
from contextlib import ExitStack

fp32 = mybir.dt.float32
i32 = mybir.dt.int32
ALU = mybir.AluOpType
ACT = mybir.ActivationFunctionType
AX = mybir.AxisListType

P = 128
N = 100000
F = 32
E = 25000
ROWS_E = 125
T = E // ROWS_E
G = 4
NG = T // G
PAD_KEY = 200000
CR = 16
NT = NG * P * CR
EPS = 1e-5
BIG = 1e30
SLOPE = 0.2
KS = 5
TAPS = KS * KS
TC = 15
HID = 64
NB = 16
REL = 86
K = 48
NCH = 17
STRIDE = (N - P * K) // (NCH - 1)
LN_EPS = EPS * F * F * F
LN_GAIN = float(F) ** 0.5


LAG0 = 2
PER_E0 = 26
PER_D0 = 11
PER_E1 = 4
PER_R1 = 5
PER_D1 = 3
PER_E2 = 14
PER_D2 = 5
PER_D3 = 2
PER_D4 = 2


class Steps:

    def __init__(self, eng, sem, per=0):
        self.eng, self.sem, self.per = eng, sem, per
        self.base, self.n = 0, 0

    def done(self, ins):
        ins.then_inc(self.sem, 1)
        self.n += 1

    def sync(self):
        self.eng.wait_ge(self.sem, self.base + self.n)

    def enter(self, first, turn):
        self.base, self.n = first + turn * self.per, 0

    def leave(self):
        assert self.n == self.per, self.n

    def resume(self, n):
        self.base, self.n = 0, n


def wait(eng, sem, value):
    if not (isinstance(value, int) and value <= 0):
        eng.wait_ge(sem, value)


def rep(ap, n):
    return ap.unsqueeze(2).to_broadcast([ap.shape[0], ap.shape[1], n])


def along(ap, n):
    return ap.unsqueeze(1).to_broadcast([ap.shape[0], n, ap.shape[1]])


def cols(g):
    return slice(G * g, G * g + G) if isinstance(g, int) else bass.ds(G * g, G)


def each_group(eng, body, steps=None, lead=2, extra=0):
    for g in range(lead):
        body(g, g % 2, g // 2)
    first, turns = steps.n if steps else 0, NG - 2 - lead
    with eng.Fori(0, turns // 2) as i:
        for u in range(2):
            if steps:
                steps.enter(first, 2 * i + u)
            body(2 * i + lead + u, u, i + lead // 2)
            if steps:
                steps.leave()
    if steps:
        steps.resume(first + turns * steps.per)
    for g in range(NG - 2, NG + extra):
        body(g, g % 2, g // 2)


def live(g):
    return not isinstance(g, int) or 0 <= g < NG


def each_chunk(eng, body, steps=None):
    lead = 2
    for c in range(lead):
        body(c, c % 2, c // 2)
    first, turns = steps.n if steps else 0, NCH - 3 - lead
    with eng.Fori(0, turns // 2) as i:
        for u in range(2):
            if steps:
                steps.enter(first, 2 * i + u)
            body(2 * i + lead + u, u, i + lead // 2)
            if steps:
                steps.leave()
    if steps:
        steps.resume(first + turns * steps.per)
    for c in range(NCH - 3, NCH):
        body(c, c % 2, c // 2)


def each_chunk_of_three(eng, body, steps=None):
    lead = 2
    for c in range(lead):
        body(c, c % 3, c // 3)
    first, turns = steps.n if steps else 0, NCH - 3 - lead
    with eng.Fori(0, turns // 3) as i:
        for u in range(3):
            if steps:
                steps.enter(first, 3 * i + u)
            body(3 * i + lead + u, (lead + u) % 3, i + (lead + u) // 3)
            if steps:
                steps.leave()
    if steps:
        steps.resume(first + turns * steps.per)
    for c in range(NCH - 3, NCH):
        body(c, c % 3, c // 3)


def chunk(table, c):
    lo = c * STRIDE
    rows = table[lo:lo + P * K, :] if isinstance(c, int) else table[bass.ds(lo, P * K), :]
    return rows.rearrange("(p k) f -> p k f", p=P)


class Semaphores:

    def __init__(self, nc, ctx):
        self.nc, self.ctx = nc, ctx
        self.free, self.resting, self.retired = [], [], []

    def phase(self, prefix, taken):
        self.free, self.resting = self.free + self.resting, []

        def sem(name):
            taken.append(self.free.pop() if self.free else self.ctx.enter_context(self.nc.semaphore(prefix + name)))
            return taken[-1]
        return sem

    def retire(self, taken):
        self.retired += taken

    def clear(self, sp):
        for s in self.retired:
            sp.sem_clear(s)
        self.resting, self.retired = self.resting + self.retired, []


class Memory:

    def __init__(self, nc, ctx):
        def sb(name, shape, dt=fp32):
            return ctx.enter_context(nc.sbuf_tensor(name, shape, dt))

        def table(name, shape, dt=fp32):
            return nc.dram_tensor(name, shape, dt).ap()

        self.sems = Semaphores(nc, ctx)
        self.keyT = {k: table("keyT_" + k, [T, P]) for k in ("src", "dst", "type")}
        self.softmax_state = [table(f"softmax_state{k}", [NT, F + 2]) for k in range(2)]
        self.max_state = [table(f"max_state{k}", [NT, F + 1]) for k in range(2)]
        self.rel_sums = table("rel_sums", [NT, F + 1])
        self.conv_sums = table("conv_sums", [NT, F])
        self.square_sums = table("square_sums", [NT, F + 1])
        self.x1 = table("x1", [N, F])
        self.x2 = table("x2", [N, F + 1])
        self.x3 = table("x3", [N, F])
        self.hs = table("hs", [N, F + 1])
        self.conv = table("conv", [N, F])

        self.ident = sb("ident", [P, P])
        self.lower = sb("lower", [P, P])
        self.ones = sb("ones", [P, P])
        self.zeros = sb("zeros", [P, CR * (F + 2)])
        self.pid = sb("pid", [P, 1])
        self.waste = sb("waste", [P, 1])
        self.waste_odd = sb("waste_odd", [P, 1])
        self.ln_eps = sb("ln_eps", [P, 1])
        self.eid1 = sb("eid1", [P, T])
        self.gidx = {k: sb("gidx_" + k, [P, T], i32) for k in ("src", "dst")}
        self.key = {k: sb("key_" + k, [P, T]) for k in ("src", "dst", "type")}
        self.rank = {k: sb("rank_" + k, [P, T]) for k in ("src", "dst")}
        self.sidx = {k: sb("sidx_" + k, [P, T], i32) for k in ("src", "dst")}
        self.before = {k: sb("before_" + k, [P, T]) for k in ("src", "dst")}
        self.pidx = {k: sb("pidx_" + k, [P, T], i32) for k in ("src", "dst")}
        self.rounds = sb("rounds", [1, 1], i32)
        kept = sb("kept", [P, T * (F + 1)])
        self.C = kept[:, 0:T * TAPS].rearrange("p (t k) -> p t k", k=TAPS)
        self.V1 = kept[:, :].rearrange("p (t f) -> p t f", f=F + 1)
        self.WB = sb("WB", [P, G, TAPS, F + 1])
        self.RA = sb("RA", [P, G])
        self.ROOT = sb("ROOT", [P, P])
        self.bias0 = sb("bias0", [P, F])
        self.W1S = sb("W1S", [P, 2, P])
        self.W1D = sb("W1D", [P, 2, P])
        self.W1E = sb("W1E", [P, 2, P])
        self.b1col = sb("b1col", [P, 1])
        self.W2B = sb("W2B", [P, 2 * F])
        self.b2row = sb("b2row", [P, F])
        self.WB2 = sb("WB2", [P, G, NB, F])
        self.A1B = sb("A1B", [P, P])
        self.A2B = sb("A2B", [P, P])
        self.SLB = sb("SLB", [P, P])
        self.WCR = sb("WCR", [P, NB + F])
        self.a1row = sb("a1row", [P, F])
        self.a2row = sb("a2row", [P, F])
        self.W3B = sb("W3B", [P, P])
        self.b3row = sb("b3row", [P, F])


def setup(nc, t, M):
    with ExitStack() as ctx:
        sb = lambda name, shape, dt=fp32: ctx.enter_context(nc.sbuf_tensor(name, shape, dt))
        taken = []
        sem = M.sems.phase("set_", taken)
        keyI = {k: sb("keyI_" + k, [P, T], i32) for k in ("src", "dst", "type")}
        kT = sb("kT", [T // 2, 3, 2, P])
        slots = 5
        column = [sb(f"column{u}", [P, G]) for u in range(slots)]
        attr = sb("attr", [P, T, 2])
        dist = sb("dist", [P, T, 2])
        hat = sb("hat", [P, T, 2, KS])
        fall = sb("fall", [P, T, 2, KS])
        rise = sb("rise", [P, T, 2, KS])
        taps0 = sb("taps0", [P, TAPS, F])
        rootw = sb("rootw", [P, F])
        att = sb("att", [P, 2, F])
        watt = sb("watt", [P, TAPS, F])
        wattk = sb("wattk", [P, TAPS])
        rattf = sb("rattf", [P, F])
        ratt = sb("ratt", [P, 1])
        a12 = sb("a12", [F, 2, G, F])
        same = [sb(f"same{u}", [P, G, P]) for u in range(slots)]
        again = sb("again", [P, T])
        pad = sb("pad", [P, T])
        gap = sb("gap", [P, T])
        rmax = sb("rmax", [P, 1])
        rmax1 = sb("rmax1", [1, 1])
        psK = [ctx.enter_context(nc.psum_tensor(f"psK{h}", [P, 3, P], fp32)) for h in range(2)]
        psB = [ctx.enter_context(nc.psum_tensor(f"psB{u}", [P, G, P], fp32)) for u in range(slots)]
        psW = ctx.enter_context(nc.psum_tensor("psW", [P, P], fp32))
        s_zero = sem("zeroed")
        s_fill = sem("filled")
        s_sel = sem("masks")
        s_idx = sem("indices")
        s_attr = sem("attr")
        s_w = sem("weights")
        s_wz = sem("weights_cleared")
        s_kf = sem("keys_float")
        s_kp = sem("keys_transposed")
        s_kc = sem("keys_copied")
        s_kt = sem("keys_stored")
        s_col = sem("columns_ready")
        s_row = sem("rows_ready")
        s_used = sem("rows_used")
        s_mr = sem("rank_max")
        s_mp = sem("rank_row")
        s_dve = sem("dve_steps")
        block = ctx.enter_context(nc.Block())
        half = T // 2
        n_weights = [0]

        @block.sync
        def _(sp):
            sp.wait_ge(s_fill, 1)
            view = lambda a: a.rearrange("(p t) -> p t", p=ROWS_E)
            for k in ("src", "dst"):
                sp.dma_start(M.gidx[k][0:ROWS_E, 0:T], view(t[k])).then_inc(s_idx, 16)
                sp.dma_start(keyI[k][0:ROWS_E, :], view(t[k])).then_inc(s_idx, 16)
            sp.dma_start(keyI["type"][0:ROWS_E, :], view(t["edge_type_86"])).then_inc(s_idx, 16)
            sp.dma_start(attr[0:ROWS_E, :, :],
                         t["edge_attr_2"].rearrange("(p t) d -> p t d", p=ROWS_E)).then_inc(s_attr, 16)

            sp.wait_ge(s_wz, 1)
            w0 = t["L0_gnn_weight"].rearrange("k f o -> f k o")
            w2 = t["L2_gnn_weight"].rearrange("b i o -> i b o")
            root = t["L0_gnn_root_weight"]
            w1 = t["L1_gnn_W1"]
            row = lambda a: a.rearrange("(a f) -> a f", a=1).to_broadcast([P, F])

            def load(dst, src):
                sp.dma_start(dst, src).then_inc(s_w, 16)
                n_weights[0] += 1

            for i in range(G):
                b = slice(F * i, F * i + F)
                load(taps0[b, :, :], w0)
                load(rootw[b, :], root)
                load(M.ROOT[b, b], root)
                load(M.WB2[b, i, :, :], w2)
                load(M.SLB[b, b], t["L2_gnn_self_loop_weight"])
                load(M.W3B[b, b], t["L3_gnn_W"])
                j, c = i // 2, slice(HID * (i % 2), HID * (i % 2) + HID)
                load(M.W1S[b, j, c], w1[0:F, :])
                load(M.W1D[b, j, c], w1[F:2 * F, :])
                load(M.W1E[b, j, c], w1[2 * F:3 * F, :])
                for n, a in enumerate((t["L2_gnn_A1_w"], t["L2_gnn_A2_w"])):
                    load(a12[:, n, i, :], a)
            for i in range(2):
                b = slice(HID * i, HID * i + HID)
                load(M.b1col[b, :], t["L1_gnn_b1"].rearrange("(f a) -> f a", a=1))
                load(M.W2B[b, F * i:F * i + F], t["L1_gnn_W2"])
                load(att[:, i, :], row(t["L0_gnn_att_weight"][F * i:F * i + F]))
            load(M.bias0[:, :], row(t["L0_gnn_bias"]))
            load(M.b2row[:, :], row(t["L1_gnn_b2"]))
            load(M.a1row[:, :], row(t["L2_gnn_A1_b"]))
            load(M.a2row[:, :], row(t["L2_gnn_A2_b"]))
            load(M.b3row[:, :], row(t["L3_gnn_b"]))
            load(M.WCR[0:REL, 0:NB], t["L2_gnn_w_comp"])
            load(M.WCR[0:REL, NB:NB + F], t["L2_gnn_rel_emb"])
            sp.wait_ge(s_kc, 2)
            for n, k in enumerate(("src", "dst", "type")):
                sp.dma_start(M.keyT[k].rearrange("(h a) p -> a h p", h=2), kT[:, n, :, :]).then_inc(s_kt, 16)
            for tab in M.softmax_state:
                w = tab.shape[1]
                sp.dma_start(tab.rearrange("(p a r) w -> p a (r w)", p=P, a=NT // P // CR),
                             along(M.zeros[:, 0:CR * w], NT // P // CR)).then_inc(s_zero, 16)
            sp.wait_ge(s_kt, 48)
            sp.wait_ge(s_w, 16 * n_weights[0])
            sp.wait_ge(s_zero, 32)

        @block.scalar
        def _(act):
            act.wait_ge(s_kf, 1)
            for n, k in enumerate(("src", "dst")):
                with act.Fori(0, NG // slots) as i:
                    for u in range(slots):
                        r = n * NG + slots * i + u
                        act.wait_ge(s_row, r + 1)
                        nc.scalar.activation(column[u][:, :], M.key[k][:, cols(slots * i + u)],
                                             ACT.Copy).then_inc(s_col, 1)

        @block.gpsimd
        def _(pool):
            nc.gpsimd.memset(M.zeros[:, :], 0.0)
            for k in ("src", "dst"):
                nc.gpsimd.memset(M.gidx[k][:, :], 0)
                nc.gpsimd.memset(keyI[k][:, :], PAD_KEY)
            nc.gpsimd.memset(attr[:, :, :], 0.0)
            nc.gpsimd.memset(keyI["type"][:, :], 0).then_inc(s_fill, 1)
            nc.gpsimd.memset(M.ident[:, :], 0.0).then_inc(s_sel, 1)
            nc.gpsimd.memset(M.lower[:, :], 1.0).then_inc(s_sel, 1)
            nc.gpsimd.memset(M.ones[:, :], 1.0)
            nc.gpsimd.memset(M.ln_eps[:, :], LN_EPS)
            nc.gpsimd.iota(M.pid[:, :], [[0, 1]], base=0, channel_multiplier=1,
                           allow_small_or_imprecise_dtypes=True)
            nc.gpsimd.iota(M.waste[:, :], [[0, 1]], base=N, channel_multiplier=1,
                           allow_small_or_imprecise_dtypes=True)
            nc.gpsimd.iota(M.waste_odd[:, :], [[0, 1]], base=N + P, channel_multiplier=1,
                           allow_small_or_imprecise_dtypes=True)
            nc.gpsimd.iota(M.eid1[:, :], [[1, T]], base=1, channel_multiplier=T,
                           allow_small_or_imprecise_dtypes=True)
            pool.wait_ge(s_sel, 2)
            nc.gpsimd.affine_select(out=M.ident[:, :], in_=M.ident[:, :], compare_op=ALU.not_equal, fill=1.0,
                                    base=0, pattern=[[-1, P]], channel_multiplier=1).then_inc(s_sel, 1)
            nc.gpsimd.affine_select(out=M.lower[:, :], in_=M.lower[:, :], compare_op=ALU.is_gt, fill=0.0,
                                    base=0, pattern=[[-1, P]], channel_multiplier=1).then_inc(s_sel, 1)

        @block.tensor
        def _(pe):
            pe.wait_ge(s_kf, 1)
            pe.wait_ge(s_sel, 4)
            for h in range(2):
                for n, k in enumerate(("src", "dst", "type")):
                    last = nc.tensor.transpose(psK[h][0:half, n, :], M.key[k][:, half * h:half * h + half],
                                               M.ident[:, :])
            last.then_inc(s_kp, 1)
            for n in range(2):
                with pe.Fori(0, NG // slots) as i:
                    for u in range(slots):
                        r = n * NG + slots * i + u
                        pe.wait_ge(s_col, r + 1)
                        pe.wait_ge(s_used, r + 1)
                        for j in range(G):
                            last = nc.tensor.transpose(psB[u][:, j, :], column[u][:, j:j + 1].to_broadcast([P, P]),
                                                       M.ident[:, :])
                        last.then_inc(s_row, 1)
            pe.wait_ge(s_w, 16 * n_weights[0])
            for n in range(2):
                last = nc.tensor.transpose(psW[:, F * n:F * n + F], a12[:, n, :, :].rearrange("a i f -> a (i f)"),
                                           M.ident[0:F, 0:F])
            last.then_inc(s_kp, 1)
            pe.wait_ge(s_mr, 1)
            nc.tensor.transpose(psW[0:1, :], rmax[:, :], M.ident[:, :]).then_inc(s_mp, 1)

        @block.vector
        def _(dve):
            s = Steps(dve, s_dve)
            nc.vector.memset(M.WB[:, :, :, :], 0.0)
            nc.vector.memset(M.WB2[:, :, :, :], 0.0)
            for w in (M.RA, M.ROOT, M.A1B, M.A2B, M.SLB, M.W3B, M.W2B, M.WCR):
                nc.vector.memset(w[:, :], 0.0)
            for w in (M.W1S, M.W1D):
                nc.vector.memset(w[:, :, :], 0.0)
            nc.vector.memset(M.W1E[:, :, :], 0.0).then_inc(s_wz, 1)
            nc.vector.sem_inc(s_row, slots)
            nc.vector.sem_inc(s_used, slots)
            dve.wait_ge(s_idx, 80)
            for k in ("src", "dst", "type"):
                last = nc.vector.tensor_copy(M.key[k][:, :], keyI[k][:, :])
            last.then_inc(s_kf, 1)
            dve.wait_ge(s_attr, 16)
            s.done(nc.vector.tensor_scalar(dist[:, :, :], attr[:, :, :], float(KS - 1), 0.0, ALU.mult, ALU.max))
            s.sync()
            s.done(nc.vector.tensor_scalar(dist[:, :, :], dist[:, :, :], float(KS - 1), None, ALU.min))
            s.sync()
            for j in range(KS):
                s.done(nc.vector.tensor_scalar(hat[:, :, :, j], dist[:, :, :], float(-j), None, ALU.add))
            s.sync()
            s.done(nc.vector.tensor_scalar(fall[:, :, :, :], hat[:, :, :, :], -1.0, 1.0, ALU.mult, ALU.add))
            s.done(nc.vector.tensor_scalar(rise[:, :, :, :], hat[:, :, :, :], 1.0, None, ALU.add))
            s.sync()
            s.done(nc.vector.tensor_tensor(hat[:, :, :, :], fall[:, :, :, :], rise[:, :, :, :], ALU.min))
            s.sync()
            s.done(nc.vector.tensor_scalar(hat[:, :, :, :], hat[:, :, :, :], 0.0, None, ALU.max))
            s.sync()
            taps = M.C[:, :, :].rearrange("p t (b a) -> p t b a", b=KS)
            for b in range(KS):
                s.done(nc.vector.tensor_tensor(taps[:, :, b, :], hat[:, :, 0, :], rep(hat[:, :, 1, b], KS), ALU.mult))
            dve.wait_ge(s_kp, 1)
            for h in range(2):
                nc.vector.tensor_copy(kT[:, :, h, :], psK[h][0:half, :, :]).then_inc(s_kc, 1)
            dve.wait_ge(s_sel, 4)
            for n, k in enumerate(("src", "dst")):
                with dve.Fori(0, NG // slots) as i:
                    for u in range(slots):
                        g = slots * i + u
                        dve.wait_ge(s_used, n * NG + g + 1)
                        dve.wait_ge(s_row, n * NG + g + slots + 1)
                        for j in range(G):
                            last = nc.vector.scalar_tensor_tensor(
                                same[u][:, j, :], psB[u][:, j, :], M.key[k][:, bass.ds(G * g + j, 1)], M.lower[:, :],
                                ALU.is_equal, ALU.mult, accum_out=M.rank[k][:, bass.ds(G * g + j, 1)])
                        last.then_inc(s_used, 1)
            dve.wait_ge(s_used, slots + 2 * NG)
            dve.wait_ge(s_w, 16 * n_weights[0])
            s.done(nc.vector.tensor_tensor(watt[:, :, :], taps0[:, :, :], along(att[:, 1, :], TAPS), ALU.mult))
            s.done(nc.vector.tensor_tensor(rattf[:, :], rootw[:, :], att[:, 0, :], ALU.mult))
            s.sync()
            s.done(nc.vector.reduce_sum(wattk[:, :], watt[:, :, :], AX.X))
            s.done(nc.vector.reduce_sum(ratt[:, :], rattf[:, :], AX.X))
            s.sync()
            dve.wait_ge(s_kp, 2)
            for i in range(G):
                b = slice(F * i, F * i + F)
                s.done(nc.vector.tensor_copy(M.WB[b, i, :, 0:F], taps0[b, :, :]))
                s.done(nc.vector.tensor_copy(M.WB[b, i, :, F], wattk[b, :]))
                s.done(nc.vector.tensor_copy(M.RA[b, i:i + 1], ratt[b, :]))
                s.done(nc.vector.tensor_copy(M.A1B[b, b], psW[b, 0:F]))
                s.done(nc.vector.tensor_copy(M.A2B[b, b], psW[b, F:2 * F]))
            for k in ("src", "dst"):
                s.done(nc.vector.tensor_scalar(again[:, :], M.rank[k][:, :], 0.5, None, ALU.is_gt))
                s.done(nc.vector.tensor_scalar(pad[:, :], M.key[k][:, :], float(N), None, ALU.is_ge))
                s.done(nc.vector.tensor_scalar(gap[:, :], M.key[k][:, :], M.waste[:, 0:1], -1.0, ALU.subtract, ALU.mult))
                s.sync()
                s.done(nc.vector.tensor_tensor(again[:, :], again[:, :], pad[:, :], ALU.max))
                s.sync()
                s.done(nc.vector.tensor_tensor(again[:, :], again[:, :], gap[:, :], ALU.mult))
                s.sync()
                s.done(nc.vector.tensor_tensor(M.sidx[k][:, :], again[:, :], M.key[k][:, :], ALU.add))
                s.sync()
            s.done(nc.vector.tensor_scalar(gap[:, :], pad[:, :], -1.0, 1.0, ALU.mult, ALU.add))
            s.sync()
            s.done(nc.vector.tensor_tensor(gap[:, :], M.rank["dst"][:, :], gap[:, :], ALU.mult))
            s.sync()
            nc.vector.reduce_max(rmax[:, :], gap[:, :], AX.X).then_inc(s_mr, 1)
            dve.wait_ge(s_mp, 1)
            s.done(nc.vector.reduce_max(rmax1[:, :], psW[0:1, :], AX.X))
            s.sync()
            s.done(nc.vector.tensor_copy(M.rounds[:, :], rmax1[:, :]))
            s.sync()
    M.sems.retire(taken)


def clear_rows(sp, M, tables, g, cleared):
    for tab in tables:
        sp.dma_start(tab[bass.ds(P * CR * g, P * CR), :].rearrange("(p r) w -> p (r w)", p=P),
                     M.zeros[:, 0:CR * tab.shape[1]]).then_inc(cleared, 16)


def spread_keys(sp, M, name, buf, free, landed, tables=(), cleared=None):
    with sp.Fori(0, NG // 2) as i:
        for u in range(2):
            sp.wait_ge(free, 2 * i + u + 1)
            sp.nop(nofuse=True)
            sp.dma_start(buf[:, u, :, :], M.keyT[name][cols(2 * i + u), :].unsqueeze(0)
                         .to_broadcast([P, G, P])).then_inc(landed[u], 16)
            clear_rows(sp, M, tables, 2 * i + u, cleared)
    if tables:
        sp.wait_ge(cleared, 16 * NG * len(tables))


def rows_at(idx, j):
    return bass.IndirectOffsetOnAxis(ap=idx[:, j:j + 1], axis=0)


def gather_and_merge(nc, pool, M, key, source, state, X, gi, si, old, new, sems, lag, cuts):
    staged_x, staged_s, x_in, x_used, state_in, state_out, merged = sems

    def stage_x(g, v):
        for n, k in enumerate(("src", "dst")):
            nc.gpsimd.tensor_copy(gi[v][:, G * n:G * n + G], M.gidx[k][:, cols(g)]).then_inc(staged_x, 1)

    def gather_x(v, some):
        for j in some:
            nc.gpsimd.indirect_dma_start(out=X[v][:, j, :], out_offset=None, in_=source,
                                         in_offset=rows_at(gi[v], j)).then_inc(x_in[v], 16)

    def gather_state(v, pair):
        for j in pair:
            nc.gpsimd.indirect_dma_start(out=old[j // 2][:, j % 2, :], out_offset=None, in_=state[j % 2],
                                         in_offset=rows_at(si[v], j)).then_inc(state_in[j], 16)

    def scatter_state(v, pair):
        for j in pair:
            nc.gpsimd.indirect_dma_start(out=state[j % 2], out_offset=rows_at(si[v], j),
                                         in_=new[j // 2][:, j % 2, :], in_offset=None).then_inc(state_out[j], 16)

    def chain(g, v, ahead):
        nc.gpsimd.tensor_copy(si[v][:, :], M.sidx[key][:, cols(g)]).then_inc(staged_s, 1)
        pool.wait_ge(staged_s, g + 1)
        wait(pool, state_out[2], 16 * g)
        wait(pool, state_out[3], 16 * g)
        pool.nop(nofuse=True)
        gather_state(v, (0, 1))
        ahead(0, cuts[0])
        pool.wait_ge(merged, 2 * g + 1)
        pool.nop(nofuse=True)
        scatter_state(v, (0, 1))
        ahead(*cuts[0:2])
        pool.wait_ge(state_out[0], 16 * g + 16)
        pool.wait_ge(state_out[1], 16 * g + 16)
        pool.nop(nofuse=True)
        gather_state(v, (2, 3))
        ahead(*cuts[1:3])
        pool.wait_ge(merged, 2 * g + 2)
        pool.nop(nofuse=True)
        scatter_state(v, (2, 3))
        ahead(cuts[2], 2 * G)

    def body(g, u, h):
        if live(g + 2):
            pool.wait_ge(x_used, g + 1)
            pool.nop(nofuse=True)
            stage_x(g + 2, u)
            pool.wait_ge(staged_x, 2 * (g + 3))
            pool.nop(nofuse=True)
            ahead = lambda a, b: gather_x(u, range(a, b))
        else:
            ahead = lambda a, b: None
        if live(g - lag):
            chain(g - lag, (u + lag) % 2, ahead)
        else:
            ahead(0, 2 * G)

    stage_x(0, 0)
    stage_x(1, 1)
    pool.wait_ge(staged_x, 4)
    gather_x(0, range(2 * G))
    gather_x(1, range(2 * G))
    each_group(pool, body, lead=2 * lag, extra=lag)
    for j in range(G):
        pool.wait_ge(state_out[j], 16 * NG)


NORM_SEMS = ("centred", "squared", "summed", "rooted", "scaled")


class Norm:

    def __init__(self, nc, M, sb, sem, n):
        self.nc, self.M, self.n = nc, M, n
        self.total, self.ssq, self.root, self.rstd = (sb(k, [P, n]) for k in ("total", "ssq", "root", "rstd"))
        self.diff, self.sq, self.normed, self.h = (sb(k, [P, n, F]) for k in ("diff", "sq", "normed", "h"))
        self.centred, self.squared, self.summed, self.rooted, self.scaled = (sem(k) for k in NORM_SEMS)
        self.h_ready = sem("h_ready")

    def centre(self, s, x):
        s.done(self.nc.vector.reduce_sum(self.total[:, :], x, AX.X))
        s.sync()
        self.nc.vector.scalar_tensor_tensor(self.diff[:, :, :], x, float(F), rep(self.total[:, :], F),
                                            ALU.mult, ALU.subtract).then_inc(self.centred, 1)

    def square(self, act, g):
        act.wait_ge(self.centred, g + 1)
        self.nc.scalar.activation(self.sq[:, :, :], self.diff[:, :, :], ACT.Square).then_inc(self.squared, 1)

    def sum_squares(self, dve, g):
        dve.wait_ge(self.squared, g + 1)
        self.nc.vector.reduce_sum(self.ssq[:, :], self.sq[:, :, :], AX.X).then_inc(self.summed, 1)

    def take_root(self, act, g):
        act.wait_ge(self.summed, g + 1)
        self.nc.scalar.activation(self.root[:, :], self.ssq[:, :], ACT.Sqrt,
                                  bias=self.M.ln_eps[:, 0:1]).then_inc(self.rooted, 1)

    def scale(self, dve, s, g):
        dve.wait_ge(self.rooted, g + 1)
        s.done(self.nc.vector.reciprocal(self.rstd[:, :], self.root[:, :]))
        s.sync()
        self.nc.vector.tensor_tensor(self.normed[:, :, :], self.diff[:, :, :], rep(self.rstd[:, :], F),
                                     ALU.mult).then_inc(self.scaled, 1)

    def relu(self, act, g, h=None):
        act.wait_ge(self.scaled, g + 1)
        self.nc.scalar.activation((h or self.h)[:, :, :], self.normed[:, :, :], ACT.Relu,
                                  scale=LN_GAIN).then_inc(self.h_ready, 1)

    def transpose(self, pe, psT, g, signal):
        pe.wait_ge(self.h_ready, g + 1)
        for n in range(2):
            last = self.nc.tensor.transpose(psT[:, n, :], self.h[:, G * n:G * n + G, :].rearrange("p a f -> p (a f)"),
                                            self.M.ident[:, :])
        last.then_inc(signal, 1)


def layer0_edges(nc, t, M):
    with ExitStack() as ctx:
        sb = lambda name, shape, dt=fp32: ctx.enter_context(nc.sbuf_tensor("e0_" + name, shape, dt))
        ps = lambda name, shape: ctx.enter_context(nc.psum_tensor("e0_" + name, shape, fp32))
        taken = []
        sem = M.sems.phase("e0_", taken)
        W = F + 2
        DEN, MAX = F, F + 1
        X = [sb(f"X{u}", [P, 2 * G, F]) for u in range(2)]
        gi = [sb(f"gi{u}", [P, 2 * G], i32) for u in range(2)]
        si = [sb(f"si{u}", [P, G], i32) for u in range(2)]
        keys = sb("keys", [P, 2, G, P])
        hT = sb("hT", [P, 2, P])
        prod = [sb(f"prod{b}", [P, TAPS, F + 1]) for b in range(2)]
        msg = [sb(f"msg{u}", [P, G, F + 1]) for u in range(2)]
        score = sb("score", [P, G])
        alpha = sb("alpha", [P, G])
        same = sb("same", [P, G, P])
        off = sb("off", [P, G, P])
        diag = sb("diag", [P, G, P])
        masked = sb("masked", [P, G, P])
        less = sb("less", [P, G])
        V = sb("V", [P, G, F + 1])
        part = [sb(f"part{u}", [P, G, W]) for u in range(2)]
        old = [sb(f"old{q}", [P, 2, W]) for q in range(2)]
        new = [sb(f"new{q}", [P, 2, W]) for q in range(2)]
        empty = sb("empty", [P, 2])
        was_max = sb("was_max", [P, 2])
        gaps = sb("gaps", [P, 2, 2])
        fade = sb("fade", [P, 2, 2])
        kept = sb("kept", [P, 2, F + 1])
        added = sb("added", [P, 2, F + 1])
        psT = ps("psT", [P, 2, P])
        psX = [[ps(f"psX{b}{c}", [P, 512]) for c in range(2)] for b in range(2)]
        psA = ps("psA", [P, G, P])
        psS = ps("psS", [P, G])
        psV = ps("psV", [P, G, F + 1])

        norm = Norm(nc, M, sb, sem, 2 * G)
        staged_x, staged_s = sem("staged_x"), sem("staged_s")
        x_in = [sem(f"x_in{u}") for u in range(2)]
        state_in = [sem(f"state_in{j}") for j in range(G)]
        state_out = [sem(f"state_out{j}") for j in range(G)]
        keys_in = [sem(f"keys_in{u}") for u in range(2)]
        keys_free = sem("keys_free")
        hT_psum, hT_ready = sem("hT_psum"), sem("hT_ready")
        taps_ready, taps_used = sem("taps_ready"), sem("taps_used")
        score_ready, alpha_ready, diag_ready = sem("score_ready"), sem("alpha_ready"), sem("diag_ready")
        spread_ready, less_ready, ex_ready = sem("spread_ready"), sem("less_ready"), sem("ex_ready")
        V_ready, sums_ready, part_ready = sem("V_ready"), sem("sums_ready"), sem("part_ready")
        gaps_ready, fade_ready, merged = sem("gaps_ready"), sem("fade_ready"), sem("merged")
        s_dve, cleared = sem("dve_steps"), sem("cleared")
        block = ctx.enter_context(nc.Block())

        @block.sync
        def _(sp):
            M.sems.clear(sp)
            spread_keys(sp, M, "src", keys, keys_free, keys_in, M.max_state + [M.rel_sums], cleared)

        @block.gpsimd
        def _(pool):
            gather_and_merge(nc, pool, M, "src", t["x"], M.softmax_state, X, gi, si, old, new,
                             (staged_x, staged_s, x_in, norm.centred, state_in, state_out, merged), LAG0, (3, 5, 8))

        @block.scalar
        def _(act):
            def merge(pair, g):
                act.wait_ge(gaps_ready, 2 * g + pair + 1)
                nc.scalar.activation(fade[:, :, :], gaps[:, :, :], ACT.Exp).then_inc(fade_ready, 1)

            def body(g, u, i):
                if live(g + 1):
                    norm.square(act, g + 1)
                if live(g - 1):
                    act.wait_ge(less_ready, g)
                    nc.scalar.activation(V[:, :, F], less[:, :], ACT.Exp).then_inc(ex_ready, 1)
                if live(g - LAG0):
                    merge(0, g - LAG0)
                if live(g + 1):
                    norm.take_root(act, g + 1)
                if live(g - 1):
                    act.wait_ge(sums_ready, g)
                    nc.scalar.activation(part[1 - u][:, :, 0:F + 1], psV[:, :, :], ACT.Copy).then_inc(part_ready, 1)
                if live(g + 1):
                    norm.relu(act, g + 1)
                    act.wait_ge(hT_psum, g + 2)
                    nc.scalar.activation(hT[:, :, :], psT[:, :, :], ACT.Copy).then_inc(hT_ready, 1)
                if live(g - LAG0):
                    merge(1, g - LAG0)
                if live(g):
                    act.wait_ge(alpha_ready, g + 1)
                    for j in range(G):
                        last = nc.scalar.activation(diag[:, j, :], M.ident[:, :], ACT.Copy, scale=alpha[:, j:j + 1])
                    last.then_inc(diag_ready, 1)

            norm.square(act, 0)
            norm.take_root(act, 0)
            norm.relu(act, 0)
            act.wait_ge(hT_psum, 1)
            nc.scalar.activation(hT[:, :, :], psT[:, :, :], ACT.Copy).then_inc(hT_ready, 1)
            each_group(act, body, lead=4, extra=LAG0)

        @block.tensor
        def _(pe):
            def taps(g, j):
                wait(pe, taps_used, G * g + j - 1)
                w = M.WB[:, j, :, :].rearrange("p k o -> p (k o)")
                cut = TC * (F + 1)
                nc.tensor.matmul(psX[j % 2][0][:, 0:cut], hT[:, 1, :], w[:, 0:cut], start=True, stop=True)
                nc.tensor.matmul(psX[j % 2][1][:, 0:TAPS * (F + 1) - cut], hT[:, 1, :], w[:, cut:],
                                 start=True, stop=True).then_inc(taps_ready, 1)

            def first_half(g):
                pe.wait_ge(hT_ready, g + 1)
                taps(g, 0)
                taps(g, 1)

            def body(g, u, i):
                if live(g):
                    taps(g, 2)
                    taps(g, 3)
                    wait(pe, alpha_ready, g)
                    nc.tensor.matmul(psS[:, :], hT[:, 0, :], M.RA[:, :], start=True, stop=True).then_inc(score_ready, 1)
                if live(g - 1):
                    pe.wait_ge(V_ready, g)
                    for j in range(G):
                        last = nc.tensor.matmul(psV[:, j, :], same[:, j, :], V[:, j, :], start=True, stop=True)
                    last.then_inc(sums_ready, 1)
                if live(g + 1):
                    norm.transpose(pe, psT, g + 1, hT_psum)
                    first_half(g + 1)
                if live(g):
                    pe.wait_ge(diag_ready, g + 1)
                    nc.tensor.matmul(psA[:, :, :].rearrange("p a b -> p (a b)"), M.ones[:, :],
                                     diag[:, :, :].rearrange("p a b -> p (a b)"),
                                     start=True, stop=True).then_inc(spread_ready, 1)

            norm.transpose(pe, psT, 0, hT_psum)
            first_half(0)
            each_group(pe, body, lead=4, extra=1)

        @block.vector
        def _(dve):
            s = Steps(dve, s_dve, PER_E0)

            def merge(pair, g, v):
                mine = part[v][:, 2 * pair:2 * pair + 2, :]
                o, n = old[pair], new[pair]
                for j in (2 * pair, 2 * pair + 1):
                    dve.wait_ge(state_in[j], 16 * g + 16)
                dve.wait_ge(part_ready, g + 1)
                s.done(nc.vector.tensor_scalar(empty[:, :], o[:, :, DEN], 0.0, -BIG, ALU.is_equal, ALU.mult))
                s.sync()
                s.done(nc.vector.tensor_tensor(was_max[:, :], o[:, :, MAX], empty[:, :], ALU.add))
                s.sync()
                s.done(nc.vector.tensor_tensor(n[:, :, MAX], was_max[:, :], mine[:, :, MAX], ALU.max))
                s.sync()
                s.done(nc.vector.tensor_tensor(gaps[:, 0, :], was_max[:, :], n[:, :, MAX], ALU.subtract))
                nc.vector.tensor_tensor(gaps[:, 1, :], mine[:, :, MAX], n[:, :, MAX], ALU.subtract).then_inc(gaps_ready, 1)

            def merge_end(pair, g, v):
                mine = part[v][:, 2 * pair:2 * pair + 2, :]
                o, n = old[pair], new[pair]
                dve.wait_ge(fade_ready, 2 * g + pair + 1)
                s.done(nc.vector.tensor_tensor(kept[:, :, :], o[:, :, 0:F + 1], rep(fade[:, 0, :], F + 1), ALU.mult))
                s.done(nc.vector.tensor_tensor(added[:, :, :], mine[:, :, 0:F + 1], rep(fade[:, 1, :], F + 1), ALU.mult))
                s.sync()
                nc.vector.tensor_tensor(n[:, :, 0:F + 1], kept[:, :, :], added[:, :, :], ALU.add).then_inc(merged, 1)

            def weigh(g, u, j):
                dve.wait_ge(taps_ready, G * g + j + 1)
                lo_j = G * g + j
                coef = M.C[:, lo_j, :] if isinstance(g, int) else \
                    M.C[:, bass.ds(lo_j, 1), :].rearrange("p a k -> p (a k)")
                for c, (lo, hi) in enumerate(((0, TC), (TC, TAPS))):
                    last = nc.vector.tensor_tensor(
                        prod[j % 2][:, lo:hi, :], psX[j % 2][c][:, 0:(hi - lo) * (F + 1)].rearrange("p (k o) -> p k o", o=F + 1),
                        rep(coef[:, lo:hi], F + 1), ALU.mult)
                    if c == 0:
                        s.done(last)
                last.then_inc(taps_used, 1)
                s.sync()
                dve.wait_ge(taps_used, G * g + j + 1)
                s.done(nc.vector.reduce_sum(msg[u][:, j, :], prod[j % 2][:, :, :].rearrange("p k o -> p o k"), AX.X))

            def body(g, u, i):
                if live(g):
                    weigh(g, u, 0)
                if live(g + 1):
                    dve.wait_ge(x_in[1 - u], 16 * 2 * G * ((g + 1) // 2 + 1 if isinstance(g, int) else i + u + 1))
                    norm.centre(s, X[1 - u][:, :, :])
                if live(g - 1):
                    dve.wait_ge(spread_ready, g)
                    s.done(nc.vector.tensor_tensor(masked[:, :, :], off[:, :, :], psA[:, :, :], ALU.add))
                    s.sync()
                    s.done(nc.vector.reduce_max(part[1 - u][:, :, MAX], masked[:, :, :], AX.X))
                    s.sync()
                    nc.vector.tensor_tensor(less[:, :], alpha[:, :], part[1 - u][:, :, MAX], ALU.subtract).then_inc(less_ready, 1)
                if live(g):
                    weigh(g, u, 1)
                if live(g - 1):
                    dve.wait_ge(ex_ready, g)
                    nc.vector.tensor_tensor(V[:, :, 0:F], msg[1 - u][:, :, 0:F], rep(V[:, :, F], F), ALU.mult).then_inc(V_ready, 1)
                if live(g - LAG0):
                    merge(0, g - LAG0, u)
                if live(g + 1):
                    norm.sum_squares(dve, g + 1)
                if live(g - LAG0):
                    merge_end(0, g - LAG0, u)
                if live(g + 1):
                    norm.scale(dve, s, g + 1)
                if live(g):
                    weigh(g, u, 2)
                    dve.wait_ge(keys_in[u], 16 * (i + 1))
                    wait(dve, sums_ready, g)
                    s.done(nc.vector.tensor_tensor(same[:, :, :], keys[:, u, :, :], rep(M.key["src"][:, cols(g)], P),
                                                   ALU.is_equal))
                    weigh(g, u, 3)
                    nc.vector.tensor_scalar(off[:, :, :], same[:, :, :], 1.0, BIG, ALU.subtract, ALU.mult).then_inc(keys_free, 1)
                    dve.wait_ge(score_ready, g + 1)
                    s.sync()
                    s.done(nc.vector.tensor_tensor(score[:, :], msg[u][:, :, F], psS[:, :], ALU.add))
                    s.sync()
                    nc.vector.scalar_tensor_tensor(alpha[:, :], score[:, :], SLOPE, score[:, :],
                                                   ALU.mult, ALU.max).then_inc(alpha_ready, 1)
                    dve.wait_ge(keys_free, g + 3)
                if live(g - LAG0):
                    merge(1, g - LAG0, u)
                    merge_end(1, g - LAG0, u)

            nc.vector.sem_inc(keys_free, 2)
            dve.wait_ge(x_in[0], 16 * 2 * G)
            norm.centre(s, X[0][:, :, :])
            norm.sum_squares(dve, 0)
            norm.scale(dve, s, 0)
            each_group(dve, body, s, lead=4, extra=LAG0)


def live_chunk(c):
    return not isinstance(c, int) or c < NCH


def after(c, u, i):
    return c + 1, 1 - u, (c + 1) // 2 if isinstance(c, int) else i + u


def project_pe(nc, pe, M, weights, h, psT, hT, psR, sems, c, u):
    h_ready, hT_psum, hT_ready, round_ready, used = sems
    flat = h[:, :, :].rearrange("p k f -> p (k f)")

    def transposes(q):
        wait(pe, hT_ready, 3 * c + q - 1)
        for n in range(G):
            last = nc.tensor.transpose(psT[(u + q) % 2][:, n, :], flat[:, P * (G * q + n):P * (G * q + n) + P],
                                       M.ident[:, :])
        last.then_inc(hT_psum, 1)

    def products(q):
        pe.wait_ge(hT_ready, 3 * c + q + 1)
        for n in range(G):
            last = nc.tensor.matmul(psR[q][:, P * n:P * n + P], hT[(u + q) % 2][:, n, :], weights[:, :],
                                    start=True, stop=True)
        last.then_inc(round_ready, 1)

    pe.wait_ge(h_ready, c + 1)
    transposes(0)
    wait(pe, used, c)
    for q in range(3):
        if q < 2:
            transposes(q + 1)
        products(q)


def project_scalar(nc, act, psT, hT, sems, c, u, q):
    h_ready, hT_psum, hT_ready, round_ready, used = sems
    r, b = 3 * c + q, (u + q) % 2
    act.wait_ge(hT_psum, r + 1)
    wait(act, round_ready, r - 1)
    nc.scalar.activation(hT[b][:, :, :], psT[b][:, :, :], ACT.Copy).then_inc(hT_ready, 1)


def dense0(nc, t, M):
    with ExitStack() as ctx:
        sb = lambda name, shape, dt=fp32: ctx.enter_context(nc.sbuf_tensor("d0_" + name, shape, dt))
        ps = lambda name, shape: ctx.enter_context(nc.psum_tensor("d0_" + name, shape, fp32))
        taken = []
        sem = M.sems.phase("d0_", taken)
        W = F + 2
        DEN, MAX = F, F + 1
        X = [sb(f"X{u}", [P, K, F]) for u in range(2)]
        S = [[sb(f"S{u}{k}", [P, K, W]) for k in range(2)] for u in range(2)]
        Y = [sb(f"Y{u}", [P, K, F]) for u in range(2)]
        hT = [sb(f"hT{q}", [P, G, P]) for q in range(2)]
        empty = sb("empty", [P, 2, K])
        top = sb("top", [P, K])
        gaps = sb("gaps", [P, 2, K])
        fade = sb("fade", [P, 2, K])
        dens = sb("dens", [P, 2, K])
        den = sb("den", [P, K])
        inv = sb("inv", [P, K])
        part = [sb(f"part{k}", [P, K, F]) for k in range(2)]
        was = sb("was", [P, 2, K])
        share = sb("share", [P, 2, K])
        sums = [sb(f"sums{u}", [P, K, F]) for u in range(2)]
        base = [sb(f"base{u}", [P, K, F]) for u in range(2)]
        both = sb("both", [P, K, F])
        psT = [ps(f"psT{q}", [P, G, P]) for q in range(2)]
        psR = [ps(f"psR{q}", [P, G * P]) for q in range(3)]
        loaded = [sem(f"loaded{u}") for u in range(2)]
        stored = sem("stored")
        norm = Norm(nc, M, sb, sem, K)
        h = [norm.h, sb("h1", [P, K, F])]
        hT_psum, hT_ready = sem("hT_psum"), sem("hT_ready")
        gaps_ready, fade_ready, share_ready, sums_ready = sem("gaps_ready"), sem("fade_ready"), sem("share_ready"), sem("sums_ready")
        round_ready = sem("round_ready")
        added, done = sem("added"), sem("done")
        proj_sems = norm.h_ready, hT_psum, hT_ready, round_ready, done
        s_dve, s_pool = sem("dve_steps"), sem("pool_steps")
        block = ctx.enter_context(nc.Block())

        @block.sync
        def _(sp):
            M.sems.clear(sp)
            def load(c, u):
                sp.dma_start(X[u][:, :, :], chunk(t["x"], c)).then_inc(loaded[u], 16)
                for k in range(2):
                    sp.dma_start(S[u][k][:, :, :], chunk(M.softmax_state[k], c)).then_inc(loaded[u], 16)

            def refill(c, u):
                sp.wait_ge(sums_ready, c + 1)
                sp.wait_ge(norm.centred, c + 1)
                sp.nop(nofuse=True)
                load(c + 2, u)

            def body(c, u, i):
                if not isinstance(c, int) or c + 3 < NCH:
                    refill(c + 1, 1 - u)
                sp.wait_ge(done, c + 1)
                sp.nop(nofuse=True)
                wait(sp, stored, 16 * c)
                sp.nop(nofuse=True)
                sp.dma_start(chunk(M.x1, c), Y[u][:, :, :]).then_inc(stored, 16)

            load(0, 0)
            load(1, 1)
            refill(0, 0)
            each_chunk(sp, body)
            sp.wait_ge(stored, 16 * NCH)

        @block.gpsimd
        def _(pool):
            s = Steps(pool, s_pool, 3)

            def body(c, u, i):
                pool.wait_ge(loaded[u], 48 * (i + 1))
                pool.wait_ge(share_ready, c + 1)
                for k in range(2):
                    s.done(nc.gpsimd.tensor_tensor(part[k][:, :, :], S[u][k][:, :, 0:F], rep(share[:, k, :], F), ALU.mult))
                wait(pool, added, c - 1)
                s.done(nc.gpsimd.tensor_tensor(base[u][:, :, :], X[u][:, :, :], along(M.bias0[:, :], K), ALU.add))
                s.sync()
                nc.gpsimd.tensor_tensor(sums[u][:, :, :], part[0][:, :, :], part[1][:, :, :], ALU.add).then_inc(sums_ready, 1)

            each_chunk(pool, body, s)

        @block.scalar
        def _(act):
            def body(c, u, i):
                n, v, _ = after(c, u, i)
                project_scalar(nc, act, psT, hT, proj_sems, c, u, 0)
                if live_chunk(n):
                    act.wait_ge(gaps_ready, n + 1)
                    nc.scalar.activation(fade[:, :, :], gaps[:, :, :], ACT.Exp).then_inc(fade_ready, 1)
                project_scalar(nc, act, psT, hT, proj_sems, c, u, 1)
                if live_chunk(n):
                    norm.square(act, n)
                project_scalar(nc, act, psT, hT, proj_sems, c, u, 2)
                if live_chunk(n):
                    norm.take_root(act, n)
                    norm.relu(act, n, h[v])

            act.wait_ge(gaps_ready, 1)
            nc.scalar.activation(fade[:, :, :], gaps[:, :, :], ACT.Exp).then_inc(fade_ready, 1)
            norm.square(act, 0)
            norm.take_root(act, 0)
            norm.relu(act, 0)
            each_chunk(act, body)

        @block.tensor
        def _(pe):
            each_chunk(pe, lambda c, u, i: project_pe(nc, pe, M, M.ROOT, h[u], psT, hT, psR, proj_sems, c, u))

        @block.vector
        def _(dve):
            s = Steps(dve, s_dve, PER_D0)

            def states(c, u, i):
                dve.wait_ge(loaded[u], 48 * (i + 1))
                wait(dve, norm.scaled, c)
                for k in range(2):
                    s.done(nc.vector.tensor_scalar(empty[:, k, :], S[u][k][:, :, DEN], 0.0, -BIG, ALU.is_equal, ALU.mult))
                s.sync()
                for k in range(2):
                    s.done(nc.vector.tensor_tensor(was[:, k, :], S[u][k][:, :, MAX], empty[:, k, :], ALU.add))
                s.sync()
                s.done(nc.vector.tensor_tensor(top[:, :], was[:, 0, :], was[:, 1, :], ALU.max))
                s.sync()
                nc.vector.tensor_tensor(gaps[:, :, :], was[:, :, :], along(top[:, :], 2), ALU.subtract).then_inc(gaps_ready, 1)

            def shares(c, u):
                dve.wait_ge(fade_ready, c + 1)
                for k in range(2):
                    s.done(nc.vector.tensor_tensor(dens[:, k, :], S[u][k][:, :, DEN], fade[:, k, :], ALU.mult))
                s.sync()
                s.done(nc.vector.scalar_tensor_tensor(den[:, :], dens[:, 0, :], 1e-16, dens[:, 1, :], ALU.add, ALU.add))
                s.sync()
                s.done(nc.vector.reciprocal(inv[:, :], den[:, :]))
                s.sync()
                wait(dve, sums_ready, c)
                nc.vector.tensor_tensor(share[:, :, :], fade[:, :, :], along(inv[:, :], 2), ALU.mult).then_inc(share_ready, 1)

            def body(c, u, i):
                n, v, k = after(c, u, i)
                if live_chunk(n):
                    states(n, v, k)
                    norm.centre(s, X[v][:, :, :])
                    shares(n, v)
                    norm.sum_squares(dve, n)
                dve.wait_ge(sums_ready, c + 1)
                wait(dve, done, c)
                nc.vector.tensor_tensor(both[:, :, :], base[u][:, :, :], sums[u][:, :, :], ALU.add).then_inc(added, 1)
                if live_chunk(n):
                    norm.scale(dve, s, n)
                dve.wait_ge(added, c + 1)
                wait(dve, stored, 16 * (c - 1))
                dve.wait_ge(round_ready, 3 * c + 3)
                m = G * G
                for q in range(3):
                    last = nc.vector.tensor_tensor(Y[u][:, m * q:m * q + m, :], both[:, m * q:m * q + m, :],
                                                   psR[q][:, :].rearrange("p (k f) -> p k f", f=F), ALU.add)
                last.then_inc(done, 1)

            states(0, 0, 0)
            norm.centre(s, X[0][:, :, :])
            shares(0, 0)
            norm.sum_squares(dve, 0)
            norm.scale(dve, s, 0)
            each_chunk(dve, body, s)
    M.sems.retire(taken)


def layer1_edges(nc, t, M):
    with ExitStack() as ctx:
        sb = lambda name, shape, dt=fp32: ctx.enter_context(nc.sbuf_tensor("e1_" + name, shape, dt))
        ps = lambda name, shape: ctx.enter_context(nc.psum_tensor("e1_" + name, shape, fp32))
        taken = []
        sem = M.sems.phase("e1_", taken)
        W = F + 1
        X = [sb(f"X{u}", [P, 2 * G, F]) for u in range(2)]
        gi = [sb(f"gi{u}", [P, 2 * G], i32) for u in range(2)]
        si = [sb(f"si{u}", [P, G], i32) for u in range(2)]
        attr = [sb(f"attr{u}", [P, G, F]) for u in range(2)]
        hT = sb("hT", [P, 3, P])
        hidden = sb("hidden", [P, 2, P])
        biased = sb("biased", [P, G, F])
        keys = {k: sb("keys_" + k, [P, 2, G, P]) for k in ("src", "dst")}
        hits = sb("hits", [P, G, P])
        again, gap, pad = sb("again", [P, T]), sb("gap", [P, T]), sb("pad", [P, T])
        old = [sb(f"old{q}", [P, 2, W]) for q in range(2)]
        new = [sb(f"new{q}", [P, 2, W]) for q in range(2)]
        psT = ps("psT", [P, 3, P])
        psH = ps("psH", [P, 2, P])
        psV = ps("psV", [P, G, F])

        staged_x, staged_s = sem("staged_x"), sem("staged_s")
        x_in = [sem(f"x_in{u}") for u in range(2)]
        state_in = [sem(f"state_in{j}") for j in range(G)]
        state_out = [sem(f"state_out{j}") for j in range(G)]
        attr_in = [sem(f"attr_in{u}") for u in range(2)]
        attr_free, attr_clear = sem("attr_free"), sem("attr_clear")
        keys_in = {k: [sem(f"keys_{k}_in{u}") for u in range(2)] for k in ("src", "dst")}
        keys_free = sem("keys_free")
        norm = Norm(nc, M, sb, sem, 2 * G)
        hT_psum, hT_ready = sem("hT_psum"), sem("hT_ready")
        hidden_psum, hidden_ready, out_ready = sem("hidden_psum"), sem("hidden_ready"), sem("out_ready")
        out_used = sem("out_used")
        merged, s_dve, cleared = sem("merged"), sem("dve_steps"), sem("cleared")
        block = ctx.enter_context(nc.Block())

        @block.sync
        def _(sp):
            M.sems.clear(sp)
            sp.wait_ge(attr_clear, 1)
            rows = t["edge_attr_32"].rearrange("(p t) f -> p t f", p=ROWS_E)
            with sp.Fori(0, NG // 2) as i:
                for u in range(2):
                    sp.wait_ge(attr_free, 2 * i + u + 1)
                    sp.nop(nofuse=True)
                    sp.dma_start(attr[u][0:ROWS_E, :, :], rows[:, cols(2 * i + u), :]).then_inc(attr_in[u], 16)
                    sp.wait_ge(keys_free, 2 * i + u + 1)
                    sp.nop(nofuse=True)
                    for k in ("src", "dst"):
                        sp.dma_start(keys[k][:, u, :, :], M.keyT[k][cols(2 * i + u), :].unsqueeze(0)
                                     .to_broadcast([P, G, P])).then_inc(keys_in[k][u], 16)
                    clear_rows(sp, M, (M.conv_sums, M.square_sums), 2 * i + u, cleared)
            sp.wait_ge(cleared, 16 * NG * 2)

        @block.gpsimd
        def _(pool):
            gather_and_merge(nc, pool, M, "dst", M.x1, M.max_state, X, gi, si, old, new,
                             (staged_x, staged_s, x_in, norm.centred, state_in, state_out, merged), 1, (2, 4, 6))

        @block.scalar
        def _(act):
            def front(g):
                norm.square(act, g)
                norm.take_root(act, g)
                norm.relu(act, g)
                act.wait_ge(hT_psum, g + 1)
                nc.scalar.activation(hT[:, :, :], psT[:, :, :], ACT.Copy).then_inc(hT_ready, 1)

            def body(g, u, i):
                act.wait_ge(hidden_psum, g + 1)
                nc.scalar.activation(hidden[:, :, :], psH[:, :, :], ACT.Relu, bias=M.b1col[:, 0:1]).then_inc(hidden_ready, 1)
                if live(g + 1):
                    front(g + 1)

            front(0)
            each_group(act, body)

        @block.tensor
        def _(pe):
            def front(g, u, i):
                pe.wait_ge(attr_in[u], 16 * (i + 1))
                nc.tensor.transpose(psT[:, 2, :], attr[u][:, :, :].rearrange("p a f -> p (a f)"),
                                    M.ident[:, :]).then_inc(attr_free, 1)
                norm.transpose(pe, psT, g, hT_psum)

            def body(g, u, i):
                pe.wait_ge(hT_ready, g + 1)
                for j in range(2):
                    for n, w in enumerate((M.W1S, M.W1D, M.W1E)):
                        last = nc.tensor.matmul(psH[:, j, :], w[:, j, :], hT[:, n, :], start=(n == 0), stop=(n == 2))
                last.then_inc(hidden_psum, 1)
                pe.wait_ge(hidden_ready, g + 1)
                wait(pe, out_used, g)
                for j in range(2):
                    last = nc.tensor.matmul(psV[:, 2 * j:2 * j + 2, :].rearrange("p a f -> p (a f)"), hidden[:, j, :],
                                            M.W2B[:, :], start=True, stop=True)
                last.then_inc(out_ready, 1)
                if live(g + 1):
                    front(g + 1, 1 - u, (g + 1) // 2 if isinstance(g, int) else i + u)

            front(0, 0, 0)
            each_group(pe, body)

        @block.vector
        def _(dve):
            s = Steps(dve, s_dve, PER_E1)

            def merge(pair, g):
                lo = G * g + 2 * pair
                mine = M.V1[:, lo:lo + 2, :] if isinstance(lo, int) else M.V1[:, bass.ds(lo, 2), :]
                for j in (2 * pair, 2 * pair + 1):
                    dve.wait_ge(state_in[j], 16 * g + 16)
                nc.vector.tensor_tensor(new[pair][:, :, :], old[pair][:, :, :], mine, ALU.max).then_inc(merged, 1)

            def look_back(g, u, i):
                for k in ("src", "dst"):
                    dve.wait_ge(keys_in[k][u], 16 * (i + 1))
                dve.wait_ge(keys_free, g + 2)
                for n, k in enumerate(("src", "dst")):
                    for j in (1, 3):
                        at = slice(G * g + j, G * g + j + 1) if isinstance(g, int) else bass.ds(G * g + j, 1)
                        last = nc.vector.scalar_tensor_tensor(
                            hits[:, 2 * n + j // 2, :], keys[k][:, u, j - 1, :], M.key[k][:, at], M.ones[:, :],
                            ALU.is_equal, ALU.mult, accum_out=M.before[k][:, at])
                last.then_inc(keys_free, 1)

            def rows_of_pairs(k):
                s.done(nc.vector.tensor_tensor(again[:, :], M.rank[k][:, :], M.before[k][:, :], ALU.add))
                s.done(nc.vector.tensor_scalar(pad[:, :], M.key[k][:, :], float(N), None, ALU.is_ge))
                halves = lambda a: a[:, :].rearrange("p (h two) -> p two h", two=2)
                for n, w in enumerate((M.waste, M.waste_odd)):
                    s.done(nc.vector.tensor_scalar(halves(gap)[:, n, :], halves(M.key[k])[:, n, :], w[:, 0:1], -1.0,
                                                   ALU.subtract, ALU.mult))
                s.sync()
                s.done(nc.vector.tensor_scalar(again[:, :], again[:, :], 0.5, None, ALU.is_gt))
                s.sync()
                s.done(nc.vector.tensor_tensor(again[:, :], again[:, :], pad[:, :], ALU.max))
                s.sync()
                s.done(nc.vector.tensor_tensor(again[:, :], again[:, :], gap[:, :], ALU.mult))
                s.sync()
                s.done(nc.vector.tensor_tensor(M.pidx[k][:, :], again[:, :], M.key[k][:, :], ALU.add))
                s.sync()

            def body(g, u, i):
                if live(g - 1):
                    merge(0, g - 1)
                if live(g):
                    dve.wait_ge(out_ready, g + 1)
                    nc.vector.tensor_tensor(biased[:, :, :], psV[:, :, :], along(M.b2row[:, :], G), ALU.add).then_inc(out_used, 1)
                if live(g + 1):
                    dve.wait_ge(x_in[1 - u], 16 * 2 * G * ((g + 1) // 2 + 1 if isinstance(g, int) else i + u + 1))
                    norm.centre(s, X[1 - u][:, :, :])
                if live(g):
                    look_back(g, u, i)
                    dve.wait_ge(out_used, g + 1)
                    s.done(nc.vector.tensor_scalar(M.V1[:, cols(g), 0:F], biased[:, :, :], 0.0, None, ALU.max))
                    s.done(nc.vector.tensor_copy(M.V1[:, cols(g), F], M.eid1[:, cols(g)]))
                if live(g + 1):
                    norm.sum_squares(dve, g + 1)
                if live(g - 1):
                    merge(1, g - 1)
                if live(g + 1):
                    norm.scale(dve, s, g + 1)
                s.sync()

            for u in range(2):
                last = nc.vector.memset(attr[u][:, :, :], 0.0)
            last.then_inc(attr_clear, 1)
            nc.vector.sem_inc(attr_free, 2)
            nc.vector.sem_inc(keys_free, 2)
            for k in ("src", "dst"):
                s.done(nc.vector.memset(M.before[k][:, :], 0.0))
            s.sync()
            dve.wait_ge(x_in[0], 16 * 2 * G)
            norm.centre(s, X[0][:, :, :])
            norm.sum_squares(dve, 0)
            norm.scale(dve, s, 0)
            each_group(dve, body, s, extra=1)
            dve.wait_ge(keys_free, NG + 2)
            for k in ("src", "dst"):
                rows_of_pairs(k)


def more_maxima(nc, M):
    with ExitStack() as ctx:
        sb = lambda name, shape, dt=fp32: ctx.enter_context(nc.sbuf_tensor("r1_" + name, shape, dt))
        taken = []
        sem = M.sems.phase("r1_", taken)
        W = F + 1
        ridx = sb("ridx", [P, T], i32)
        si = sb("si", [P, 2], i32)
        old = sb("old", [P, 2, W])
        new = sb("new", [P, 2, W])
        turn = sb("turn", [P, 2])
        other = sb("other", [P, T])
        pad = sb("pad", [P, T])
        gap = sb("gap", [P, T])
        shift = sb("shift", [P, T])
        chosen, staged, merged = sem("chosen"), sem("staged"), sem("merged")
        state_in = [sem(f"state_in_{k}") for k in range(2)]
        state_out = [sem(f"state_out_{k}") for k in range(2)]
        s_dve = sem("dve_steps")
        block = ctx.enter_context(nc.Block())
        pairs = T // 2

        @block.gpsimd
        def _(pool):
            rounds = pool.value_load(M.rounds[0:1, 0:1], min_val=0, max_val=P)
            with pool.If(rounds > 0):
                with pool.Fori(0, rounds) as r:
                    pool.wait_ge(chosen, r + 1)
                    pool.nop(nofuse=True)
                    with pool.Fori(0, pairs) as i:
                        n = r * pairs + i
                        nc.gpsimd.tensor_copy(si[:, :], ridx[:, bass.ds(2 * i, 2)]).then_inc(staged, 1)
                        pool.wait_ge(staged, n + 1)
                        pool.nop(nofuse=True)
                        for k in range(2):
                            nc.gpsimd.indirect_dma_start(out=old[:, k, :], out_offset=None, in_=M.max_state[k],
                                                         in_offset=rows_at(si, k)).then_inc(state_in[k], 16)
                        pool.wait_ge(merged, n + 1)
                        pool.nop(nofuse=True)
                        for k in range(2):
                            nc.gpsimd.indirect_dma_start(out=M.max_state[k], out_offset=rows_at(si, k),
                                                         in_=new[:, k, :], in_offset=None).then_inc(state_out[k], 16)
                        pool.wait_ge(state_out[0], 16 * n + 16)
                        pool.wait_ge(state_out[1], 16 * n + 16)
                        pool.nop(nofuse=True)

        @block.vector
        def _(dve):
            rounds = dve.value_load(M.rounds[0:1, 0:1], min_val=0, max_val=P)
            s = Steps(dve, s_dve)
            s.done(nc.vector.memset(turn[:, 0:1], 0.0))
            s.done(nc.vector.tensor_scalar(pad[:, :], M.key["dst"][:, :], float(N), None, ALU.is_ge))
            s.done(nc.vector.tensor_scalar(gap[:, :], M.key["dst"][:, :], M.waste[:, 0:1], -1.0, ALU.subtract, ALU.mult))
            s.sync()
            s.per, before = PER_R1, s.n
            with dve.If(rounds > 0):
                with dve.Fori(0, rounds) as r:
                    s.enter(before, r)
                    s.done(nc.vector.tensor_scalar(turn[:, 1:2], turn[:, 0:1], 1.0, None, ALU.add))
                    s.sync()
                    s.done(nc.vector.tensor_copy(turn[:, 0:1], turn[:, 1:2]))
                    s.done(nc.vector.tensor_scalar(other[:, :], M.rank["dst"][:, :], turn[:, 1:2], None, ALU.not_equal))
                    s.sync()
                    s.done(nc.vector.tensor_tensor(shift[:, :], other[:, :], pad[:, :], ALU.max))
                    s.sync()
                    s.done(nc.vector.tensor_tensor(other[:, :], shift[:, :], gap[:, :], ALU.mult))
                    s.sync()
                    nc.vector.tensor_tensor(ridx[:, :], other[:, :], M.key["dst"][:, :], ALU.add).then_inc(chosen, 1)
                    s.leave()
                    with dve.Fori(0, pairs) as i:
                        n = r * pairs + i
                        for k in range(2):
                            dve.wait_ge(state_in[k], 16 * n + 16)
                        nc.vector.tensor_tensor(new[:, :, :], old[:, :, :], M.V1[:, bass.ds(2 * i, 2), :],
                                                ALU.max).then_inc(merged, 1)


def dense1(nc, t, M):
    with ExitStack() as ctx:
        sb = lambda name, shape, dt=fp32: ctx.enter_context(nc.sbuf_tensor("d1_" + name, shape, dt))
        taken = []
        sem = M.sems.phase("d1_", taken)
        W = F + 1
        X = [sb(f"X{u}", [P, K, F]) for u in range(3)]
        S = [[sb(f"S{u}{k}", [P, K, W]) for k in range(2)] for u in range(3)]
        Y = [sb(f"Y{u}", [P, K, W]) for u in range(3)]
        top = sb("top", [P, K, W])
        best = sb("best", [P, K, F])
        x_in = [sem(f"x_in{u}") for u in range(3)]
        states_in = [sem(f"states_in{u}") for u in range(3)]
        states_used = sem("states_used")
        stored = sem("stored")
        norm = Norm(nc, M, sb, sem, K)
        best_ready, done = sem("best_ready"), sem("done")
        s_dve = sem("dve_steps")
        block = ctx.enter_context(nc.Block())

        @block.sync
        def _(sp):
            M.sems.clear(sp)
            def load(c, u):
                sp.dma_start(X[u][:, :, :], chunk(M.x1, c)).then_inc(x_in[u], 16)

                for k in range(2):
                    sp.dma_start(S[u][k][:, :, :], chunk(M.max_state[k], c)).then_inc(states_in[u], 16)

            def body(c, u, i):
                sp.wait_ge(done, c + 1)
                sp.nop(nofuse=True)
                if not isinstance(c, int) or c + 3 < NCH:
                    load(c + 3, u)
                wait(sp, stored, 16 * c)
                sp.nop(nofuse=True)
                sp.dma_start(chunk(M.x2, c), Y[u][:, :, :]).then_inc(stored, 16)

            for c in range(3):
                load(c, c)
            each_chunk_of_three(sp, body)
            sp.wait_ge(stored, 16 * NCH)

        @block.gpsimd
        def _(pool):
            def body(c, u, i):
                pool.wait_ge(x_in[u], 16 * (i + 1))
                pool.wait_ge(best_ready, c + 1)
                nc.gpsimd.tensor_tensor(Y[u][:, :, 0:F], X[u][:, :, :], best[:, :, :], ALU.add).then_inc(done, 1)

            each_chunk_of_three(pool, body)

        @block.scalar
        def _(act):
            def body(c, u, i):
                norm.square(act, c)
                norm.take_root(act, c)
                norm.relu(act, c)

            each_chunk_of_three(act, body)

        @block.vector
        def _(dve):
            s = Steps(dve, s_dve, PER_D1)

            def begin(c, u, i):
                dve.wait_ge(x_in[u], 16 * (i + 1))
                wait(dve, norm.scaled, c)
                norm.centre(s, X[u][:, :, :])

            def end(c, u, i):
                wait(dve, stored, 16 * (c - 2))
                s.done(nc.vector.tensor_copy(Y[u][:, :, F], top[:, :, F]))
                dve.wait_ge(norm.h_ready, c + 1)
                wait(dve, done, c)
                nc.vector.tensor_tensor(best[:, :, :], norm.h[:, :, :], top[:, :, 0:F], ALU.max).then_inc(best_ready, 1)

            def states(c, u, i):
                dve.wait_ge(states_in[u], 32 * (i + 1))
                wait(dve, best_ready, c)
                nc.vector.tensor_tensor(top[:, :, :], S[u][0][:, :, :], S[u][1][:, :, :], ALU.max).then_inc(states_used, 1)
                norm.sum_squares(dve, c)
                norm.scale(dve, s, c)
                dve.wait_ge(states_used, c + 1)

            def body(c, u, i):
                n, v, k = c + 1, (u + 1) % 3, (c + 1) // 3 if isinstance(c, int) else i + (u + 1) // 3
                if live_chunk(n):
                    begin(n, v, k)
                end(c, u, i)
                if live_chunk(n):
                    s.sync()
                    states(n, v, k)

            begin(0, 0, 0)
            states(0, 0, 0)
            each_chunk_of_three(dve, body, s)
    M.sems.retire(taken)


def equal_keys(nc, M, name, g, rows, same, cross):
    mine = M.key[name][:, cols(g)]
    nc.vector.tensor_tensor(cross[:, :, :], rows.rearrange("p (h two) k -> p two h k", two=2)[:, 0, :, :],
                            rep(mine.rearrange("p (h two) -> p two h", two=2)[:, 1, :], P), ALU.is_equal)
    return nc.vector.tensor_tensor(same[:, :, :], rows, rep(mine, P), ALU.is_equal)


def sum_equal(nc, psV, same, cross, V, width):
    for j in range(G):
        first = j % 2 == 0
        last = nc.tensor.matmul(psV[:, j, :], same[:, j, :], V[:, j, 0:width], start=True, stop=not first)
        if first:
            last = nc.tensor.matmul(psV[:, j, :], cross[:, j // 2, :], V[:, j + 1, 0:width], start=False, stop=True)
    return last


def gather_and_add(nc, pool, M, wanted, key, source, sums, X, gi, si, part, sems):
    staged_x, staged_s, x_in, x_used, part_ready, landed = sems
    nx = G * len(wanted)

    def stage_x(g, v):
        for n, k in enumerate(wanted):
            nc.gpsimd.tensor_copy(gi[v][:, G * n:G * n + G], M.gidx[k][:, cols(g)]).then_inc(staged_x, 1)

    def gather_x(v, some):
        for j in some:
            nc.gpsimd.indirect_dma_start(out=X[v][:, j, :], out_offset=None, in_=source,
                                         in_offset=rows_at(gi[v], j)).then_inc(x_in[v], 16)

    def adds(g, v, ahead):
        ahead(0, nx // 2)
        wait(pool, landed, 16 * G * g)
        pool.nop(nofuse=True)
        nc.gpsimd.tensor_copy(si[v][:, :], M.pidx[key][:, cols(g)]).then_inc(staged_s, 1)
        pool.wait_ge(staged_s, g + 1)
        pool.nop(nofuse=True)
        pool.wait_ge(part_ready, g + 1)
        pool.nop(nofuse=True)
        for j in range(G):
            if j == 2:
                ahead(nx // 2, nx)
                pool.wait_ge(landed, 16 * (G * g + j))
                pool.nop(nofuse=True)
            nc.gpsimd.indirect_dma_start(out=sums, out_offset=rows_at(si[v], j), in_=part[v][:, j, :],
                                         in_offset=None, compute_op=ALU.add).then_inc(landed, 16)

    def body(g, u, h):
        if live(g + 2):
            pool.wait_ge(x_used, g + 1)
            pool.nop(nofuse=True)
            stage_x(g + 2, u)
            pool.wait_ge(staged_x, len(wanted) * (g + 3))
            pool.nop(nofuse=True)
            ahead = lambda a, b: gather_x(u, range(a, b))
        else:
            ahead = lambda a, b: None
        if live(g - 1):
            adds(g - 1, 1 - u, ahead)
        else:
            ahead(0, nx)

    stage_x(0, 0)
    stage_x(1, 1)
    pool.wait_ge(staged_x, 2 * len(wanted))
    gather_x(0, range(nx))
    gather_x(1, range(nx))
    each_group(pool, body, extra=1)
    pool.wait_ge(landed, 16 * G * NG)


def layer2_edges(nc, t, M):
    with ExitStack() as ctx:
        sb = lambda name, shape, dt=fp32: ctx.enter_context(nc.sbuf_tensor("e2_" + name, shape, dt))
        ps = lambda name, shape: ctx.enter_context(nc.psum_tensor("e2_" + name, shape, fp32))
        taken = []
        sem = M.sems.phase("e2_", taken)
        W = F + 1
        X = [sb(f"X{u}", [P, 2 * G, W]) for u in range(2)]
        gi = [sb(f"gi{u}", [P, 2 * G], i32) for u in range(2)]
        si = [sb(f"si{u}", [P, G], i32) for u in range(2)]
        keys = sb("keys", [P, 2, G, P])
        types = sb("types", [P, 2, G, P])
        hT = sb("hT", [P, 2, P])
        same = sb("same", [P, G, P])
        cross = sb("cross", [P, G // 2, P])
        onehot = sb("onehot", [P, G, P])
        is_last = [sb(f"is_last{u}", [P, G]) for u in range(2)]
        CR = [sb(f"CR{u}", [P, G, NB + F]) for u in range(2)]
        xhat = sb("xhat", [P, G, F])
        yhat = sb("yhat", [P, G, F])
        yrel = sb("yrel", [P, G, F])
        pair = sb("pair", [P, G, F])
        dot = sb("dot", [P, G])
        dot0 = sb("dot0", [P, G])
        gate = sb("gate", [P, G])
        prod = [sb(f"prod{b}", [P, NB, F]) for b in range(2)]
        msg = sb("msg", [P, G, F])
        gated = sb("gated", [P, G, F])
        loop = sb("loop", [P, G, F])
        V = sb("V", [P, G, W])
        part = [sb(f"part{u}", [P, G, W]) for u in range(2)]
        psT = ps("psT", [P, 2, P])
        psB = [ps(f"psB{b}", [P, NB, F]) for b in range(2)]
        psQ = ps("psQ", [P, 3, G, F])
        psC = ps("psC", [P, G, NB + F])
        psV = ps("psV", [P, G, W])

        staged_x, staged_s, landed, part_ready = sem("staged_x"), sem("staged_s"), sem("landed"), sem("part_ready")
        x_in = [sem(f"x_in{u}") for u in range(2)]
        keys_in = [sem(f"keys_in{u}") for u in range(2)]
        types_in = [sem(f"types_in{u}") for u in range(2)]
        keys_free, types_free, ones_ready = sem("keys_free"), sem("types_free"), sem("ones_ready")
        norm = Norm(nc, M, sb, sem, 2 * G)
        hT_psum, hT_ready = sem("hT_psum"), sem("hT_ready")
        onehot_ready, CR_psum, CR_ready = sem("onehot_ready"), sem("CR_psum"), sem("CR_ready")
        hats_ready, bases_ready, bases_used = sem("hats_ready"), sem("bases_ready"), sem("bases_used")
        dot_ready, gate_ready, V_ready, sums_ready = sem("dot_ready"), sem("gate_ready"), sem("V_ready"), sem("sums_ready")
        s_dve = sem("dve_steps")
        block = ctx.enter_context(nc.Block())

        @block.sync
        def _(sp):
            M.sems.clear(sp)
            with sp.Fori(0, NG // 2) as i:
                for u in range(2):
                    for name, buf, free, landed_ in (("type", types, types_free, types_in), ("dst", keys, keys_free, keys_in)):
                        sp.wait_ge(free, 2 * i + u + 1)
                        sp.nop(nofuse=True)
                        sp.dma_start(buf[:, u, :, :], M.keyT[name][cols(2 * i + u), :].unsqueeze(0)
                                     .to_broadcast([P, G, P])).then_inc(landed_[u], 16)

        @block.gpsimd
        def _(pool):
            gather_and_add(nc, pool, M, ("src", "dst"), "dst", M.x2, M.rel_sums, X, gi, si, part,
                           (staged_x, staged_s, x_in, norm.centred, part_ready, landed))

        @block.scalar
        def _(act):
            def copy_out(g, v):
                act.wait_ge(sums_ready, g + 1)
                wait(act, landed, 16 * G * (g - 1))
                nc.scalar.activation(part[v][:, :, :], psV[:, :, :], ACT.Copy).then_inc(part_ready, 1)

            def front(g, v):
                norm.take_root(act, g)
                act.wait_ge(CR_psum, g + 1)
                nc.scalar.activation(CR[v][:, :, :], psC[:, :, :], ACT.Copy).then_inc(CR_ready, 1)
                norm.relu(act, g)
                act.wait_ge(hT_psum, g + 1)
                nc.scalar.activation(hT[:, :, :], psT[:, :, :], ACT.Copy).then_inc(hT_ready, 1)

            def body(g, u, i):
                if live(g - 1):
                    copy_out(g - 1, 1 - u)
                if live(g + 1):
                    norm.square(act, g + 1)
                if live(g):
                    act.wait_ge(dot_ready, g + 1)
                    nc.scalar.activation(gate[:, :], dot0[:, :], ACT.Tanh, scale=float(F) ** -0.5).then_inc(gate_ready, 1)
                if live(g + 1):
                    front(g + 1, 1 - u)

            norm.square(act, 0)
            front(0, 0)
            each_group(act, body, lead=4, extra=1)

        @block.tensor
        def _(pe):
            def bases(g, j):
                wait(pe, bases_used, G * g + j - 1)
                nc.tensor.matmul(psB[j % 2][:, :, :].rearrange("p b f -> p (b f)"), hT[:, 0, :],
                                 M.WB2[:, j, :, :].rearrange("p b f -> p (b f)"),
                                 start=True, stop=True).then_inc(bases_ready, 1)

            def relation(g):
                pe.wait_ge(onehot_ready, g + 1)
                for j in range(G):
                    last = nc.tensor.matmul(psC[:, j, :], onehot[:, j, :], M.WCR[:, :], start=True, stop=True)
                last.then_inc(CR_psum, 1)

            def front(g):
                norm.transpose(pe, psT, g, hT_psum)
                pe.wait_ge(hT_ready, g + 1)
                for n, (side, w) in enumerate(((0, M.A1B), (1, M.A2B), (0, M.SLB))):
                    last = nc.tensor.matmul(psQ[:, n, :, :].rearrange("p a f -> p (a f)"), hT[:, side, :], w[:, :],
                                            start=True, stop=True)
                last.then_inc(hats_ready, 1)
                bases(g, 0)

            def body(g, u, i):
                bases(g, 2)
                if live(g + 1):
                    relation(g + 1)
                bases(g, 3)
                if live(g + 1):
                    front(g + 1)
                pe.wait_ge(V_ready, g + 1)
                wait(pe, part_ready, g)
                sum_equal(nc, psV, same, cross, V, W).then_inc(sums_ready, 1)
                if live(g + 1):
                    bases(g + 1, 1)

            relation(0)
            front(0)
            bases(0, 1)
            each_group(pe, body)

        @block.vector
        def _(dve):
            s = Steps(dve, s_dve, PER_E2)

            def begin(g, v, i):
                dve.wait_ge(x_in[v], 16 * 2 * G * (i + 1))
                s.done(nc.vector.tensor_tensor(is_last[v][:, :], X[v][:, G:2 * G, F], M.eid1[:, cols(g)], ALU.is_equal))
                norm.centre(s, X[v][:, :, 0:F])

            def relation(g, v, i):
                dve.wait_ge(types_in[v], 16 * (i + 1))
                nc.vector.tensor_scalar(onehot[:, :, :], types[:, v, :, :], M.pid[:, 0:1], None,
                                        ALU.is_equal).then_inc(onehot_ready, 1)
                dve.wait_ge(onehot_ready, g + 1)
                nc.vector.sem_inc(types_free, 1)

            def weigh(g, u, j):
                dve.wait_ge(bases_ready, G * g + j + 1)
                nc.vector.tensor_tensor(prod[j % 2][:, :, :], psB[j % 2][:, :, :], rep(CR[u][:, j, 0:NB], F),
                                        ALU.mult).then_inc(bases_used, 1)
                s.sync()
                dve.wait_ge(bases_used, G * g + j + 1)
                s.done(nc.vector.reduce_sum(msg[:, j, :], prod[j % 2][:, :, :].rearrange("p b f -> p f b"), AX.X))

            def body(g, u, i):
                n, v = (g + 1) // 2 if isinstance(g, int) else i + u, 1 - u
                dve.wait_ge(hats_ready, g + 1)
                s.done(nc.vector.tensor_tensor(xhat[:, :, :], psQ[:, 0, :, :], along(M.a1row[:, :], G), ALU.add))
                s.done(nc.vector.tensor_tensor(yhat[:, :, :], psQ[:, 1, :, :], along(M.a2row[:, :], G), ALU.add))
                s.done(nc.vector.tensor_tensor(loop[:, :, :], psQ[:, 2, :, :], rep(is_last[u][:, :], F), ALU.mult))
                if live(g + 1):
                    begin(g + 1, v, n)
                dve.wait_ge(CR_ready, g + 1)
                s.sync()
                s.done(nc.vector.tensor_tensor(yrel[:, :, :], yhat[:, :, :], CR[u][:, :, NB:NB + F], ALU.add))
                s.sync()
                s.done(nc.vector.tensor_tensor(pair[:, :, :], xhat[:, :, :], yrel[:, :, :], ALU.mult))
                if live(g + 1):
                    norm.sum_squares(dve, g + 1)
                s.sync()
                s.done(nc.vector.reduce_sum(dot[:, :], pair[:, :, :], AX.X))
                weigh(g, u, 0)
                nc.vector.tensor_scalar(dot0[:, :], dot[:, :], 0.0, None, ALU.max).then_inc(dot_ready, 1)
                if live(g + 1):
                    relation(g + 1, v, n)
                weigh(g, u, 1)
                if live(g + 1):
                    norm.scale(dve, s, g + 1)
                weigh(g, u, 2)
                dve.wait_ge(keys_in[u], 16 * (i + 1))
                wait(dve, sums_ready, g)
                equal_keys(nc, M, "dst", g, keys[:, u, :, :], same, cross).then_inc(keys_free, 1)
                weigh(g, u, 3)
                dve.wait_ge(gate_ready, g + 1)
                s.sync()
                s.done(nc.vector.tensor_tensor(gated[:, :, :], msg[:, :, :], rep(gate[:, :], F), ALU.mult))
                s.sync()
                nc.vector.tensor_tensor(V[:, :, 0:F], gated[:, :, :], loop[:, :, :], ALU.add).then_inc(V_ready, 1)
                dve.wait_ge(V_ready, g + 1)

            nc.vector.memset(V[:, :, :], 1.0).then_inc(ones_ready, 1)
            dve.wait_ge(ones_ready, 1)
            nc.vector.sem_inc(keys_free, 2)
            nc.vector.sem_inc(types_free, 2)
            begin(0, 0, 0)
            norm.sum_squares(dve, 0)
            relation(0, 0, 0)
            norm.scale(dve, s, 0)
            each_group(dve, body, s)


def dense2(nc, t, M):
    with ExitStack() as ctx:
        sb = lambda name, shape, dt=fp32: ctx.enter_context(nc.sbuf_tensor("d2_" + name, shape, dt))
        ps = lambda name, shape: ctx.enter_context(nc.psum_tensor("d2_" + name, shape, fp32))
        taken = []
        sem = M.sems.phase("d2_", taken)
        W = F + 1
        X = [sb(f"X{u}", [P, K, W]) for u in range(2)]
        S = [sb(f"S{u}", [P, K, W]) for u in range(2)]
        Y = [sb(f"Y{u}", [P, K, F]) for u in range(2)]
        Z = [sb(f"Z{u}", [P, K, W]) for u in range(2)]
        hT = [sb(f"hT{q}", [P, G, P]) for q in range(2)]
        factor = [sb(f"factor{u}", [P, K]) for u in range(2)]
        droot = [sb(f"droot{u}", [P, K]) for u in range(2)]
        psT = [ps(f"psT{q}", [P, G, P]) for q in range(2)]
        psR = [ps(f"psR{q}", [P, G * P]) for q in range(3)]
        loaded = [sem(f"loaded{u}") for u in range(2)]
        x3_stored, hs_stored = sem("x3_stored"), sem("hs_stored")
        norm = Norm(nc, M, sb, sem, K)
        h = [norm.h, sb("h1", [P, K, F])]
        hT_psum, hT_ready, round_ready = sem("hT_psum"), sem("hT_ready"), sem("round_ready")
        degree_root, done, s_dve = sem("degree_root"), sem("done"), sem("dve_steps")
        proj_sems = norm.h_ready, hT_psum, hT_ready, round_ready, done
        block = ctx.enter_context(nc.Block())

        @block.sync
        def _(sp):
            M.sems.clear(sp)
            def load(c, u):
                sp.dma_start(X[u][:, :, :], chunk(M.x2, c)).then_inc(loaded[u], 16)
                sp.dma_start(S[u][:, :, :], chunk(M.rel_sums, c)).then_inc(loaded[u], 16)

            def after_x3(c, u):
                sp.wait_ge(norm.centred, c + 1)
                sp.wait_ge(degree_root, c + 1)
                sp.nop(nofuse=True)
                if not isinstance(c, int) or c + 2 < NCH:
                    load(c + 2, u)
                wait(sp, x3_stored, 16 * c)
                sp.nop(nofuse=True)
                sp.dma_start(chunk(M.x3, c), Y[u][:, :, :]).then_inc(x3_stored, 16)

            def body(c, u, i):
                if live_chunk(c + 1):
                    after_x3(c + 1, 1 - u)
                sp.wait_ge(done, c + 1)
                sp.nop(nofuse=True)
                wait(sp, hs_stored, 16 * c)
                sp.nop(nofuse=True)
                sp.dma_start(chunk(M.hs, c), Z[u][:, :, :]).then_inc(hs_stored, 16)

            load(0, 0)
            load(1, 1)
            after_x3(0, 0)
            each_chunk(sp, body)
            sp.wait_ge(x3_stored, 16 * NCH)
            sp.wait_ge(hs_stored, 16 * NCH)

        @block.scalar
        def _(act):
            def root_of_degree(c, u, i):
                act.wait_ge(loaded[u], 32 * (i + 1))
                wait(act, done, c - 1)
                nc.scalar.activation(droot[u][:, :], S[u][:, :, F], ACT.Sqrt, bias=M.ones[:, 0:1]).then_inc(degree_root, 1)

            def positive(c, h):
                nc.scalar.activation(h[:, :, :], norm.diff[:, :, :], ACT.Relu, scale=LN_GAIN).then_inc(norm.h_ready, 1)

            def body(c, u, i):
                n, v, k = after(c, u, i)
                project_scalar(nc, act, psT, hT, proj_sems, c, u, 0)
                if live_chunk(n):
                    root_of_degree(n, v, k)
                project_scalar(nc, act, psT, hT, proj_sems, c, u, 1)
                project_scalar(nc, act, psT, hT, proj_sems, c, u, 2)
                if live_chunk(n):
                    norm.square(act, n)
                    positive(n, h[v])
                    norm.take_root(act, n)

            root_of_degree(0, 0, 0)
            norm.square(act, 0)
            positive(0, h[0])
            norm.take_root(act, 0)
            each_chunk(act, body)

        @block.tensor
        def _(pe):
            each_chunk(pe, lambda c, u, i: project_pe(nc, pe, M, M.W3B, h[u], psT, hT, psR, proj_sems, c, u))

        @block.vector
        def _(dve):
            s = Steps(dve, s_dve, PER_D2)

            def begin(c, u, i):
                dve.wait_ge(loaded[u], 32 * (i + 1))
                wait(dve, norm.h_ready, c)
                wait(dve, x3_stored, 16 * (c - 1))
                s.done(nc.vector.scalar_tensor_tensor(Y[u][:, :, :], S[u][:, :, 0:F], 0.0, X[u][:, :, 0:F], ALU.max, ALU.add))
                s.sync()
                norm.centre(s, Y[u][:, :, :])
                norm.sum_squares(dve, c)

            def factors(c, u):
                dve.wait_ge(norm.rooted, c + 1)
                dve.wait_ge(degree_root, c + 1)
                wait(dve, hs_stored, 16 * (c - 1))
                s.done(nc.vector.reciprocal(norm.rstd[:, :], norm.root[:, :]))
                s.done(nc.vector.reciprocal(Z[u][:, :, F], droot[u][:, :]))
                s.sync()
                s.done(nc.vector.tensor_tensor(factor[u][:, :], norm.rstd[:, :], Z[u][:, :, F], ALU.mult))
                s.sync()

            def body(c, u, i):
                n, v, k = after(c, u, i)
                if live_chunk(n):
                    begin(n, v, k)
                dve.wait_ge(round_ready, 3 * c + 3)
                m = G * G
                for q in range(3):
                    last = nc.vector.tensor_tensor(Z[u][:, m * q:m * q + m, 0:F],
                                                   psR[q][:, :].rearrange("p (k f) -> p k f", f=F),
                                                   rep(factor[u][:, m * q:m * q + m], F), ALU.mult)
                last.then_inc(done, 1)
                if live_chunk(n):
                    factors(n, v)

            begin(0, 0, 0)
            factors(0, 0)
            each_chunk(dve, body, s)
    M.sems.retire(taken)


def conv_edges(nc, t, M):
    with ExitStack() as ctx:
        sb = lambda name, shape, dt=fp32: ctx.enter_context(nc.sbuf_tensor("e3_" + name, shape, dt))
        taken = []
        sem = M.sems.phase("e3_", taken)
        X = [sb(f"X{u}", [P, G, F + 1]) for u in range(2)]
        gi = [sb(f"gi{u}", [P, G], i32) for u in range(2)]
        si = [sb(f"si{u}", [P, G], i32) for u in range(2)]
        keys = sb("keys", [P, 2, G, P])
        same = [sb(f"same{u}", [P, G, P]) for u in range(2)]
        cross = [sb(f"cross{u}", [P, G // 2, P]) for u in range(2)]
        part = [sb(f"part{u}", [P, G, F]) for u in range(2)]
        psV = [ctx.enter_context(nc.psum_tensor(f"e3_psV{u}", [P, G, F], fp32)) for u in range(2)]
        staged_x, staged_s, landed, part_ready = sem("staged_x"), sem("staged_s"), sem("landed"), sem("part_ready")
        x_in = [sem(f"x_in{u}") for u in range(2)]
        keys_in = [sem(f"keys_in{u}") for u in range(2)]
        same_ready, sums_ready, keys_free = sem("same_ready"), sem("sums_ready"), sem("keys_free")
        block = ctx.enter_context(nc.Block())

        @block.sync
        def _(sp):
            M.sems.clear(sp)
            spread_keys(sp, M, "dst", keys, keys_free, keys_in)

        @block.gpsimd
        def _(pool):
            gather_and_add(nc, pool, M, ("src",), "dst", M.hs, M.conv_sums, X, gi, si, part,
                           (staged_x, staged_s, x_in, sums_ready, part_ready, landed))

        @block.scalar
        def _(act):
            def edges(g, u, i):
                act.wait_ge(sums_ready, g + 1)
                wait(act, landed, 16 * G * (g - 1))
                nc.scalar.activation(part[u][:, :, :], psV[u][:, :, :], ACT.Copy).then_inc(part_ready, 1)

            each_group(act, edges)

        @block.tensor
        def _(pe):
            def edges(g, u, i):
                pe.wait_ge(x_in[u], 16 * G * (i + 1))
                pe.wait_ge(same_ready, g + 1)
                wait(pe, part_ready, g - 1)
                sum_equal(nc, psV[u], same[u], cross[u], X[u], F).then_inc(sums_ready, 1)

            each_group(pe, edges)

        @block.vector
        def _(dve):
            def edges(g, u, i):
                dve.wait_ge(keys_in[u], 16 * (i + 1))
                wait(dve, sums_ready, g - 1)
                equal_keys(nc, M, "dst", g, keys[:, u, :, :], same[u], cross[u]).then_inc(same_ready, 1)
                dve.wait_ge(same_ready, g + 1)
                nc.vector.sem_inc(keys_free, 1)

            nc.vector.sem_inc(keys_free, 2)
            each_group(dve, edges)


def dense3(nc, t, M):
    with ExitStack() as ctx:
        sb = lambda name, shape, dt=fp32: ctx.enter_context(nc.sbuf_tensor("d3_" + name, shape, dt))
        taken = []
        sem = M.sems.phase("d3_", taken)
        Z = [sb(f"Z{u}", [P, K, F + 1]) for u in range(3)]
        S = [sb(f"S{u}", [P, K, F]) for u in range(3)]
        Y = [sb(f"Y{u}", [P, K, F]) for u in range(3)]
        both = sb("both", [P, K, F])
        scaled = sb("scaled", [P, K, F])
        biased = sb("biased", [P, K, F])
        loaded = [sem(f"loaded{u}") for u in range(3)]
        stored, biased_ready, done, s_dve = sem("stored"), sem("biased_ready"), sem("done"), sem("dve_steps")
        block = ctx.enter_context(nc.Block())

        @block.sync
        def _(sp):
            M.sems.clear(sp)
            def load(c, u):
                sp.dma_start(Z[u][:, :, :], chunk(M.hs, c)).then_inc(loaded[u], 16)
                sp.dma_start(S[u][:, :, :], chunk(M.conv_sums, c)).then_inc(loaded[u], 16)

            def body(c, u, i):
                sp.wait_ge(done, c + 1)
                sp.nop(nofuse=True)
                if not isinstance(c, int) or c + 3 < NCH:
                    load(c + 3, u)
                wait(sp, stored, 16 * c)
                sp.nop(nofuse=True)
                sp.dma_start(chunk(M.conv, c), Y[u][:, :, :]).then_inc(stored, 16)

            for c in range(3):
                load(c, c)
            each_chunk_of_three(sp, body)
            sp.wait_ge(stored, 16 * NCH)

        @block.scalar
        def _(act):
            def body(c, u, i):
                act.wait_ge(biased_ready, c + 1)
                wait(act, stored, 16 * (c - 2))
                nc.scalar.activation(Y[u][:, :, :], biased[:, :, :], ACT.Relu).then_inc(done, 1)

            each_chunk_of_three(act, body)

        @block.vector
        def _(dve):
            s = Steps(dve, s_dve, PER_D3)

            def body(c, u, i):
                dve.wait_ge(loaded[u], 32 * (i + 1))
                s.done(nc.vector.tensor_tensor(both[:, :, :], Z[u][:, :, 0:F], S[u][:, :, :], ALU.add))
                s.sync()
                s.done(nc.vector.tensor_tensor(scaled[:, :, :], both[:, :, :], rep(Z[u][:, :, F], F), ALU.mult))
                s.sync()
                wait(dve, done, c)
                nc.vector.tensor_tensor(biased[:, :, :], scaled[:, :, :], along(M.b3row[:, :], K),
                                        ALU.add).then_inc(biased_ready, 1)
                dve.wait_ge(biased_ready, c + 1)

            each_chunk_of_three(dve, body, s)
    M.sems.retire(taken)


def square_edges(nc, t, M):
    with ExitStack() as ctx:
        sb = lambda name, shape, dt=fp32: ctx.enter_context(nc.sbuf_tensor("e4_" + name, shape, dt))
        taken = []
        sem = M.sems.phase("e4_", taken)
        W = F + 1
        X = [sb(f"X{u}", [P, 2 * G, F]) for u in range(2)]
        gi = [sb(f"gi{u}", [P, 2 * G], i32) for u in range(2)]
        si = [sb(f"si{u}", [P, G], i32) for u in range(2)]
        keys = sb("keys", [P, 2, G, P])
        same = [sb(f"same{u}", [P, G, P]) for u in range(2)]
        cross = [sb(f"cross{u}", [P, G // 2, P]) for u in range(2)]
        diff = [sb(f"diff{u}", [P, G, F]) for u in range(2)]
        V = [sb(f"V{u}", [P, G, W]) for u in range(2)]
        part = [sb(f"part{u}", [P, G, W]) for u in range(2)]
        psV = [ctx.enter_context(nc.psum_tensor(f"e4_psV{u}", [P, G, W], fp32)) for u in range(2)]
        staged_x, staged_s, landed, part_ready = sem("staged_x"), sem("staged_s"), sem("landed"), sem("part_ready")
        x_in = [sem(f"x_in{u}") for u in range(2)]
        keys_in = [sem(f"keys_in{u}") for u in range(2)]
        diff_ready, V_ready, sums_ready, keys_free = sem("diff_ready"), sem("V_ready"), sem("sums_ready"), sem("keys_free")
        ones_ready = sem("ones_ready")
        block = ctx.enter_context(nc.Block())

        @block.sync
        def _(sp):
            M.sems.clear(sp)
            spread_keys(sp, M, "src", keys, keys_free, keys_in)

        @block.gpsimd
        def _(pool):
            gather_and_add(nc, pool, M, ("src", "dst"), "src", M.conv, M.square_sums, X, gi, si, part,
                           (staged_x, staged_s, x_in, diff_ready, part_ready, landed))

        @block.scalar
        def _(act):
            def edges(g, u, i):
                act.wait_ge(diff_ready, g + 1)
                wait(act, sums_ready, g - 1)
                nc.scalar.activation(V[u][:, :, 0:F], diff[u][:, :, :], ACT.Square).then_inc(V_ready, 1)
                act.wait_ge(sums_ready, g + 1)
                wait(act, landed, 16 * G * (g - 1))
                nc.scalar.activation(part[u][:, :, :], psV[u][:, :, :], ACT.Copy).then_inc(part_ready, 1)

            act.wait_ge(ones_ready, 1)
            each_group(act, edges)

        @block.tensor
        def _(pe):
            def edges(g, u, i):
                pe.wait_ge(V_ready, g + 1)
                pe.wait_ge(keys_free, g + 3)
                wait(pe, part_ready, g - 1)
                sum_equal(nc, psV[u], same[u], cross[u], V[u], W).then_inc(sums_ready, 1)

            each_group(pe, edges)

        @block.vector
        def _(dve):
            def edges(g, u, i):
                dve.wait_ge(x_in[u], 16 * 2 * G * (i + 1))
                wait(dve, V_ready, g - 1)
                nc.vector.tensor_tensor(diff[u][:, :, :], X[u][:, 0:G, :], X[u][:, G:2 * G, :],
                                        ALU.subtract).then_inc(diff_ready, 1)
                dve.wait_ge(keys_in[u], 16 * (i + 1))
                wait(dve, sums_ready, g - 1)
                equal_keys(nc, M, "src", g, keys[:, u, :, :], same[u], cross[u]).then_inc(keys_free, 1)

            for u in range(2):
                last = nc.vector.memset(V[u][:, :, :], 1.0)
            last.then_inc(ones_ready, 1)
            nc.vector.sem_inc(keys_free, 2)
            each_group(dve, edges)


def dense4(nc, t, M, out):
    with ExitStack() as ctx:
        sb = lambda name, shape, dt=fp32: ctx.enter_context(nc.sbuf_tensor("d4_" + name, shape, dt))
        taken = []
        sem = M.sems.phase("d4_", taken)
        X = [sb(f"X{u}", [P, K, F]) for u in range(3)]
        S = [sb(f"S{u}", [P, K, F + 1]) for u in range(3)]
        Y = [sb(f"Y{u}", [P, K, F]) for u in range(3)]
        count = sb("count", [P, K])
        share = sb("share", [P, K])
        mean = [sb(f"mean{u}", [P, K, F]) for u in range(3)]
        curve = [sb(f"curve{u}", [P, K, F]) for u in range(3)]
        loaded = [sem(f"loaded{u}") for u in range(3)]
        stored, mean_ready, curve_ready, done, s_dve = sem("stored"), sem("mean_ready"), sem("curve_ready"), sem("done"), sem("dve_steps")
        block = ctx.enter_context(nc.Block())

        @block.sync
        def _(sp):
            M.sems.clear(sp)
            def load(c, u):
                sp.dma_start(X[u][:, :, :], chunk(M.x3, c)).then_inc(loaded[u], 16)
                sp.dma_start(S[u][:, :, :], chunk(M.square_sums, c)).then_inc(loaded[u], 16)

            def body(c, u, i):
                sp.wait_ge(done, c + 1)
                sp.nop(nofuse=True)
                if not isinstance(c, int) or c + 3 < NCH:
                    load(c + 3, u)
                wait(sp, stored, 16 * c)
                sp.nop(nofuse=True)
                sp.dma_start(chunk(out, c), Y[u][:, :, :]).then_inc(stored, 16)

            for c in range(3):
                load(c, c)
            each_chunk_of_three(sp, body)
            sp.wait_ge(stored, 16 * NCH)

        @block.gpsimd
        def _(pool):
            def body(c, u, i):
                pool.wait_ge(curve_ready, c + 1)
                wait(pool, stored, 16 * (c - 2))
                nc.gpsimd.tensor_tensor(Y[u][:, :, :], X[u][:, :, :], curve[u][:, :, :], ALU.add).then_inc(done, 1)

            each_chunk_of_three(pool, body)

        @block.scalar
        def _(act):
            def body(c, u, i):
                act.wait_ge(mean_ready, c + 1)
                wait(act, done, c - 2)
                nc.scalar.activation(curve[u][:, :, :], mean[u][:, :, :], ACT.Tanh).then_inc(curve_ready, 1)

            each_chunk_of_three(act, body)

        @block.vector
        def _(dve):
            s = Steps(dve, s_dve, PER_D4)

            def body(c, u, i):
                dve.wait_ge(loaded[u], 32 * (i + 1))
                wait(dve, mean_ready, c)
                s.done(nc.vector.tensor_scalar(count[:, :], S[u][:, :, F], 1.0, None, ALU.max))
                s.sync()
                s.done(nc.vector.reciprocal(share[:, :], count[:, :]))
                s.sync()
                wait(dve, curve_ready, c - 2)
                nc.vector.tensor_tensor(mean[u][:, :, :], S[u][:, :, 0:F], rep(share[:, :], F),
                                        ALU.mult).then_inc(mean_ready, 1)

            each_chunk_of_three(dve, body, s)
    M.sems.retire(taken)


def gnn_program(nc, t, out):
    with ExitStack() as ctx:
        ctx.enter_context(nc.allow_non_contiguous_dma(reason="small tables, once"))
        M = Memory(nc, ctx)
        setup(nc, t, M)
        layer0_edges(nc, t, M)
        dense0(nc, t, M)
        layer1_edges(nc, t, M)
        more_maxima(nc, M)
        dense1(nc, t, M)
        layer2_edges(nc, t, M)
        dense2(nc, t, M)
        conv_edges(nc, t, M)
        dense3(nc, t, M)
        square_edges(nc, t, M)
        dense4(nc, t, M, out)


_INS = ['x', 'src', 'dst', 'edge_attr_2', 'edge_attr_32', 'edge_type_86', 'L0_gnn_weight', 'L0_gnn_root_weight',
        'L0_gnn_att_weight', 'L0_gnn_bias', 'L1_gnn_W1', 'L1_gnn_b1', 'L1_gnn_W2', 'L1_gnn_b2', 'L2_gnn_weight',
        'L2_gnn_w_comp', 'L2_gnn_self_loop_weight', 'L2_gnn_A1_w', 'L2_gnn_A1_b', 'L2_gnn_A2_w', 'L2_gnn_A2_b',
        'L2_gnn_rel_emb', 'L3_gnn_W', 'L3_gnn_b']


def kernel(**inputs):
    import numpy as _np
    import concourse.bacc as _bacc
    from concourse import mybir as _mybir
    from concourse.bass_utils import run_bass_kernel_spmd as _run

    nc = _bacc.Bacc("TRN2", target_bir_lowering=False, num_devices=1)
    arrays, tensors = {}, {}
    for name in _INS:
        a = _np.ascontiguousarray(inputs[name])
        arrays[f"in_{name}_dram"] = a
        tensors[name] = nc.dram_tensor(f"in_{name}_dram", a.shape, _mybir.dt.from_np(a.dtype),
                                       kind="ExternalInput").ap()
    out = nc.dram_tensor("out_0_dram", (N, F), fp32, kind="ExternalOutput").ap()
    gnn_program(nc, tensors, out)
    r = _run(nc, [arrays], core_ids=[0])
    return r.results[0]["out_0_dram"]
```
